# Optimizing a Trainium2 kernel written in Bass

```python
import numpy as np
import jax
import jax.numpy as jnp

def _softmax(x, axis=-1):
    return jax.nn.softmax(x, axis=axis)

def _gelu(x):
    return jax.nn.gelu(x, approximate=True)

def _silu(x):
    return jax.nn.silu(x)

def _sigmoid(x):
    return jax.nn.sigmoid(x)

def _layernorm(x, axis=-1, eps=1e-05):
    m = jnp.mean(x, axis=axis, keepdims=True)
    v = jnp.var(x, axis=axis, keepdims=True)
    return (x - m) / jnp.sqrt(v + eps)

def _scatter_add(tgt, idx, src, axis=0):
    return tgt.at[idx].add(src)

def _segment_sum(src, seg, n):
    return jax.ops.segment_sum(src, seg, n)
kernel_name = 'mk_gnn_resnorm_d2_gnn_r8_118ed0'

def setup_inputs(seed: int=0):
    np.random.seed(seed)
    _w = jnp.asarray

    def _rec_inputs():
        import jax
        import jax.numpy as jnp
        _gk = jax.random.key(seed)
        x = -0.0002117 + 1 * jax.random.normal(jax.random.fold_in(_gk, 1), (6250, 256), jnp.float32)
        _s = jax.random.randint(jax.random.fold_in(_gk, 2), (50000,), 0, 6250, jnp.int32)
        _d = jax.random.randint(jax.random.fold_in(_gk, 3), (50000,), 0, 6250, jnp.int32)
        _loop = jnp.arange(6250, dtype=jnp.int32)
        src = jnp.concatenate([_s, _d, _loop])
        dst = jnp.concatenate([_d, _s, _loop])
        _o = jnp.argsort(dst, stable=True)
        src = src[_o]
        dst = dst[_o]
        edge_weight = jax.random.uniform(jax.random.fold_in(_gk, 13), (106250,), jnp.float32, 0.0, 0.999998)
        edge_weight_n2 = jax.random.uniform(jax.random.fold_in(_gk, 14), (106250,), jnp.float32, 0.0, 0.999998)
        return (x, src, dst, edge_weight, edge_weight_n2)
    x, src, dst, edge_weight, edge_weight_n2 = _rec_inputs()

    def _L0_gnn_setup():
        import jax, jax.numpy as jnp
        import numpy as np
        N_NODES = 12500
        N_EDGES = 100000
        DIM = 256
        EPS = 1e-05
        key = jax.random.key(seed)
        ks = jax.random.split(key, 12)
        H = DIM
        s = 1.0 / np.sqrt(H)
        s2 = 1.0 / np.sqrt(2 * H)
        return {'feat': jax.random.normal(ks[0], (N_NODES, DIM), dtype=jnp.float32), 'src': jax.random.randint(ks[1], (N_EDGES,), 0, N_NODES, dtype=jnp.int32), 'dst': jax.random.randint(ks[2], (N_EDGES,), 0, N_NODES, dtype=jnp.int32), 'iw': jax.random.uniform(ks[3], (N_EDGES,), dtype=jnp.float32), 'ow': jax.random.uniform(ks[4], (N_EDGES,), dtype=jnp.float32), 'gamma': jnp.ones((DIM,), jnp.float32), 'beta': jnp.zeros((DIM,), jnp.float32), 'W_in': jax.random.uniform(ks[5], (H, H), jnp.float32, -s, s), 'b_in': jax.random.uniform(ks[6], (H,), jnp.float32, -s, s), 'W_out': jax.random.uniform(ks[7], (H, H), jnp.float32, -s, s), 'b_out': jax.random.uniform(ks[8], (H,), jnp.float32, -s, s), 'W_x2i': jax.random.uniform(ks[9], (2 * H, 2 * H), jnp.float32, -s2, s2), 'b_x2i': jax.random.uniform(ks[10], (2 * H,), jnp.float32, -s2, s2), 'W_h2h': jax.random.uniform(ks[11], (H, 2 * H), jnp.float32, -s, s)}
    _L0_gnn_all = _L0_gnn_setup()
    _L0_gnn_in = {k: v for k, v in _L0_gnn_all.items() if k in ('gamma', 'beta', 'W_in', 'b_in', 'W_out', 'b_out', 'W_x2i', 'b_x2i', 'W_h2h')}
    del _L0_gnn_all

    def _L1_gnn_setup():
        import jax, jax.numpy as jnp
        import numpy as np
        N = 12500
        E = 400000
        F_IN = 256
        F_OUT = 256

        def _spmm(edge_index, edge_weight, x, n):
            dst, src = (edge_index[0], edge_index[1])
            msg = edge_weight[:, None] * x[src]
            return jax.ops.segment_sum(msg, dst, num_segments=n)
        key = jax.random.key(seed)
        k1, k2, k3, k4, k5 = jax.random.split(key, 5)
        feature = jax.random.normal(k1, (N, F_IN), dtype=jnp.float32)
        edge_index = jax.random.randint(k2, (2, E), 0, N)
        edge_weight = jax.random.uniform(k3, (E,), dtype=jnp.float32)
        stdv = 1.0 / np.sqrt(F_OUT)
        weight = jax.random.uniform(k4, (F_IN, F_OUT), dtype=jnp.float32, minval=-stdv, maxval=stdv)
        bias = jax.random.uniform(k5, (F_OUT,), dtype=jnp.float32, minval=-stdv, maxval=stdv)
        return {'feature': feature, 'edge_weight': edge_weight, 'weight': weight, 'bias': bias, 'edge_index': edge_index, 'mode': 2}
    _L1_gnn_all = _L1_gnn_setup()
    _L1_gnn_in = {k: v for k, v in _L1_gnn_all.items() if k in ('weight', 'bias')}
    del _L1_gnn_all
    return {'x': x, 'src': src, 'dst': dst, 'edge_weight': edge_weight, 'edge_weight_n2': edge_weight_n2, 'L0_gnn_gamma': _L0_gnn_in['gamma'], 'L0_gnn_beta': _L0_gnn_in['beta'], 'L0_gnn_W_in': _L0_gnn_in['W_in'], 'L0_gnn_b_in': _L0_gnn_in['b_in'], 'L0_gnn_W_out': _L0_gnn_in['W_out'], 'L0_gnn_b_out': _L0_gnn_in['b_out'], 'L0_gnn_W_x2i': _L0_gnn_in['W_x2i'], 'L0_gnn_b_x2i': _L0_gnn_in['b_x2i'], 'L0_gnn_W_h2h': _L0_gnn_in['W_h2h'], 'L1_gnn_weight': _L1_gnn_in['weight'], 'L1_gnn_bias': _L1_gnn_in['bias']}

def reference(x, src, dst, edge_weight, edge_weight_n2, L0_gnn_gamma, L0_gnn_beta, L0_gnn_W_in, L0_gnn_b_in, L0_gnn_W_out, L0_gnn_b_out, L0_gnn_W_x2i, L0_gnn_b_x2i, L0_gnn_W_h2h, L1_gnn_weight, L1_gnn_bias):
    import jax
    import jax.numpy as jnp

    def _L0_gnn_ref(feat, src, dst, iw, ow, gamma, beta, W_in, b_in, W_out, b_out, W_x2i, b_x2i, W_h2h):
        import jax, jax.numpy as jnp
        import numpy as np
        N_NODES = 12500
        N_EDGES = 100000
        DIM = 256
        EPS = 1e-05
        N = feat.shape[0]
        num_steps = 1
        mean = jnp.mean(feat, axis=0)
        var = jnp.var(feat, axis=0)
        h = (feat - mean) * jax.lax.rsqrt(var + EPS) * gamma + beta
        for _ in range(num_steps):
            feat_in = h @ W_in + b_in
            feat_out = h @ W_out + b_out
            a_in = jax.ops.segment_sum(feat_in[src] * iw[:, None], dst, num_segments=N)
            a_out = jax.ops.segment_sum(feat_out[dst] * ow[:, None], src, num_segments=N)
            a = jnp.concatenate((a_in, a_out), axis=1)
            xi = a @ W_x2i + b_x2i
            hh = h @ W_h2h
            i_i, i_n = jnp.split(xi, 2, axis=1)
            h_i, h_n = jnp.split(hh, 2, axis=1)
            input_gate = jax.nn.sigmoid(i_i + h_i)
            new_gate = jnp.tanh(i_n + h_n)
            h = new_gate + input_gate * (h - new_gate)
        return h

    def _L1_gnn_ref(feature, edge_weight, weight, bias, edge_index, mode):
        import jax, jax.numpy as jnp
        import numpy as np
        N = 12500
        E = 400000
        F_IN = 256
        F_OUT = 256

        def _spmm(edge_index, edge_weight, x, n):
            dst, src = (edge_index[0], edge_index[1])
            msg = edge_weight[:, None] * x[src]
            return jax.ops.segment_sum(msg, dst, num_segments=n)
        if mode in (1, 2):
            feature = feature - jnp.mean(feature, axis=0, keepdims=True)
        if mode == 2:
            std = jnp.std(feature, axis=0, ddof=1) + 0.0001
            feature = feature / std
        support = _spmm(edge_index, edge_weight, feature, feature.shape[0])
        output = support @ weight
        return output + bias
    edge_index = jnp.stack([src, dst])
    x = _layernorm(x + _L0_gnn_ref(x, src, dst, edge_weight, edge_weight_n2, L0_gnn_gamma, L0_gnn_beta, L0_gnn_W_in, L0_gnn_b_in, L0_gnn_W_out, L0_gnn_b_out, L0_gnn_W_x2i, L0_gnn_b_x2i, L0_gnn_W_h2h), axis=-1)
    x = _layernorm(x + _L1_gnn_ref(x, edge_weight, L1_gnn_weight, L1_gnn_bias, edge_index, 2), axis=-1)
    return x

_drawn_inputs = setup_inputs


def setup_inputs(seed=0):
    import zlib

    import numpy as np

    out = dict(_drawn_inputs(seed))
    spreads = {'L0_gnn_gamma': (1.0, 0.2), 'L0_gnn_beta': (0.0, 0.1)}
    factors = {'L0_gnn_b_x2i': 8.0}
    for name, (base, spread) in spreads.items():
        noise = np.random.default_rng([zlib.crc32(name.encode()), seed]).standard_normal(out[name].shape)
        drawn = base * np.exp(spread * noise) if base else spread * noise
        out[name] = jnp.asarray(drawn.astype(out[name].dtype))
    for name, factor in factors.items():
        out[name] = (out[name] * factor).astype(out[name].dtype)
    return out
```

```python
import numpy as np
import concourse.bass as bass
import concourse.mybir as mybir
from contextlib import ExitStack

P = 128
N, D, E = 6250, 256, 106250
NT = -(-N // P)
NTP = NT + 1
FULL = N // P
TAIL = N - FULL * P
CPG = 4
GE = CPG * P
NG = -(-(E // GE + NT) // 8) * 8
NG_PLAIN = -(-(-(-E // GE)) // 8) * 8
NC = NG * CPG
UR = 256
NU = E // UR + NT
MW = 260
MROWS = NU * UR + NG * GE - E
RING = 4
EPS = 1e-5

F32 = mybir.dt.float32
I32 = mybir.dt.int32
ALU = mybir.AluOpType
ACT = mybir.ActivationFunctionType
AX = mybir.AxisListType


class Chain:

    def __init__(self, engine, semaphore, base=0):
        self.engine, self.semaphore, self.base, self.n = engine, semaphore, base, 0

    def __call__(self, instruction):
        instruction.then_inc(self.semaphore, 1)
        self.n += 1
        self.engine.wait_ge(self.semaphore, self.base + self.n)


def loop(engine, count, body):
    body(0, True)
    if count > 1:
        with engine.Fori(1, count) as i:
            body(i, False)


def gnn_program(nc, x, src, dst, edge_weight, edge_weight_n2, gamma, beta, w_in, b_in, w_out, b_out,
                w_x2i, b_x2i, w_h2h, w_l1, b_l1, out):
    ctx = ExitStack()
    with ctx:
        def sb(name, shape, dt=F32):
            return ctx.enter_context(nc.sbuf_tensor(name, shape, dt))

        def pb(name, shape, dt=F32):
            return ctx.enter_context(nc.psum_tensor(name, shape, dt))

        def sem(name):
            return ctx.enter_context(nc.semaphore(name))

        def dram(name, shape, dt=F32):
            return nc.dram_tensor(name, shape, dt, kind="Internal").ap()

        in_table = dram("in_table", [NTP * P, D])
        out_table = dram("out_table", [NTP * P, D])
        z_table = dram("z_table", [NTP * P, D])
        place_row = dram("place_row", [NG * GE])
        group_row = dram("group_row", [2, NG], I32)
        records = dram("records", [NG * GE, 4])
        messages = dram("messages", [MROWS, MW])

        node_a = sb("node_a", [P, NTP, D])
        node_c = sb("node_c", [P, NTP, D])
        work = sb("work", [P, 6 * NC + 4 * 1024])

        def area(at, shape, dt=F32):
            n = 1
            for d in shape:
                n *= d
            v = work[:, at:at + n]
            if len(shape) == 2:
                v = v.rearrange("p (a b) -> p a b", b=shape[1])
            elif len(shape) == 3:
                v = v.rearrange("p (a b c) -> p a b c", b=shape[1], c=shape[2])
            return v if dt == F32 else v.bitcast(dt)

        flat_c = node_c[:, :, :].rearrange("p t d -> p (t d)")

        def part_c(k, n=1):
            return flat_c[:, k * NC:(k + n) * NC]

        raw_si, raw_di = area(0, [NC], I32), area(NC, [NC], I32)
        raw_place, raw_place2 = area(0, [NC]), area(NC, [NC])
        raw = [area((2 + k) * NC, [NC]) for k in range(4)]
        wint, wint2 = area(4 * NC, [NC], I32), area(5 * NC, [NC], I32)
        win, mask, scan, rank = (part_c(k) for k in range(4))
        rec = part_c(4, 4).rearrange("p (c k) -> p c k", k=4)
        reload = part_c(4, 4).rearrange("p (h q k) -> p h q k", h=2, k=4)
        win2 = part_c(8)
        rec_put = sb("rec_put", [P, RING, 4])

        src_id = sb("src_id", [P, NC], I32)
        iw_col, ow_col = sb("iw_col", [P, NC]), sb("ow_col", [P, NC])
        place2 = sb("place2", [P, NC])
        src_key = sb("src_key", [P, NC])
        slot = sb("slot", [P, NC], I32)

        wio = sb("wio", [P, 2, 2 * D])
        wx = sb("wx", [P, 4, 2 * D])
        wh = sb("wh", [P, 2, 2 * D])
        w1 = sb("w1", [P, 2, D])
        gamma_b, beta_b, b1_b = sb("gamma_b", [P, D]), sb("beta_b", [P, D]), sb("b1_b", [P, D])
        bio_b, bx_b = sb("bio_b", [P, 2 * D]), sb("bx_b", [P, 2 * D])
        mean_b, scale_b = sb("mean_b", [P, D]), sb("scale_b", [P, D])
        mean2_b, scale2_b = mean_b, scale_b
        eps_c = sb("eps_c", [P, 1])

        ident, ones, upper = sb("ident", [P, P]), sb("ones", [P, P]), sb("upper", [P, P])
        iota2 = sb("iota2", [P, 2 * P])
        iota_w = sb("iota_w", [P, NTP])
        iota_u = sb("iota_u", [P, NU])
        pcol = sb("pcol", [P, 1])
        cnt, ends, starts = sb("cnt", [P, NTP]), sb("ends", [P, NTP]), sb("starts", [P, NTP])
        alig, aligi = sb("alig", [P, NTP]), sb("aligi", [P, NTP], I32)
        basew, diag = sb("basew", [P, NTP]), sb("diag", [P, NTP])
        endcol = sb("endcol", [P, 1])
        dlow, dhigh = sb("dlow", [P, 2]), sb("dhigh", [P, 2])
        dlowi, dwini, doffi = sb("dlowi", [P, 2], I32), sb("dwini", [P, 2], I32), sb("doffi", [P, 2], I32)
        doff, wide, widest = sb("doff", [P, 2]), sb("wide", [P, 2]), sb("widest", [P, 1])
        flag = sb("flag", [1, 1], I32)
        low_tab, win_tab = sb("low_tab", [1, NG], I32), sb("win_tab", [1, NG], I32)
        unit_win, unit_row = sb("unit_win", [1, NU], I32), sb("unit_row", [1, NU], I32)
        fill_row = sb("fill_row", [1, NTP], I32)
        zeros = sb("zeros", [P, UR // P, MW])

        at = 0
        big = area(at, [RING, CPG, MW])
        at += RING * CPG * MW
        hot = area(at, [2, CPG, 2 * P])
        at += 2 * CPG * 2 * P
        tab = area(at, [2, D])
        at += 2 * D
        place_b = area(at, [2, GE])
        at += 2 * GE
        unit = area(at, [RING, 2, MW])
        stage = sb("stage", [P, RING, CPG], I32)
        xr, st = area(0, [2, D]), area(2 * D, [2, 2 * D])
        at = 6 * NC
        hr = area(at, [2, D])
        gb = area(at + 512, [2, 2 * D])
        ub = area(at + 1536, [2, 2 * D])
        tT = area(at + 2560, [2, 6 * P])
        bn6, mv = sb("bn6", [P, 6]), sb("mv", [P, NT, 2])
        rstd, mv_t = sb("rstd", [P, NT]), sb("mv_t", [P, 2])

        ps = [pb(f"ps{i}", [P, 2 * D]) for i in range(8)]

        names = """ld_raw ld_w ld_x cst d1 p1 a1 cast tr trv trd lowrow lowtab placed flagged
        e1 e2 e3 zf rows_ready sum1 sq sqd sum2 stats h_ready hT hTd mm tabd tab_free0 tab_free1 zt
        gs_rec gs_pos gs_sc gs_rl gs_init gs_d pos_ready
        g_stage g_hot g_mm g_acc g_g dacc
        ax_f bx_f dd pp aa f_xl f_h f_st f_tr f_ev f_mm f_u f_act f_dv f_y
        r1 n1 n2 s2 s2q s2d z_r z_s l_st l_tr l_ev l_mm l_y o_r o_s0 o_s1 gate_pool gate_act gate_dve xl0 xl1 zs0 zs1
        clear_a clear_c done_xi done_a done_o done_l1 done_rb0 done_rb1 fin_y fin_y2 r2 msg_zero""".split()
        S = {n: sem(n) for n in names}
        g_rows = [sem(f"g_rows{k}") for k in range(RING)]
        tab_store = [sem(f"tab_store{k}") for k in range(2)]

        def pass_sems(tag):
            return {
                **{n: sem(f"{tag}_{n}") for n in ("hot", "mm", "msg", "key", "rb_hot", "rb_mm", "rb_acc")},
                "load": [sem(f"{tag}_load{k}") for k in range(2)],
                "sent": [sem(f"{tag}_sent{k}") for k in range(RING)],
                "rb_load": [sem(f"{tag}_rb_load{k}") for k in range(RING)],
            }

        X = [pass_sems("out"), pass_sems("l1")]
        LAST = TAIL

        def by_group(v):
            return v.rearrange("p (g j) -> p j g", j=CPG)

        block = ctx.enter_context(nc.Block())

        @block.sync
        def _(sp):
            sp.wait_ge(S["cst"], 1)
            full2 = (E - P * GE) // GE
            rest = E - (P + full2) * GE
            for k, (a, to) in enumerate(((src, raw_si), (dst, raw_di), (edge_weight, raw[2]), (edge_weight_n2, raw[3]))):
                v = to.rearrange("p (h q) -> p h q", h=2)
                for s, d in ((a[0:P * GE].rearrange("(g q) -> g q", q=GE), v[:, 0, :]),
                             (a[P * GE:(P + full2) * GE].rearrange("(g q) -> g q", q=GE), v[0:full2, 1, :]),
                             (a[(P + full2) * GE:E].rearrange("(g q) -> g q", g=1), v[full2:full2 + 1, 1, 0:rest])):
                    sp.dma_start(d, s).then_inc(S["ld_raw"], 16)
            sp.wait_ge(S["clear_a"], 1)
            sp.dma_start(node_a[:, 0:FULL, :], x[0:FULL * P, :].rearrange("(t p) d -> p t d", p=P)).then_inc(S["ld_x"], 16)
            sp.dma_start(node_a[0:TAIL, FULL, :], x[FULL * P:N, :]).then_inc(S["ld_x"], 16)

            def store_tables(t, slot_, n):
                sp.wait_ge(S["tabd"], t + 1)
                for k, tb in enumerate((in_table, out_table)):
                    sp.dma_start(tb[bass.ds(t * P, P), :], ub[:, slot_, k * D:(k + 1) * D]).then_inc(tab_store[slot_], 16)

            def tables(i, first):
                for s in range(2):
                    store_tables(i * 2 + s, s, s)
            loop(sp, FULL // 2, tables)
            store_tables(FULL, 0, 0)
            sp.wait_ge(S["p1"], 5)
            for tb in (in_table, out_table, z_table):
                sp.dma_start(tb[NT * P:NTP * P, :], zeros[:, 0, 0:D]).then_inc(S["zt"], 16)

            sp.wait_ge(S["flagged"], 1)
            general = nc.sync.value_load(flag[0:1, 0:1], min_val=0, max_val=1)
            with sp.If(general):
                for g in range(NG // 16):
                    sp.wait_ge(S["gs_init"], 1)
                    sp.dma_start(records[g * 16 * GE:(g + 1) * 16 * GE, :].rearrange("(p q) k -> p (q k)", p=P),
                                 rec[:, 0:16 * GE // P, :].rearrange("p q k -> p (q k)")).then_inc(S["gs_rec"], 16)
                sp.wait_ge(S["gs_sc"], 16 * NC)
                rv = records.rearrange("(h g q) k -> h g (q k)", h=2, q=GE)
                for hh in range(2):
                    sp.dma_start(reload[:, hh, :, :].rearrange("p q k -> p (q k)"), rv[hh]).then_inc(S["gs_rl"], 16)

            sp.wait_ge(S["lowrow"], 1)
            for k, v in ((0, dlowi), (1, dwini)):
                sp.dma_start(group_row[k, :].rearrange("(h g) -> g h", h=2), v[:, :], allow_slow_non_contiguous=True).then_inc(S["lowtab"], 16)
            sp.dma_start(place_row.rearrange("(h g q) -> g h q", h=2, q=GE),
                         raw_place.rearrange("p (h q) -> p h q", h=2)).then_inc(S["placed"], 16)
            sp.wait_ge(S["lowtab"], 32)
            sp.dma_start(low_tab[:, :], group_row[0:1, :]).then_inc(S["lowtab"], 16)
            sp.dma_start(win_tab[:, :], group_row[1:2, :]).then_inc(S["lowtab"], 16)

            sp.wait_ge(S["rows_ready"], 1)
            for w in range(NT):
                r = nc.sync.value_load(fill_row[0:1, w:w + 1], min_val=0, max_val=NU * UR - UR)
                sp.dma_start(messages[bass.ds(r, UR), :].rearrange("(p j) c -> p j c", p=P), zeros[:, :, :]).then_inc(S["msg_zero"], 16)

            def edge_pass(q, table, groups, start):
                def body(i, first):
                    for s in range(2):
                        g = 2 * i + s
                        if start or not first:
                            sp.wait_ge(q["mm"], g - 1)
                        r = nc.sync.value_load(low_tab[0:1, bass.ds(g, 1)], min_val=0, max_val=N - 1)
                        sp.dma_start(tab[:, s, :], table[bass.ds(r, P), :]).then_inc(q["load"][s], 16)
                        sp.dma_start(place_b[:, s, :], place_row[bass.ds(g * GE, GE)].rearrange("(o q) -> o q", o=1).broadcast_to([P, GE])).then_inc(q["load"][s], 16)
                if start:
                    with sp.Fori(start // 2, groups // 2) as i:
                        body(i, False)
                else:
                    loop(sp, groups // 2, body)

            def read_back(q):
                def body(i, first):
                    for s in range(RING):
                        u = RING * i + s
                        if not first:
                            sp.wait_ge(q["rb_mm"], u - RING + 1)
                        r = nc.sync.value_load(unit_row[0:1, bass.ds(u, 1)], min_val=0, max_val=NU * UR - UR)
                        sp.dma_start(unit[:, s, :, :], messages[bass.ds(r, UR), :].rearrange("(p j) c -> p j c", p=P)).then_inc(q["rb_load"][s], 16)
                loop(sp, NU // RING, body)

            def sent(q):
                for k in range(RING):
                    if True:
                        sp.wait_ge(q["sent"][k], 16 * CPG * NG_PLAIN // RING)
                with sp.If(general):
                    for k in range(RING):
                        sp.wait_ge(q["sent"][k], 16 * CPG * NG // RING)

            sp.wait_ge(tab_store[0], 32 * (FULL // 2 + 1))
            sp.wait_ge(tab_store[1], 32 * (FULL // 2))
            sp.wait_ge(S["zt"], 48)
            sp.wait_ge(S["placed"], 16)
            sp.wait_ge(S["lowtab"], 64)
            sp.sem_inc(S["h_ready"], 1)
            edge_pass(X[0], out_table, NG_PLAIN, 0)
            with sp.If(general):
                edge_pass(X[0], out_table, NG, NG_PLAIN)
            sent(X[0])
            read_back(X[0])

            def x_tile(t, s, wait):
                if wait is not None:
                    sp.wait_ge(S["f_y"], wait)
                sp.dma_start(xr[:, s, :], x[bass.ds(t * P, P), :]).then_inc(S["xl0" if s == 0 else "xl1"], 16)

            def x_tiles(i, first):
                for s in range(2):
                    t = 2 * i + s
                    x_tile(t, s, None if first else t - 1)
            sp.wait_ge(S["f_xl"], 1)
            loop(sp, FULL // 2, x_tiles)
            sp.wait_ge(S["f_y"], FULL - 1)
            sp.dma_start(xr[0:TAIL, 0, :], x[FULL * P:N, :]).then_inc(S["xl0"], 16)

            def z_store(t, s):
                sp.wait_ge(S["z_r"], t + 1)
                sp.dma_start(z_table[bass.ds(t * P, P), :], hr[:, s, :]).then_inc(S["zs0" if s == 0 else "zs1"], 16)

            def z_stores(i, first):
                for s in range(2):
                    z_store(2 * i + s, s)
            loop(sp, FULL // 2, z_stores)
            z_store(FULL, 0)
            sp.wait_ge(S["zs0"], 16 * (FULL // 2 + 1))
            sp.wait_ge(S["zs1"], 16 * (FULL // 2))
            edge_pass(X[1], z_table, NG_PLAIN, 0)
            with sp.If(general):
                edge_pass(X[1], z_table, NG, NG_PLAIN)
            sent(X[1])
            read_back(X[1])

            def o_store(t, s):
                sp.wait_ge(S["o_r"], t + 1)
                sp.dma_start(out[bass.ds(t * P, P), :], gb[:, s, 0:D]).then_inc(S["o_s0" if s == 0 else "o_s1"], 16)

            def o_stores(i, first):
                for s in range(2):
                    o_store(2 * i + s, s)
            loop(sp, FULL // 2, o_stores)
            sp.wait_ge(S["o_r"], NT)
            sp.dma_start(out[FULL * P:N, :], gb[0:TAIL, 0, 0:D]).then_inc(S["o_s0"], 16)
            sp.wait_ge(S["o_s0"], 16 * (FULL // 2 + 1))
            sp.wait_ge(S["o_s1"], 16 * (FULL // 2))
            sp.wait_ge(S["msg_zero"], 16 * NT)

        @block.gpsimd
        def _(pool):
            link = Chain(pool, S["p1"])
            nc.gpsimd.memset(ones[:, :], 1.0)
            nc.gpsimd.memset(zeros[:, :, :], 0.0)
            nc.gpsimd.memset(eps_c[:, :], EPS)
            link(nc.gpsimd.memset(ident[:, :], 0.0))
            link(nc.gpsimd.affine_select(out=ident[:, :], in_=ident[:, :], compare_op=ALU.not_equal, fill=1.0,
                                         base=0, pattern=[[-1, P]], channel_multiplier=1))
            link(nc.gpsimd.affine_select(out=upper[:, :], in_=ones[:, :], compare_op=ALU.is_gt, fill=0.0,
                                         base=0, pattern=[[1, P]], channel_multiplier=-1))
            nc.gpsimd.iota(iota2[:, :], [[1, 2 * P]], base=0, channel_multiplier=0, allow_small_or_imprecise_dtypes=True)
            nc.gpsimd.iota(iota_u[:, :], [[UR, NU]], base=0, channel_multiplier=0, allow_small_or_imprecise_dtypes=True)
            nc.gpsimd.iota(pcol[:, :], [[0, 1]], base=0, channel_multiplier=1, allow_small_or_imprecise_dtypes=True)
            nc.gpsimd.iota(iota_w[:, :], [[1, NTP]], base=0, channel_multiplier=0, allow_small_or_imprecise_dtypes=True).then_inc(S["p1"], 2)

            pool.wait_ge(S["flagged"], 1)
            general = nc.gpsimd.value_load(flag[0:1, 0:1], min_val=0, max_val=1)
            with pool.If(general):
                pool.wait_ge(S["gs_rec"], 16 * (NG // 16))
                for c in range(0):
                    pass

                def put(i, first):
                    pool.wait_ge(S["gs_pos"], i + 1)
                    pool.sem_inc(S["gate_pool"], 1)
                    for j in range(RING):
                        nc.gpsimd.indirect_dma_start(
                            out=records, out_offset=bass.IndirectOffsetOnAxis(ap=stage[:, j, 0:1], axis=0),
                            in_=rec_put[:, j, :], in_offset=None, bounds_check=NG * GE - 1, oob_is_err=False).then_inc(S["gs_sc"], 16)
                loop(pool, NC // RING, put)

            def scatter(q, lo, hi):
                def body(i, first):
                    for s in range(RING):
                        g = RING * i + s
                        pool.wait_ge(q["msg"], g + 1)
                        pool.wait_ge(q["key"], g + 1)
                        pool.sem_inc(S["gate_pool"], 1)
                        for j in range(CPG):
                            nc.gpsimd.indirect_dma_start(
                                out=messages, out_offset=bass.IndirectOffsetOnAxis(ap=stage[:, s, j:j + 1], axis=0),
                                in_=big[:, s, j, :], in_offset=None).then_inc(q["sent"][s], 16)
                if lo:
                    with pool.Fori(lo // RING, hi // RING) as i:
                        body(i, False)
                else:
                    loop(pool, hi // RING, body)

            pool.wait_ge(S["msg_zero"], 16 * NT)
            pool.sem_inc(S["gate_pool"], 1)
            scatter(X[0], 0, NG_PLAIN)
            with pool.If(general):
                scatter(X[0], NG_PLAIN, NG)

            def gather(lo, hi):
                def body(i, first):
                    for s in range(RING):
                        g = RING * i + s
                        pool.wait_ge(S["g_stage"], g + 1)
                        pool.sem_inc(S["gate_pool"], 1)
                        for j in range(CPG):
                            nc.gpsimd.indirect_dma_start(
                                out=big[:, s, j, 0:D], out_offset=None, in_=in_table,
                                in_offset=bass.IndirectOffsetOnAxis(ap=stage[:, s, j:j + 1], axis=0)).then_inc(g_rows[s], 16)
                if lo:
                    with pool.Fori(lo // RING, hi // RING) as i:
                        body(i, False)
                else:
                    loop(pool, hi // RING, body)
            gather(0, NG_PLAIN)
            with pool.If(general):
                gather(NG_PLAIN, NG)
            scatter(X[1], 0, NG_PLAIN)
            with pool.If(general):
                scatter(X[1], NG_PLAIN, NG)

        @block.scalar
        def _(act):
            for d, s in ((wio[:, :, 0:D], w_in.rearrange("(k p) n -> p k n", p=P)),
                         (wio[:, :, D:2 * D], w_out.rearrange("(k p) n -> p k n", p=P)),
                         (wx[:, :, :], w_x2i.rearrange("(k p) n -> p k n", p=P)),
                         (wh[:, :, :], w_h2h.rearrange("(k p) n -> p k n", p=P)),
                         (w1[:, :, :], w_l1.rearrange("(k p) n -> p k n", p=P)),
                         (gamma_b[:, :], gamma.rearrange("(o n) -> o n", o=1).broadcast_to([P, D])),
                         (beta_b[:, :], beta.rearrange("(o n) -> o n", o=1).broadcast_to([P, D])),
                         (bio_b[:, 0:D], b_in.rearrange("(o n) -> o n", o=1).broadcast_to([P, D])),
                         (bio_b[:, D:2 * D], b_out.rearrange("(o n) -> o n", o=1).broadcast_to([P, D])),
                         (bx_b[:, :], b_x2i.rearrange("(o n) -> o n", o=1).broadcast_to([P, 2 * D])),
                         (b1_b[:, :], b_l1.rearrange("(o n) -> o n", o=1).broadcast_to([P, D]))):
                act.dma_start(d, s).then_inc(S["ld_w"], 16)
            def squares(count, made, used, into, signal):
                def body(i, first):
                    for s in range(2):
                        t = 2 * i + s
                        act.wait_ge(made, t + 1)
                        if not first:
                            act.wait_ge(used, t - 1)
                        nc.scalar.activation(gb[:, s, 0:D], into[:, s, :], ACT.Square).then_inc(signal, 1)
                loop(act, count // 2, body)
                act.wait_ge(made, count + 1)
                act.wait_ge(used, count - 1)
                nc.scalar.activation(gb[:, 0, 0:D], into[:, 0, :], ACT.Square).then_inc(signal, 1)

            squares(FULL, S["sq"], S["sum2"], hr, S["sqd"])
            act.wait_ge(S["stats"], 1)
            nc.scalar.activation(scale_b[:, :], scale_b[:, :], ACT.Sqrt, bias=eps_c[:, :]).then_inc(S["stats"], 1)

            def out_of_psum(t, s, first):
                act.wait_ge(S["hT"], t + 1)
                if not first:
                    act.wait_ge(S["mm"], t - 1)
                nc.scalar.activation(tT[:, s, 0:D], ps[s][:, 0:D], ACT.Copy).then_inc(S["hTd"], 1)

            def outs(i, first):
                for s in range(2):
                    out_of_psum(2 * i + s, s, first)
            loop(act, FULL // 2, outs)
            out_of_psum(FULL, 0, False)

            act.wait_ge(S["flagged"], 1)
            general = nc.scalar.value_load(flag[0:1, 0:1], min_val=0, max_val=1)

            def messages_of(q, weight, lo, hi):
                def body(i, first):
                    for s in range(RING):
                        g = RING * i + s
                        act.wait_ge(q["mm"], g + 1)
                        if not first:
                            act.wait_ge(q["sent"][s], i * 16 * CPG)
                        act.sem_inc(S["gate_act"], 1)
                        for j in range(CPG):
                            b = ps[2 * (s % 2) + j // 2]
                            last = nc.scalar.activation(big[:, s, j, 0:D], b[:, (j % 2) * D:(j % 2 + 1) * D], ACT.Copy,
                                                        scale=weight[:, bass.ds(g * CPG + j, 1)])
                        last.then_inc(q["msg"], 1)
                if lo:
                    with act.Fori(lo // RING, hi // RING) as i:
                        body(i, False)
                else:
                    loop(act, hi // RING, body)

            act.wait_ge(S["pos_ready"], 1)
            act.sem_inc(S["gate_act"], 1)
            messages_of(X[0], ow_col, 0, NG_PLAIN)
            with act.If(general):
                messages_of(X[0], ow_col, NG_PLAIN, NG)

            def gates(t, s, first):
                act.wait_ge(S["f_h"], t + 1)
                if not first:
                    act.wait_ge(S["f_tr"], t - 1)
                act.sem_inc(S["gate_act"], 1)
                nc.scalar.activation(st[:, s, 0:D], node_a[:, bass.ds(t, 1), :], ACT.Copy)
                nc.scalar.activation(st[:, s, D:2 * D], node_c[:, bass.ds(t, 1), :], ACT.Copy).then_inc(S["f_st"], 1)
                act.wait_ge(S["f_tr"], t + 1)
                if not first:
                    act.wait_ge(S["f_mm"], t - 1)
                nc.scalar.activation(tT[:, s, 0:4 * P], ps[2 * s][:, :], ACT.Copy)
                nc.scalar.activation(tT[:, s, 4 * P:6 * P], ps[2 * s + 1][:, 0:2 * P], ACT.Copy).then_inc(S["f_ev"], 1)
                act.wait_ge(S["f_u"], t + 1)
                nc.scalar.activation(gb[:, s, 0:D], ub[:, s, 0:D], ACT.Sigmoid)
                nc.scalar.activation(gb[:, s, D:2 * D], ub[:, s, D:2 * D], ACT.Tanh).then_inc(S["f_act"], 1)

            def gates2(i, first):
                for s in range(2):
                    gates(2 * i + s, s, first)
            loop(act, FULL // 2, gates2)
            gates(FULL, 0, False)

            act.wait_ge(S["r1"], 1)
            nc.scalar.activation(rstd[:, :], mv[:, :, 1], ACT.Sqrt, bias=eps_c[:, :]).then_inc(S["r1"], 1)
            squares(FULL, S["s2"], S["s2q"], hr, S["s2d"])
            act.wait_ge(S["n1"], 1)
            nc.scalar.activation(scale2_b[:, :], scale2_b[:, :], ACT.Sqrt).then_inc(S["n1"], 1)

            messages_of(X[1], iw_col, 0, NG_PLAIN)
            with act.If(general):
                messages_of(X[1], iw_col, NG_PLAIN, NG)

            def l1(t, s, first):
                if first and s == 0:
                    act.wait_ge(S["done_l1"], 1)
                if not first:
                    act.wait_ge(S["l_tr"], t - 1)
                act.sem_inc(S["gate_act"], 1)
                nc.scalar.activation(st[:, s, 0:D], node_c[:, bass.ds(t, 1), :], ACT.Copy).then_inc(S["l_st"], 1)
                act.wait_ge(S["l_tr"], t + 1)
                if not first:
                    act.wait_ge(S["l_mm"], t - 1)
                nc.scalar.activation(tT[:, s, 0:2 * P], ps[s][:, 0:2 * P], ACT.Copy).then_inc(S["l_ev"], 1)

            def l1s(i, first):
                for s in range(2):
                    l1(2 * i + s, s, first)
            loop(act, FULL // 2, l1s)
            l1(FULL, 0, False)
            act.wait_ge(S["r2"], 1)
            nc.scalar.activation(rstd[:, :], mv[:, :, 1], ACT.Sqrt, bias=eps_c[:, :]).then_inc(S["r2"], 1)

        @block.tensor
        def _(pe):
            pe.wait_ge(S["p1"], 5)

            def node_sum(to, table, ready, signal):
                def one(t):
                    if ready is not None:
                        pe.wait_ge(ready, t + 1)
                pe.wait_ge(ready, 1) if ready is not None else None
                nc.tensor.matmul(to, ones[:, :], table[:, 0, :], start=True, stop=False)
                with pe.Fori(1, FULL) as t:
                    if ready is not None:
                        pe.wait_ge(ready, t + 1)
                    nc.tensor.matmul(to, ones[:, :], table[:, bass.ds(t, 1), :], start=False, stop=False)
                if ready is not None:
                    pe.wait_ge(ready, NT)
                nc.tensor.matmul(to, ones[0:TAIL, :], table[0:TAIL, FULL, :], start=False, stop=True).then_inc(signal, 1)

            def square_sum(to, made, used):
                def one(i, s, first):
                    t = 2 * i + s
                    pe.wait_ge(made, t + 1)
                    nc.tensor.matmul(to, ones[:, :], gb[:, s, 0:D], start=first and s == 0, stop=False).then_inc(used, 1)

                def body(i, first):
                    for s in range(2):
                        one(i, s, first)
                loop(pe, FULL // 2, body)
                pe.wait_ge(made, NT)
                nc.tensor.matmul(to, ones[0:TAIL, :], gb[0:TAIL, 0, 0:D], start=False, stop=True).then_inc(used, 1)

            pe.wait_ge(S["ld_x"], 32)
            node_sum(ps[4][:, 0:D], node_a, None, S["sum1"])
            square_sum(ps[5][:, 0:D], S["sqd"], S["sum2"])

            pe.wait_ge(S["ld_w"], 176)

            def table(t, s, first):
                pe.wait_ge(S["h_ready"], t + 1)
                if not first:
                    pe.wait_ge(S["hTd"], t - 1)
                for k in range(2):
                    last = nc.tensor.transpose(ps[s][:, k * P:(k + 1) * P], hr[:, s, k * P:(k + 1) * P], ident[:, :])
                last.then_inc(S["hT"], 1)
                pe.wait_ge(S["hTd"], t + 1)
                if not first:
                    pe.wait_ge(S["tabd"], t - 1)
                for k in range(2):
                    last = nc.tensor.matmul(ps[2 + s][:, :], tT[:, s, k * P:(k + 1) * P], wio[:, k, :], start=k == 0, stop=k == 1)
                last.then_inc(S["mm"], 1)

            def tables(i, first):
                for s in range(2):
                    table(2 * i + s, s, first)
            loop(pe, FULL // 2, tables)
            table(FULL, 0, False)

            pe.wait_ge(S["e1"], 1)
            nc.tensor.matmul(ps[6][:, 0:1], ones[:, :], widest[:, :], start=True, stop=True).then_inc(S["e1"], 1)

            def to_columns(arrays, n0):
                n = n0
                for v in arrays:
                    vv = v.rearrange("p (h j q) -> p h j q", h=2, j=CPG)
                    for hh in range(2):
                        if n >= 2:
                            pe.wait_ge(S["trv"], n - 1)
                        for j in range(CPG):
                            last = nc.tensor.transpose(ps[6 + n % 2][:, j * P:(j + 1) * P], vv[:, hh, j, :], ident[:, :])
                        last.then_inc(S["tr"], 1)
                        n += 1

            def place_sums(ready, done):
                pe.wait_ge(ready, 1)
                nc.tensor.matmul(ps[6][:, 0:NTP], upper[:, :], cnt[:, :], start=True, stop=True)
                nc.tensor.matmul(ps[7][:, 0:NTP], ones[:, :], cnt[:, :], start=True, stop=True).then_inc(done, 1)

            pe.wait_ge(S["flagged"], 1)
            general = nc.tensor.value_load(flag[0:1, 0:1], min_val=0, max_val=1)
            with pe.If(general):
                for n, v in enumerate(raw):
                    vv = v.rearrange("p (h j q) -> p h j q", h=2, j=CPG)
                    for hh in range(2):
                        if n or hh:
                            pe.wait_ge(S["gs_d"], 2 * n + hh)
                        for j in range(CPG):
                            last = nc.tensor.transpose(ps[6][:, j * P:(j + 1) * P], vv[:, hh, j, :], ident[:, :])
                        last.then_inc(S["pp"], 1)
                place_sums(S["ax_f"], S["bx_f"])
            pe.wait_ge(S["cast"], 1)
            to_columns([raw[0], raw[2], raw[3], raw_place2], 0)
            place_sums(S["e2"], S["e3"])
            pe.wait_ge(S["e2"], 2)
            nc.tensor.matmul(ps[6][:, 0:NU], ones[0:NT, :], mask[0:NT, 0:NU], start=True, stop=True).then_inc(S["e3"], 1)

            def expand(q, lo, hi):
                def body(i, first):
                    for s in range(2):
                        g = 2 * i + s
                        pe.wait_ge(q["hot"], g + 1)
                        if not first:
                            pe.wait_ge(q["msg"], g - 1)
                        for j in range(CPG):
                            b = ps[2 * s + j // 2]
                            last = nc.tensor.matmul(b[:, (j % 2) * D:(j % 2 + 1) * D], hot[:, s, :, :].rearrange("p a b -> p (a b)")[:, j * P:(j + 1) * P],
                                                    tab[:, s, :], start=True, stop=True)
                        last.then_inc(q["mm"], 1)
                if lo:
                    with pe.Fori(lo // 2, hi // 2) as i:
                        body(i, False)
                else:
                    loop(pe, hi // 2, body)

            def collect(q):
                def body(i, first):
                    for s in range(2):
                        u = 2 * i + s
                        pe.wait_ge(q["rb_hot"], u + 1)
                        if not first:
                            pe.wait_ge(q["rb_acc"], u - 1)
                        raise_ = None
                loop(pe, 0 or 1, lambda i, first: None)

            def collect_units(q):
                def body(i, first):
                    for s in range(RING):
                        u = RING * i + s
                        h = s % 2
                        pe.wait_ge(q["rb_hot"], u + 1)
                        if not (first and s < 2):
                            pe.wait_ge(q["rb_acc"], u - 1)
                        for j in range(2):
                            last = nc.tensor.matmul(ps[4 + h][:, 0:D], hot[:, h, j, 0:P], unit[:, s, j, 0:D], start=j == 0, stop=j == 1)
                        last.then_inc(q["rb_mm"], 1)
                loop(pe, NU // RING, body)

            pe.wait_ge(S["pos_ready"], 1)
            expand(X[0], 0, NG_PLAIN)
            with pe.If(general):
                expand(X[0], NG_PLAIN, NG)

            def add_in_edges(lo, hi):
                def body(i, first):
                    for s in range(RING):
                        g = RING * i + s
                        h = s % 2
                        pe.wait_ge(g_rows[s], (i + 1) * 16 * CPG)
                        pe.wait_ge(S["g_hot"], g + 1)
                        if not (first and s < 2):
                            pe.wait_ge(S["g_acc"], g - 1)
                        for w in range(2):
                            for j in range(CPG):
                                last = nc.tensor.matmul(ps[4 + h][:, w * D:(w + 1) * D], hot[:, h, j, w * P:(w + 1) * P],
                                                        big[:, s, j, 0:D], start=j == 0, stop=j == CPG - 1)
                        last.then_inc(S["g_mm"], 1)
                if lo:
                    with pe.Fori(lo // RING, hi // RING) as i:
                        body(i, False)
                else:
                    loop(pe, hi // RING, body)

            add_in_edges(0, NG_PLAIN)
            with pe.If(general):
                add_in_edges(NG_PLAIN, NG)
            collect_units(X[0])

            def layer0(t, s, first):
                pe.wait_ge(S["f_st"], t + 1)
                if not first:
                    pe.wait_ge(S["f_ev"], t - 1)
                for k in range(6):
                    v = st[:, s, k * P:(k + 1) * P] if k < 4 else hr[:, s, (k - 4) * P:(k - 3) * P]
                    o = ps[2 * s + k // 4]
                    last = nc.tensor.transpose(o[:, (k % 4) * P:(k % 4 + 1) * P], v, ident[:, :])
                last.then_inc(S["f_tr"], 1)
                pe.wait_ge(S["f_ev"], t + 1)
                if not first:
                    pe.wait_ge(S["f_u"], t - 1)
                for k in range(6):
                    v = wx[:, k, :] if k < 4 else wh[:, k - 4, :]
                    last = nc.tensor.matmul(ps[4 + s][:, :], tT[:, s, k * P:(k + 1) * P], v, start=k == 0, stop=k == 5)
                last.then_inc(S["f_mm"], 1)

            def layer0s(i, first):
                for s in range(2):
                    layer0(2 * i + s, s, first)
            loop(pe, FULL // 2, layer0s)
            layer0(FULL, 0, False)

            node_sum(ps[6][:, 0:D], node_a, S["n2"], S["sum1"])
            square_sum(ps[7][:, 0:D], S["s2d"], S["s2q"])

            expand(X[1], 0, NG_PLAIN)
            with pe.If(general):
                expand(X[1], NG_PLAIN, NG)
            collect_units(X[1])

            def layer1(t, s, first):
                pe.wait_ge(S["l_st"], t + 1)
                if not first:
                    pe.wait_ge(S["l_ev"], t - 1)
                for k in range(2):
                    last = nc.tensor.transpose(ps[s][:, k * P:(k + 1) * P], st[:, s, k * P:(k + 1) * P], ident[:, :])
                last.then_inc(S["l_tr"], 1)
                pe.wait_ge(S["l_ev"], t + 1)
                if not first:
                    pe.wait_ge(S["l_y"], t - 1)
                for k in range(2):
                    last = nc.tensor.matmul(ps[2 + s][:, 0:D], tT[:, s, k * P:(k + 1) * P], w1[:, k, :], start=k == 0, stop=k == 1)
                last.then_inc(S["l_mm"], 1)

            def layer1s(i, first):
                for s in range(2):
                    layer1(2 * i + s, s, first)
            loop(pe, FULL // 2, layer1s)
            layer1(FULL, 0, False)

        @block.vector
        def _(dve):
            link = Chain(dve, S["d1"])
            V = nc.vector
            for v, c in ((raw_si, NT * P), (raw_di, N - 1)):
                V.memset(v[:, GE:2 * GE], c)
            V.memset(raw[2][:, GE:2 * GE], 0.0)
            link(V.memset(raw[3][:, GE:2 * GE], 0.0))
            dve.sem_inc(S["cst"], 1)
            link(V.memset(node_a[:, FULL:NTP, :], 0.0))
            dve.sem_inc(S["clear_a"], 1)
            dve.wait_ge(S["ld_raw"], 192)
            V.tensor_copy(raw[0], raw_si)
            link(V.tensor_copy(raw[1], raw_di))

            def by_half(v):
                return v.rearrange("p (h q) -> p h q", h=2)

            def low_high():
                V.tensor_reduce(dlow[:, :], by_half(raw[1]), AX.X, ALU.min)
                link(V.tensor_reduce(dhigh[:, :], by_half(raw[1]), AX.X, ALU.max))

            low_high()
            link(V.tensor_tensor(wide[:, :], dhigh[:, :], dlow[:, :], ALU.subtract))
            link(V.tensor_scalar(wide[:, :], wide[:, :], float(P - 1), None, ALU.is_gt))
            V.tensor_reduce(widest[:, :], wide[:, :], AX.X, ALU.max).then_inc(S["e1"], 1)

            dve.wait_ge(S["sum1"], 1)
            link(V.tensor_scalar(mean_b[:, :], ps[4][:, 0:D], 1.0 / N, None, ALU.mult))

            def centred(table, mean, made, used):
                def one(t, s, first):
                    if not first:
                        dve.wait_ge(used, t - 1)
                    V.tensor_tensor(hr[:, s, :], table[:, bass.ds(t, 1), :].rearrange("p o d -> p (o d)"), mean, ALU.subtract).then_inc(made, 1)

                def body(i, first):
                    for s in range(2):
                        one(2 * i + s, s, first)
                loop(dve, FULL // 2, body)
                dve.wait_ge(used, FULL - 1)
                V.tensor_tensor(hr[:, 0, :], table[:, FULL, :], mean, ALU.subtract).then_inc(made, 1)

            centred(node_a, mean_b[:, :], S["sq"], S["sqd"])
            dve.wait_ge(S["sum2"], NT)
            V.tensor_scalar(scale_b[:, :], ps[5][:, 0:D], 1.0 / N, None, ALU.mult).then_inc(S["stats"], 1)
            dve.wait_ge(S["stats"], 2)
            link(V.reciprocal(scale_b[:, :], scale_b[:, :]))
            dve.wait_ge(S["ld_w"], 176)
            link(V.tensor_tensor(scale_b[:, :], scale_b[:, :], gamma_b[:, :], ALU.mult))

            def normal(to, v, chain):
                chain(V.tensor_tensor(to, v, mean_b[:, :], ALU.subtract))
                chain(V.tensor_tensor(to, to, scale_b[:, :], ALU.mult))
                return V.tensor_tensor(to, to, beta_b[:, :], ALU.add)

            def h_tile(t, s, first):
                if not first:
                    dve.wait_ge(S["hT"], t - 1)
                normal(hr[:, s, :], node_a[:, bass.ds(t, 1), :].rearrange("p o d -> p (o d)"), Chain(dve, S["dd"], t * 2)).then_inc(S["h_ready"], 1)

            def table_tile(t, s, first):
                dve.wait_ge(S["mm"], t + 1)
                if not first:
                    dve.wait_ge(tab_store[s], tab_count(t, s))
                V.tensor_tensor(ub[:, s, :], ps[2 + s][:, :], bio_b[:, :], ALU.add).then_inc(S["tabd"], 1)

            def tab_count(t, s):
                return 0

            def tile_pair(i, first):
                for s in range(2):
                    h_tile(2 * i + s, s, first)
                for s in range(2):
                    dve.wait_ge(S["mm"], 2 * i + s + 1)
                    if not first:
                        dve.wait_ge(tab_store[s], 32 * i)
                    V.tensor_tensor(ub[:, s, :], ps[2 + s][:, :], bio_b[:, :], ALU.add).then_inc(S["tabd"], 1)
            loop(dve, FULL // 2, tile_pair)
            h_tile(FULL, 0, False)
            dve.wait_ge(S["mm"], NT)
            dve.wait_ge(tab_store[0], 32 * (FULL // 2))
            V.tensor_tensor(ub[:, 0, :], ps[2][:, :], bio_b[:, :], ALU.add).then_inc(S["tabd"], 1)

            dve.wait_ge(S["e1"], 2)
            link(V.tensor_scalar(flag[0:1, 0:1], ps[6][0:1, 0:1], 1.0, None, ALU.min))
            dve.sem_inc(S["flagged"], 1)
            general = V.value_load(flag[0:1, 0:1], min_val=0, max_val=1)

            def counts(w_of, sem_, base):
                link(V.memset(rank, 0.0))

                def body(w, first):
                    chain = Chain(dve, sem_, w * 4)
                    chain(V.tensor_scalar(mask, w_of, iota_w[:, bass.ds(w, 1)], None, ALU.is_equal))
                    chain(V.tensor_tensor_scan(scan, mask, mask, 0.0, ALU.add, ALU.max))
                    V.tensor_copy(cnt[:, bass.ds(w, 1)], scan[:, NC - 1:NC])
                    chain(V.tensor_tensor(mask, scan, mask, ALU.mult))
                    chain(V.tensor_tensor(rank, rank, mask, ALU.add))
                with dve.Fori(0, NTP) as w:
                    body(w, False)

            def starts_of(align, ready, done):
                dve.sem_inc(ready, 1)
                dve.wait_ge(done, 1)
                link(V.tensor_copy(aligi[:, :], ps[7][:, 0:NTP]))
                link(V.tensor_scalar(aligi[:, :], aligi[:, :], ~(align - 1), None, ALU.bitwise_and))
                link(V.tensor_scalar(alig[:, :], aligi[:, :], float(align), None, ALU.add))
                link(V.tensor_tensor_scan(ends[:, :], alig[:, :], alig[:, :], 0.0, ALU.add, ALU.max))
                link(V.tensor_tensor(starts[:, :], ends[:, :], alig[:, :], ALU.subtract))
                link(V.scalar_tensor_tensor(basew[:, :], starts[:, :], -1.0, ps[6][:, 0:NTP], ALU.add, ALU.add))

            def add_bases(w_of, sem_):
                def body(w, first):
                    chain = Chain(dve, sem_, w * 2)
                    chain(V.tensor_scalar(mask, w_of, iota_w[:, bass.ds(w, 1)], basew[:, bass.ds(w, 1)], ALU.is_equal, ALU.mult))
                    chain(V.tensor_tensor(rank, rank, mask, ALU.add))
                with dve.Fori(0, NTP) as w:
                    body(w, False)

            gs_cnt, gs_base, po_cnt, po_base = S["aa"], S["f_dv"], S["done_xi"], S["done_a"]
            with dve.If(general):
                sub = Chain(dve, S["done_o"])
                r4 = rec[:, 0:16 * GE // P, :]
                V.memset(r4, 0.0)
                sub(V.memset(mask, 0.0))
                V.memset(r4[:, :, 0], float(NT * P))
                sub(V.memset(r4[:, :, 1], -1.0))
                dve.sem_inc(S["gs_init"], 1)
                dve.wait_ge(S["gs_rec"], 16 * (NG // 16))
                for n in range(8):
                    k, hh = n // 2, n % 2
                    dve.wait_ge(S["pp"], n + 1)
                    o = rec[:, hh * NC // 2:(hh + 1) * NC // 2, k].rearrange("p (g j) -> p g j", j=CPG)
                    V.tensor_copy(o, ps[6][:, :].rearrange("p (j g) -> p g j", j=CPG)).then_inc(S["gs_d"], 1)
                dve.wait_ge(S["gs_d"], 8)
                V.tensor_copy(wint, rec[:, :, 1])
                sub(V.tensor_copy(wint2, rec[:, :, 0]))
                V.tensor_scalar(wint, wint, 7, None, ALU.logical_shift_right)
                sub(V.tensor_scalar(wint2, wint2, 7, None, ALU.logical_shift_right))
                V.tensor_copy(win, wint)
                sub(V.tensor_copy(win2, wint2))
                sub(V.tensor_scalar(win2, win2, float(NT), None, ALU.is_equal))
                sub(V.tensor_tensor(win, win, win2, ALU.add))
                sub(V.memset(rank, 0.0))
                with dve.Fori(0, NTP) as w:
                    chain = Chain(dve, gs_cnt, w * 4)
                    chain(V.tensor_scalar(mask, win, iota_w[:, bass.ds(w, 1)], None, ALU.is_equal))
                    chain(V.tensor_tensor_scan(scan, mask, mask, 0.0, ALU.add, ALU.max))
                    V.tensor_copy(cnt[:, bass.ds(w, 1)], scan[:, NC - 1:NC])
                    chain(V.tensor_tensor(mask, scan, mask, ALU.mult))
                    chain(V.tensor_tensor(rank, rank, mask, ALU.add))
                dve.sem_inc(S["ax_f"], 1)
                dve.wait_ge(S["bx_f"], 1)
                sub(V.tensor_copy(aligi[:, :], ps[7][:, 0:NTP]))
                sub(V.tensor_scalar(aligi[:, :], aligi[:, :], ~(GE - 1), None, ALU.bitwise_and))
                sub(V.tensor_scalar(alig[:, :], aligi[:, :], float(GE), None, ALU.add))
                sub(V.tensor_tensor_scan(ends[:, :], alig[:, :], alig[:, :], 0.0, ALU.add, ALU.max))
                sub(V.tensor_tensor(starts[:, :], ends[:, :], alig[:, :], ALU.subtract))
                sub(V.scalar_tensor_tensor(basew[:, :], starts[:, :], -1.0, ps[6][:, 0:NTP], ALU.add, ALU.add))
                with dve.Fori(0, NTP) as w:
                    chain = Chain(dve, gs_base, w * 2)
                    chain(V.tensor_scalar(mask, win, iota_w[:, bass.ds(w, 1)], basew[:, bass.ds(w, 1)], ALU.is_equal, ALU.mult))
                    chain(V.tensor_tensor(rank, rank, mask, ALU.add))

                def hand(i, first):
                    if not first:
                        dve.wait_ge(S["gs_sc"], i * 16 * RING)
                    dve.sem_inc(S["gate_dve"], 1)
                    V.tensor_copy(rec_put[:, :, :], rec[:, bass.ds(i * RING, RING), :])
                    V.tensor_copy(stage[:, :, 0], rank[:, bass.ds(i * RING, RING)]).then_inc(S["done_rb0"], 1)
                    dve.wait_ge(S["done_rb0"], i + 1)
                    dve.sem_inc(S["gs_pos"], 1)
                loop(dve, NC // RING, hand)
                dve.wait_ge(S["gs_rl"], 32)
                rl = reload
                for k in range(4):
                    last = V.tensor_copy(by_half(raw[k]), rl[:, :, :, k])
                sub(last)
                V.tensor_reduce(dhigh[:, :], by_half(raw[1]), AX.X, ALU.max).then_inc(S["done_rb1"], 1)
                dve.wait_ge(S["done_rb1"], 1)
                sub(V.tensor_scalar(dhigh[:, :], dhigh[:, :], 0.0, None, ALU.max))
                sub(V.tensor_copy(dwini[:, :], dhigh[:, :]))
                sub(V.tensor_scalar(dwini[:, :], dwini[:, :], ~(P - 1), None, ALU.bitwise_and))
                sub(V.tensor_copy(dhigh[:, :], dwini[:, :]))
                for hh in range(2):
                    v = raw[1][:, hh * GE:(hh + 1) * GE]
                    last = V.tensor_scalar(v, v, dhigh[:, hh:hh + 1], None, ALU.max)
                sub(last)

            low_high()
            link(V.tensor_copy(dlowi[:, :], dlow[:, :]))
            V.tensor_scalar(dwini[:, :], dlowi[:, :], 7, None, ALU.logical_shift_right)
            link(V.tensor_scalar(doffi[:, :], dlowi[:, :], P - 1, None, ALU.bitwise_and))
            link(V.tensor_copy(doff[:, :], doffi[:, :]))
            for hh in range(2):
                c = slice(hh * GE, (hh + 1) * GE)
                V.tensor_scalar(raw_place[:, c], raw[1][:, c], dlow[:, hh:hh + 1], None, ALU.subtract)
                last = V.tensor_scalar(raw_place2[:, c], raw[1][:, c], dlow[:, hh:hh + 1], doff[:, hh:hh + 1], ALU.subtract, ALU.add)
            link(last)
            dve.sem_inc(S["lowrow"], 1)
            dve.sem_inc(S["cast"], 1)
            for n in range(8):
                k, hh = n // 2, n % 2
                dve.wait_ge(S["tr"], n + 1)
                to = (win2, iw_col[:, :], ow_col[:, :], place2[:, :])[k]
                o = to[:, hh * NC // 2:(hh + 1) * NC // 2].rearrange("p (g j) -> p g j", j=CPG)
                V.tensor_copy(o, ps[6 + n % 2][:, :].rearrange("p (j g) -> p g j", j=CPG)).then_inc(S["trv"], 1)
            dve.wait_ge(S["trv"], 8)
            link(V.tensor_copy(src_id[:, :], win2))
            V.tensor_scalar(wint, src_id[:, :], 7, None, ALU.logical_shift_right)
            link(V.tensor_scalar(wint2, src_id[:, :], P - 1, None, ALU.bitwise_and))
            V.tensor_copy(win, wint)
            link(V.tensor_copy(src_key[:, :], wint2))
            link(V.memset(rank, 0.0))
            with dve.Fori(0, NTP) as w:
                chain = Chain(dve, po_cnt, w * 4)
                chain(V.tensor_scalar(mask, win, iota_w[:, bass.ds(w, 1)], None, ALU.is_equal))
                chain(V.tensor_tensor_scan(scan, mask, mask, 0.0, ALU.add, ALU.max))
                V.tensor_copy(cnt[:, bass.ds(w, 1)], scan[:, NC - 1:NC])
                chain(V.tensor_tensor(mask, scan, mask, ALU.mult))
                chain(V.tensor_tensor(rank, rank, mask, ALU.add))
            starts_of(UR, S["e2"], S["e3"])
            with dve.Fori(0, NTP) as w:
                chain = Chain(dve, po_base, w * 2)
                chain(V.tensor_scalar(mask, win, iota_w[:, bass.ds(w, 1)], basew[:, bass.ds(w, 1)], ALU.is_equal, ALU.mult))
                chain(V.tensor_tensor(rank, rank, mask, ALU.add))
            link(V.tensor_copy(slot[:, :], rank))
            link(V.tensor_tensor(diag[:, :], ends[:, :], ident[:, 0:NTP], ALU.mult))
            link(V.tensor_reduce(endcol[:, :], diag[:, :], AX.X, ALU.add))
            link(V.tensor_scalar(mask[:, 0:NU], iota_u[:, :], endcol[:, :], None, ALU.is_ge))
            dve.sem_inc(S["e2"], 1)
            link(V.tensor_scalar(starts[0:1, :], ends[0:1, :], float(-UR), None, ALU.add))
            V.tensor_copy(fill_row[:, :], starts[0:1, :])
            V.tensor_scalar(unit_row[:, :], iota_u[0:1, :], starts[0:1, NT - 1:NT], None, ALU.min)
            dve.wait_ge(S["e3"], 2)
            link(V.tensor_copy(unit_win[:, :], ps[6][0:1, 0:NU]))
            dve.sem_inc(S["rows_ready"], 1)
            dve.wait_ge(S["placed"], 16)
            V.memset(node_a[:, :, :], 0.0)
            link(V.memset(node_c[:, :, :], 0.0))
            dve.sem_inc(S["pos_ready"], 1)
            dve.wait_ge(S["h_ready"], NT + 1)

            def spread(q, lo, hi):
                def body(i, first):
                    for s in range(RING):
                        g, h = RING * i + s, s % 2
                        dve.wait_ge(q["load"][h], (g // 2 + 1) * 32 if isinstance(g, int) else (2 * i + s // 2 + 1) * 32)
                        if not (first and s < 2):
                            dve.wait_ge(q["mm"], g - 1)
                        V.tensor_scalar(hot[:, h, :, :].rearrange("p a b -> p (a b)")[:, 0:GE], place_b[:, h, :], pcol[:, :], None, ALU.is_equal).then_inc(q["hot"], 1)
                        if not first:
                            dve.wait_ge(q["sent"][s], i * 16 * CPG)
                        dve.sem_inc(S["gate_dve"], 1)
                        V.tensor_copy(big[:, s, :, D], src_key[:, bass.ds(g * CPG, CPG)])
                        V.tensor_copy(stage[:, s, :], slot[:, bass.ds(g * CPG, CPG)]).then_inc(q["key"], 1)
                if lo:
                    with dve.Fori(lo // RING, hi // RING) as i:
                        body(i, False)
                else:
                    loop(dve, hi // RING, body)

            def wait_sent(q, groups):
                for k in range(RING):
                    dve.wait_ge(q["sent"][k], 16 * CPG * groups // RING)
                dve.sem_inc(S["gate_dve"], 1)

            spread(X[0], 0, NG_PLAIN)
            with dve.If(general):
                spread(X[0], NG_PLAIN, NG)
            wait_sent(X[0], NG_PLAIN)
            with dve.If(general):
                wait_sent(X[0], NG)

            def in_edges(lo, hi):
                def stage_group(g, s):
                    V.tensor_copy(stage[:, s, :], src_id[:, bass.ds(g * CPG, CPG)]).then_inc(S["g_stage"], 1)

                def body(i, first):
                    for s in range(RING):
                        g, h = RING * i + s, s % 2
                        if not first:
                            dve.wait_ge(S["g_mm"], g - RING + 1)
                        dve.sem_inc(S["gate_dve"], 1)
                        stage_group(g, s)
                    for s in range(RING):
                        g, h = RING * i + s, s % 2
                        if not (first and s < 2):
                            dve.wait_ge(S["g_mm"], g - 1)
                        for j in range(CPG):
                            last = V.tensor_scalar(hot[:, h, j, :], iota2[:, :], place2[:, bass.ds(g * CPG + j, 1)],
                                                   iw_col[:, bass.ds(g * CPG + j, 1)], ALU.is_equal, ALU.mult)
                        last.then_inc(S["g_hot"], 1)
                        w = V.value_load(win_tab[0:1, bass.ds(g, 1)], min_val=0, max_val=NT - 1)
                        dve.wait_ge(S["g_mm"], g + 1)
                        if not (first and s == 0):
                            dve.wait_ge(S["g_acc"], g)
                        o = node_a[:, bass.ds(w, 2), :].rearrange("p a d -> p (a d)")
                        V.tensor_tensor(o, o, ps[4 + h][:, :], ALU.add).then_inc(S["g_acc"], 1)
                if lo:
                    with dve.Fori(lo // RING, hi // RING) as i:
                        body(i, False)
                else:
                    loop(dve, hi // RING, body)

            in_edges(0, NG_PLAIN)
            with dve.If(general):
                in_edges(NG_PLAIN, NG)

            def gather_units(q):
                def body(i, first):
                    for s in range(RING):
                        u, h = RING * i + s, s % 2
                        dve.wait_ge(q["rb_load"][s], (i + 1) * 16)
                        if not (first and s < 2):
                            dve.wait_ge(q["rb_mm"], u - 1)
                        for j in range(2):
                            last = V.tensor_scalar(hot[:, h, j, 0:P], iota2[:, 0:P], unit[:, s, j, D:D + 1], None, ALU.is_equal)
                        last.then_inc(q["rb_hot"], 1)
                        w = V.value_load(unit_win[0:1, bass.ds(u, 1)], min_val=0, max_val=NT)
                        dve.wait_ge(q["rb_mm"], u + 1)
                        if not (first and s == 0):
                            dve.wait_ge(q["rb_acc"], u)
                        o = node_c[:, bass.ds(w, 1), :].rearrange("p a d -> p (a d)")
                        V.tensor_tensor(o, o, ps[4 + h][:, 0:D], ALU.add).then_inc(q["rb_acc"], 1)
                loop(dve, NU // RING, body)

            gather_units(X[0])
            dve.wait_ge(X[0]["rb_acc"], NU)
            dve.sem_inc(S["f_xl"], 1)

            K = 9

            def layer0_h(t, s, first):
                chain = Chain(dve, S["done_o"] if False else S["clear_c"], t * K)
                dve.wait_ge(S["xl0" if s == 0 else "xl1"], 16 * (t // 2 + 1) if isinstance(t, int) else None)

            def layer0(i, s, t, first, n=P):
                chain = Chain(dve, S["clear_c"], t * K)
                dve.wait_ge(S["xl0" if s == 0 else "xl1"], 16 * (i + 1))
                if not first:
                    dve.wait_ge(S["f_tr"], t - 1)
                h, x_ = hr[:, s, :], xr[:, s, :]
                normal(h, x_, chain).then_inc(S["f_h"], 1)
                dve.wait_ge(S["f_mm"], t + 1)
                if not first:
                    dve.wait_ge(S["f_act"], t - 1)
                V.tensor_tensor(ub[:, s, :], ps[4 + s][:, :], bx_b[:, :], ALU.add).then_inc(S["f_u"], 1)
                dve.wait_ge(S["f_act"], t + 1)
                dve.wait_ge(S["f_h"], t + 1)
                gate, new = gb[:, s, 0:D], gb[:, s, D:2 * D]
                y = node_a[:, bass.ds(t, 1), :].rearrange("p a d -> p (a d)")
                chain(V.tensor_tensor(y, h, new, ALU.subtract))
                chain(V.tensor_tensor(y, y, gate, ALU.mult))
                chain(V.tensor_tensor(y, y, new, ALU.add))
                chain(V.tensor_tensor(y, y, x_, ALU.add))
                dve.sem_inc(S["gate_dve"], 1)
                chain(V.bn_stats(bn6[:, :], y))
                dve.sem_inc(S["gate_dve"], 1)
                chain(V.bn_aggr(mv_t[:, :], bn6[:, :]))
                chain(V.tensor_scalar(mv[:, bass.ds(t, 1), :].rearrange("p a d -> p (a d)"), mv_t[:, :], 0.0, None, ALU.add))
                dve.sem_inc(S["f_y"], 1)
                assert chain.n == K

            def layer0s(i, first):
                for s in range(2):
                    layer0(i, s, 2 * i + s, first)
            loop(dve, FULL // 2, layer0s)
            layer0(FULL // 2, 0, FULL, False)
            dve.sem_inc(S["r1"], 1)
            dve.wait_ge(S["r1"], 2)
            link(V.reciprocal(rstd[:, :], rstd[:, :]))

            with dve.Fori(0, NT) as t:
                y = node_a[:, bass.ds(t, 1), :].rearrange("p a d -> p (a d)")
                V.tensor_scalar(y, y, mv[:, bass.ds(t, 1), 0], rstd[:, bass.ds(t, 1)], ALU.subtract, ALU.mult).then_inc(S["n2"], 1)
            dve.wait_ge(S["sum1"], 2)
            link(V.tensor_scalar(mean2_b[:, :], ps[6][:, 0:D], 1.0 / N, None, ALU.mult))
            centred(node_a, mean2_b[:, :], S["s2"], S["s2d"])
            dve.wait_ge(S["s2q"], NT)
            V.tensor_scalar(scale2_b[:, :], ps[7][:, 0:D], 1.0 / (N - 1), None, ALU.mult).then_inc(S["n1"], 1)
            dve.wait_ge(S["n1"], 2)
            link(V.tensor_scalar(scale2_b[:, :], scale2_b[:, :], 1e-4, None, ALU.add))
            link(V.reciprocal(scale2_b[:, :], scale2_b[:, :]))
            V.memset(node_c[:, :, :], 0.0).then_inc(S["done_l1"], 0) if False else link(V.memset(node_c[:, :, :], 0.0))

            def z_tile(i, s, t, first):
                if not first:
                    dve.wait_ge(S["zs0" if s == 0 else "zs1"], 16 * i)
                v = node_a[:, bass.ds(t, 1), :].rearrange("p a d -> p (a d)")
                V.tensor_tensor(hr[:, s, :], v, mean2_b[:, :], ALU.subtract).then_inc(S["z_s"], 1)
                dve.wait_ge(S["z_s"], t + 1)
                V.tensor_tensor(hr[:, s, :], hr[:, s, :], scale2_b[:, :], ALU.mult).then_inc(S["z_r"], 1)

            def z_tiles(i, first):
                for s in range(2):
                    z_tile(i, s, 2 * i + s, first)
            loop(dve, FULL // 2, z_tiles)
            z_tile(FULL // 2, 0, FULL, False)

            spread(X[1], 0, NG_PLAIN)
            with dve.If(general):
                spread(X[1], NG_PLAIN, NG)
            gather_units(X[1])
            dve.wait_ge(X[1]["rb_acc"], NU)
            dve.sem_inc(S["done_l1"], 1)

            K2 = 4

            def layer1(i, s, t, first):
                chain = Chain(dve, S["fin_y"], t * K2)
                dve.wait_ge(S["l_mm"], t + 1)
                y = node_c[:, bass.ds(t, 1), :].rearrange("p a d -> p (a d)")
                v = node_a[:, bass.ds(t, 1), :].rearrange("p a d -> p (a d)")
                V.tensor_tensor(y, ps[2 + s][:, 0:D], b1_b[:, :], ALU.add).then_inc(S["l_y"], 1)
                dve.wait_ge(S["l_y"], t + 1)
                chain(V.tensor_tensor(y, y, v, ALU.add))
                dve.sem_inc(S["gate_dve"], 1)
                chain(V.bn_stats(bn6[:, :], y))
                dve.sem_inc(S["gate_dve"], 1)
                chain(V.bn_aggr(mv_t[:, :], bn6[:, :]))
                chain(V.tensor_scalar(mv[:, bass.ds(t, 1), :].rearrange("p a d -> p (a d)"), mv_t[:, :], 0.0, None, ALU.add))
                assert chain.n == K2

            def layer1s(i, first):
                for s in range(2):
                    layer1(i, s, 2 * i + s, first)
            loop(dve, FULL // 2, layer1s)
            layer1(FULL // 2, 0, FULL, False)
            dve.sem_inc(S["r2"], 1)
            dve.wait_ge(S["r2"], 2)
            link(V.reciprocal(rstd[:, :], rstd[:, :]))

            def o_tile(i, s, t, first):
                if not first:
                    dve.wait_ge(S["o_s0" if s == 0 else "o_s1"], 16 * i)
                V.tensor_scalar(gb[:, s, 0:D], node_c[:, bass.ds(t, 1), :].rearrange("p a d -> p (a d)"),
                                mv[:, bass.ds(t, 1), 0], rstd[:, bass.ds(t, 1)], ALU.subtract, ALU.mult).then_inc(S["o_r"], 1)

            def o_tiles(i, first):
                for s in range(2):
                    o_tile(i, s, 2 * i + s, first)
            loop(dve, FULL // 2, o_tiles)
            o_tile(FULL // 2, 0, FULL, False)


_INS = ["x", "src", "dst", "edge_weight", "edge_weight_n2", "L0_gnn_gamma", "L0_gnn_beta", "L0_gnn_W_in",
        "L0_gnn_b_in", "L0_gnn_W_out", "L0_gnn_b_out", "L0_gnn_W_x2i", "L0_gnn_b_x2i", "L0_gnn_W_h2h",
        "L1_gnn_weight", "L1_gnn_bias"]


def kernel(**inputs):
    import numpy as _np
    import concourse.bacc as _bacc
    from concourse import mybir as _mybir
    from concourse.bass_utils import run_bass_kernel_spmd as _run

    nc = _bacc.Bacc("TRN2", target_bir_lowering=False, num_devices=1)
    arrays, args = {}, []
    for name in _INS:
        a = _np.ascontiguousarray(inputs[name])
        arrays[f"in_{name}"] = a
        args.append(nc.dram_tensor(f"in_{name}", a.shape, _mybir.dt.from_np(a.dtype), kind="ExternalInput").ap())
    args.append(nc.dram_tensor("out_0", (N, D), _mybir.dt.float32, kind="ExternalOutput").ap())
    gnn_program(nc, *args)
    r = _run(nc, [arrays], core_ids=[0])
    return r.results[0]["out_0"]
```

```python
import numpy as np
import concourse.bass as bass
import concourse.mybir as mybir
from contextlib import ExitStack

P = 128
N, D, E = 6250, 256, 106250
NT = -(-N // P)
NTP = NT + 1
FULL = N // P
TAIL = N - FULL * P
CPG = 4
GE = CPG * P
NG = -(-(E // GE + NT) // 8) * 8
NG_PLAIN = -(-(-(-E // GE)) // 8) * 8
NC = NG * CPG
UR = 256
NU = E // UR + NT
RW = 3
MW = 260
MROWS = NU * UR + NG * GE - E
RING = 4
EPS = 1e-5

F32 = mybir.dt.float32
I32 = mybir.dt.int32
ALU = mybir.AluOpType
ACT = mybir.ActivationFunctionType
AX = mybir.AxisListType


class Chain:

    def __init__(self, engine, semaphore, base=0):
        self.engine, self.semaphore, self.base, self.n = engine, semaphore, base, 0

    def __call__(self, instruction):
        instruction.then_inc(self.semaphore, 1)
        self.n += 1
        self.engine.wait_ge(self.semaphore, self.base + self.n)


def need(engine, semaphore, value):
    if not isinstance(value, int) or value > 0:
        engine.wait_ge(semaphore, value)


def is_tile(t):
    return not isinstance(t, int) or 0 <= t < NT


def over_tiles(engine, step, after=3):
    for s in range(2):
        step(s, s)
    with engine.Fori(1, FULL // 2) as i:
        for s in range(2):
            step(2 * i + s, s)
    for t in range(FULL, FULL + 1 + after):
        step(t, t % 2)


def turns(engine, lo, hi, body):
    body(lo)
    if hi - lo > 2:
        with engine.Fori(lo + 1, hi - 1) as i:
            body(i)
    if hi - lo > 1:
        body(hi - 1)


def gnn_program(nc, x, src, dst, edge_weight, edge_weight_n2, gamma, beta, w_in, b_in, w_out, b_out,
                w_x2i, b_x2i, w_h2h, w_l1, b_l1, out):
    ctx = ExitStack()
    with ctx:
        def sb(name, shape, dt=F32):
            return ctx.enter_context(nc.sbuf_tensor(name, shape, dt))

        def dram(name, shape, dt=F32):
            return nc.dram_tensor(name, shape, dt, kind="Internal").ap()

        class Semaphores(dict):
            def __missing__(self, name):
                self[name] = ctx.enter_context(nc.semaphore(name))
                return self[name]

        S = Semaphores()

        in_table = dram("in_table", [NTP * P, D])
        out_table = dram("out_table", [NTP * P, D])
        z_table = dram("z_table", [NTP * P, D])
        place_row = dram("place_row", [NG * GE])
        group_row = dram("group_row", [2, NG], I32)
        records = dram("records", [NG * GE, 4])
        messages = dram("messages", [MROWS, MW])
        gate_rows = dram("gate_rows", [NT * P, 3 * D])

        node_a = sb("node_a", [P, NTP, D])
        node_c = sb("node_c", [P, NTP, D])
        work = sb("work", [P, 6 * NC + 4 * 1024])

        def area(at, shape, dt=F32):
            n = 1
            for d in shape:
                n *= d
            v = work[:, at:at + n]
            if len(shape) == 2:
                v = v.rearrange("p (a b) -> p a b", b=shape[1])
            elif len(shape) == 3:
                v = v.rearrange("p (a b c) -> p a b c", b=shape[1], c=shape[2])
            return v if dt == F32 else v.bitcast(dt)

        flat_c = node_c[:, :, :].rearrange("p t d -> p (t d)")

        def part_c(k, n=1):
            return flat_c[:, k * NC:(k + n) * NC]

        raw_si, raw_di = area(0, [NC], I32), area(NC, [NC], I32)
        raw_place, raw_place2 = area(0, [NC]), area(NC, [NC])
        raw = [area((2 + k) * NC, [NC]) for k in range(4)]
        win, mask, scan, rank, half_win, half_unit, upper_half, win_b = (part_c(k) for k in range(8))
        mask_i, scan_i = mask.bitcast(I32), scan.bitcast(I32)
        rec = part_c(8, 4).rearrange("p (c k) -> p c k", k=4)
        reload = part_c(8, 4).rearrange("p (h q k) -> p h q k", h=2, k=4)
        rec_put = sb("rec_put", [P, RING, 4])

        columns = sb("columns", [P, 7 * NC])
        src_id = columns[:, 0:NC].bitcast(I32)
        place2 = columns[:, NC:2 * NC]
        ow_col = columns[:, 2 * NC:3 * NC]
        slot = columns[:, 3 * NC:4 * NC].bitcast(I32)
        carried = columns[:, 4 * NC:7 * NC].rearrange("p (c k) -> p c k", k=RW)
        back = columns[:, 0:2 * NU * RW].rearrange("p (c k) -> p c k", k=RW)
        back_id = columns[:, 3 * NC:3 * NC + 2 * NU].bitcast(I32)

        wio = sb("wio", [P, 2, 2 * D])
        wx = sb("wx", [P, 4, 2 * D])
        wh = sb("wh", [P, 2, 2 * D])
        w1 = sb("w1", [P, 2, D])
        gamma_b, beta_b, b1_b = sb("gamma_b", [P, D]), sb("beta_b", [P, D]), sb("b1_b", [P, D])
        bio_b, bx_b = sb("bio_b", [P, 2 * D]), sb("bx_b", [P, 2 * D])
        mean_b, scale_b = sb("mean_b", [P, D]), sb("scale_b", [P, D])
        eps_c = sb("eps_c", [P, 1])

        ident, ones, upper = sb("ident", [P, P]), sb("ones", [P, P]), sb("upper", [P, P])
        iota2 = sb("iota2", [P, 2 * P])
        iota_w = sb("iota_w", [P, NTP])
        iota_u = flat_c[:, 12 * NC:12 * NC + NU]
        pcol = sb("pcol", [P, 1])
        cnt, ends, starts = sb("cnt", [P, NTP]), sb("ends", [P, NTP]), sb("starts", [P, NTP])
        alig, aligi = sb("alig", [P, NTP]), sb("aligi", [P, NTP], I32)
        basew, diag = sb("basew", [P, NTP]), sb("diag", [P, NTP])
        endcol = sb("endcol", [P, 1])
        dlow, dhigh = sb("dlow", [P, 2]), sb("dhigh", [P, 2])
        dlowi, dwini, doffi = sb("dlowi", [P, 2], I32), sb("dwini", [P, 2], I32), sb("doffi", [P, 2], I32)
        doff, wide, widest = sb("doff", [P, 2]), sb("wide", [P, 2]), sb("widest", [P, 1])
        flag = sb("flag", [1, 1], I32)
        low_tab, win_tab = sb("low_tab", [1, NG], I32), sb("win_tab", [1, NG], I32)
        by_unit = sb("by_unit", [33, NU], I32)
        unit_win, unit_row = by_unit[0:1, :], by_unit[32:33, :]
        fill_row = sb("fill_row", [1, NTP], I32)
        zeros = sb("zeros", [P, UR // P, MW])
        stage = sb("stage", [P, RING, CPG], I32)
        bn6, mv = sb("bn6", [P, 6]), sb("mv", [P, NT, 2])
        rstd, mv_t = sb("rstd", [P, NT]), sb("mv_t", [P, 2])

        big = area(0, [RING, CPG, MW])
        hot_at = RING * CPG * MW
        hot = area(hot_at, [2, CPG, 2 * P])
        tab = area(hot_at + 2048, [2, D])
        place_b = area(hot_at + 2560, [2, GE])
        extra = hot_at + 3584
        unit = area(extra, [RING, 2, MW])
        cx, cg, cs, ct = (area(extra + a, [n]) for a, n in ((0, D), (D, 3 * D), (4 * D, D), (5 * D, 2 * D)))
        gates_in = area(0, [2, 4 * D])
        ub, gb = area(2048, [2, 2 * D]), area(3072, [2, 2 * D])
        st, tT = area(hot_at, [2, D]), area(hot_at + 512, [2, D])
        xn = area(hot_at + 1024, [2, D])
        hr, sq = area(6 * NC, [2, D]), area(6 * NC + 512, [2, D])
        tabs, hT = area(6 * NC + 1024, [2, 2 * D]), area(6 * NC + 2048, [2, D])

        ps = [ctx.enter_context(nc.psum_tensor(f"ps{i}", [P, 2 * D], F32)) for i in range(8)]

        def hot_flat(h):
            return hot[:, h, :, :].rearrange("p a b -> p (a b)")

        def tile_of(table, t):
            return table[:, bass.ds(t, 1), :].rearrange("p o d -> p (o d)")

        def row_view(v):
            return v.rearrange("(o n) -> o n", o=1)

        IN_TURNS = (0, NG_PLAIN // RING), (NG_PLAIN // RING, NG // RING)
        PACKED = NTP // 2
        BACK_TURNS = NU // (2 * RING)
        LOADS_W = 11 * 16

        block = ctx.enter_context(nc.Block())

        @block.sync
        def _(sp):
            sp.dma_start(node_a[:, 0:FULL, :], x[0:FULL * P, :].rearrange("(t p) d -> p t d", p=P)).then_inc(S["x_loaded"], 16)
            sp.wait_ge(S["pads_set"], 1)
            sp.dma_start(node_a[0:TAIL, FULL, :], x[FULL * P:N, :]).then_inc(S["x_loaded"], 16)
            full2 = (E - P * GE) // GE
            rest = E - (P + full2) * GE
            for a, to in ((src, raw_si), (dst, raw_di), (edge_weight, raw[2]), (edge_weight_n2, raw[3])):
                v = to.rearrange("p (h q) -> p h q", h=2)
                for s, d in ((a[0:P * GE].rearrange("(g q) -> g q", q=GE), v[:, 0, :]),
                             (a[P * GE:(P + full2) * GE].rearrange("(g q) -> g q", q=GE), v[0:full2, 1, :]),
                             (a[(P + full2) * GE:E].rearrange("(g q) -> g q", g=1), v[full2:full2 + 1, 1, 0:rest])):
                    sp.dma_start(d, s).then_inc(S["edges_loaded"], 16)
            sp.wait_ge(S["constants"], 5)
            for tb in (in_table, out_table, z_table):
                sp.dma_start(tb[NT * P:NTP * P, :], zeros[:, 0, 0:D]).then_inc(S["spare_rows"], 16)

            def store_tables(t, s):
                if not is_tile(t):
                    return
                sp.wait_ge(S["tables_made"], t + 1)
                for k, tb in enumerate((in_table, out_table)):
                    sp.dma_start(tb[bass.ds(t * P, P), :], tabs[:, s, k * D:(k + 1) * D]).then_inc(S[f"tables_stored{s}"], 16)
            over_tiles(sp, store_tables, 0)

            sp.wait_ge(S["flagged"], 1)
            general = nc.sync.value_load(flag[0:1, 0:1], min_val=0, max_val=1)
            with sp.If(general):
                sp.wait_ge(S["re_empty"], 1)
                for g in range(NG // 16):
                    sp.dma_start(records[g * 16 * GE:(g + 1) * 16 * GE, :].rearrange("(p q) k -> p (q k)", p=P),
                                 rec[:, 0:16 * GE // P, :].rearrange("p q k -> p (q k)")).then_inc(S["re_cleared"], 16)
                sp.wait_ge(S["re_put"], 16 * NC)
                rv = records.rearrange("(h g q) k -> h g (q k)", h=2, q=GE)
                for hh in range(2):
                    sp.dma_start(reload[:, hh, :, :].rearrange("p q k -> p (q k)"), rv[hh]).then_inc(S["re_loaded"], 16)

            sp.wait_ge(S["lows"], 1)
            for k, v in ((0, dlowi), (1, dwini)):
                sp.dma_start(group_row[k, :].rearrange("(h g) -> g h", h=2), v[:, :],
                             allow_slow_non_contiguous=True).then_inc(S["low_tabs"], 16)
            sp.dma_start(place_row.rearrange("(h g q) -> g h q", h=2, q=GE),
                         raw_place.rearrange("p (h q) -> p h q", h=2)).then_inc(S["places_stored"], 16)
            sp.wait_ge(S["low_tabs"], 32)
            sp.dma_start(low_tab[:, :], group_row[0:1, :]).then_inc(S["low_tabs"], 16)
            sp.dma_start(win_tab[:, :], group_row[1:2, :]).then_inc(S["low_tabs"], 16)
            sp.wait_ge(S["tables_stored0"], 32 * (FULL // 2 + 1))
            sp.wait_ge(S["tables_stored1"], 32 * (FULL // 2))
            sp.wait_ge(S["spare_rows"], 48)
            sp.wait_ge(S["places_stored"], 16)
            sp.wait_ge(S["low_tabs"], 64)
            sp.sem_inc(S["tables_ready"], 1)

            sp.wait_ge(S["rows_ready"], 1)
            for w in range(NT):
                r = nc.sync.value_load(fill_row[0:1, w:w + 1], min_val=0, max_val=NU * UR - UR)
                sp.dma_start(messages[bass.ds(r, UR), :].rearrange("(p j) c -> p j c", p=P), zeros[:, :, :]).then_inc(S["zero_rows"], 16)

            sp.wait_ge(S["in_done"], 1)
            sp.dma_start(cx, x[0:P, :]).then_inc(S["cx_loaded"], 16)

            def out_turn(i):
                for s in range(RING):
                    g = RING * i + s
                    need(sp, S["out_mm"], g - 1)
                    r = nc.sync.value_load(low_tab[0:1, bass.ds(g, 1)], min_val=0, max_val=N - 1)
                    sp.dma_start(tab[:, s % 2, :], out_table[bass.ds(r, P), :]).then_inc(S[f"out_load{s % 2}"], 16)
                    sp.dma_start(place_b[:, s % 2, :], row_view(place_row[bass.ds(g * GE, GE)]).broadcast_to([P, GE])).then_inc(S[f"out_load{s % 2}"], 16)
                    if s == 2 and is_tile(i):
                        sp.wait_ge(S["c_h"], i + 1)
                        if isinstance(i, int) and i + 1 == FULL:
                            sp.dma_start(cx[0:TAIL, :], x[FULL * P:N, :]).then_inc(S["cx_loaded"], 16)
                        elif is_tile(i + 1):
                            sp.dma_start(cx, x[bass.ds((i + 1) * P, P), :]).then_inc(S["cx_loaded"], 16)
                    if s == 3 and is_tile(i):
                        sp.wait_ge(S["c_sum"], i + 1)
                        sp.dma_start(gate_rows[bass.ds(i * P, P), :], cg).then_inc(S["c_stored"], 16)

            out_turn(0)
            with sp.Fori(1, FULL - 1) as i:
                out_turn(i)
            for i in range(FULL - 1, NG_PLAIN // RING):
                out_turn(i)
            with sp.If(general):
                with sp.Fori(*IN_TURNS[1]) as i:
                    for s in range(RING):
                        g = RING * i + s
                        sp.wait_ge(S["out_mm"], g - 1)
                        r = nc.sync.value_load(low_tab[0:1, bass.ds(g, 1)], min_val=0, max_val=N - 1)
                        sp.dma_start(tab[:, s % 2, :], out_table[bass.ds(r, P), :]).then_inc(S[f"out_load{s % 2}"], 16)
                        sp.dma_start(place_b[:, s % 2, :], row_view(place_row[bass.ds(g * GE, GE)]).broadcast_to([P, GE])).then_inc(S[f"out_load{s % 2}"], 16)
            for k in range(RING):
                sp.wait_ge(S[f"sent{k}"], 16 * CPG * NG_PLAIN // RING)
            with sp.If(general):
                for k in range(RING):
                    sp.wait_ge(S[f"sent{k}"], 16 * CPG * NG // RING)

            def back_turn(i):
                for s in range(RING):
                    u = RING * i + s
                    need(sp, S["back_mm"], u - RING + 1)
                    need(sp, S["back_kept"], u - RING + 1)
                    r = nc.sync.value_load(unit_row[0:1, bass.ds(u, 1)], min_val=0, max_val=NU * UR - UR)
                    sp.dma_start(unit[:, s, :, :], messages[bass.ds(r, UR), :].rearrange("(p j) c -> p j c", p=P)).then_inc(S[f"back_load{s}"], 16)
            back_turn(0)
            with sp.Fori(1, NU // RING) as i:
                back_turn(i)

            def gates_load(t, s):
                if not is_tile(t):
                    return
                need(sp, S["y_made"], t - 1)
                need(sp, S["xn_made"], t - 1)
                sp.dma_start(gates_in[:, s, 0:3 * D], gate_rows[bass.ds(t * P, P), :]).then_inc(S[f"gates_load{s}"], 16)
                if isinstance(t, int) and t == FULL:
                    sp.dma_start(gates_in[0:TAIL, s, 3 * D:4 * D], x[FULL * P:N, :]).then_inc(S[f"gates_load{s}"], 16)
                else:
                    sp.dma_start(gates_in[:, s, 3 * D:4 * D], x[bass.ds(t * P, P), :]).then_inc(S[f"gates_load{s}"], 16)
            sp.wait_ge(S["c_stored"], 16 * NT)
            over_tiles(sp, gates_load, 0)

            for k in range(7):
                sp.wait_ge(S["z_made"], 7 * (k + 1))
                sp.dma_start(z_table[7 * k * P:7 * (k + 1) * P, :].rearrange("(t p) d -> p t d", p=P),
                             node_c[:, 7 * k:7 * (k + 1), :]).then_inc(S["z_stored"], 16)
            sp.wait_ge(S["z_stored"], 16 * 7)
            sp.sem_inc(S["z_ready"], 1)

            def result_store(t, s):
                if not is_tile(t):
                    return
                sp.wait_ge(S["result"], t + 1)
                if isinstance(t, int) and t == FULL:
                    sp.dma_start(out[FULL * P:N, :], gb[0:TAIL, s, 0:D]).then_inc(S[f"result_stored{s}"], 16)
                else:
                    sp.dma_start(out[bass.ds(t * P, P), :], gb[:, s, 0:D]).then_inc(S[f"result_stored{s}"], 16)
            over_tiles(sp, result_store, 0)
            sp.wait_ge(S["result_stored0"], 16 * (FULL // 2 + 1))
            sp.wait_ge(S["result_stored1"], 16 * (FULL // 2))
            sp.wait_ge(S["zero_rows"], 16 * NT)

        @block.gpsimd
        def _(pool):
            link = Chain(pool, S["constants"])
            nc.gpsimd.memset(ones[:, :], 1.0)
            link(nc.gpsimd.memset(ident[:, :], 0.0))
            link(nc.gpsimd.affine_select(out=ident[:, :], in_=ident[:, :], compare_op=ALU.not_equal, fill=1.0,
                                         base=0, pattern=[[-1, P]], channel_multiplier=1))
            link(nc.gpsimd.affine_select(out=upper[:, :], in_=ones[:, :], compare_op=ALU.is_gt, fill=0.0,
                                         base=0, pattern=[[1, P]], channel_multiplier=-1))
            nc.gpsimd.memset(zeros[:, :, :], 0.0)
            nc.gpsimd.memset(eps_c[:, :], EPS)
            nc.gpsimd.iota(iota2[:, :], [[1, 2 * P]], base=0, channel_multiplier=0, allow_small_or_imprecise_dtypes=True)
            nc.gpsimd.iota(iota_u, [[UR, NU]], base=0, channel_multiplier=0, allow_small_or_imprecise_dtypes=True)
            nc.gpsimd.iota(pcol[:, :], [[0, 1]], base=0, channel_multiplier=1, allow_small_or_imprecise_dtypes=True)
            nc.gpsimd.iota(iota_w[:, :], [[1, NTP]], base=0, channel_multiplier=0,
                           allow_small_or_imprecise_dtypes=True).then_inc(S["constants"], 2)

            pool.wait_ge(S["flagged"], 1)
            general = nc.gpsimd.value_load(flag[0:1, 0:1], min_val=0, max_val=1)
            with pool.If(general):
                pool.wait_ge(S["re_cleared"], 16 * (NG // 16))
                with pool.Fori(0, NC // RING) as i:
                    pool.wait_ge(S["re_staged"], i + 1)
                    pool.sem_inc(S["pool_may"], 1)
                    for j in range(RING):
                        nc.gpsimd.indirect_dma_start(
                            out=records, out_offset=bass.IndirectOffsetOnAxis(ap=stage[:, j, 0:1], axis=0),
                            in_=rec_put[:, j, :], in_offset=None, bounds_check=NG * GE - 1, oob_is_err=False).then_inc(S["re_put"], 16)

            def gather(table, tag, lo, hi):
                with pool.Fori(lo, hi) as i:
                    for s in range(RING):
                        pool.wait_ge(S[f"{tag}_staged"], RING * i + s + 1)
                        pool.sem_inc(S["pool_may"], 1)
                        for j in range(CPG):
                            nc.gpsimd.indirect_dma_start(
                                out=big[:, s, j, 0:D], out_offset=None, in_=table,
                                in_offset=bass.IndirectOffsetOnAxis(ap=stage[:, s, j:j + 1], axis=0)).then_inc(S[f"{tag}_rows{s}"], 16)

            pool.wait_ge(S["tables_ready"], 1)
            pool.sem_inc(S["pool_may"], 1)
            gather(in_table, "in", *IN_TURNS[0])
            with pool.If(general):
                gather(in_table, "in", *IN_TURNS[1])

            def scatter(lo, hi):
                with pool.Fori(lo, hi) as i:
                    for s in range(RING):
                        g = RING * i + s
                        pool.wait_ge(S["out_msg"], g + 1)
                        pool.wait_ge(S["out_carried"], g + 1)
                        pool.sem_inc(S["pool_may"], 1)
                        for j in range(CPG):
                            nc.gpsimd.indirect_dma_start(
                                out=messages, out_offset=bass.IndirectOffsetOnAxis(ap=stage[:, s, j:j + 1], axis=0),
                                in_=big[:, s, j, :], in_offset=None).then_inc(S[f"sent{s}"], 16)
            pool.wait_ge(S["zero_rows"], 16 * NT)
            pool.sem_inc(S["pool_may"], 1)
            scatter(*IN_TURNS[0])
            with pool.If(general):
                scatter(*IN_TURNS[1])

            def x_and_new(t, s):
                if not is_tile(t):
                    return
                pool.wait_ge(S["gates_made"], t + 1)
                need(pool, S["y_made"], t - 1)
                pool.sem_inc(S["pool_may"], 1)
                nc.gpsimd.tensor_tensor(xn[:, s, :], gb[:, s, D:2 * D], gates_in[:, s, 3 * D:4 * D], ALU.add).then_inc(S["xn_made"], 1)
            over_tiles(pool, x_and_new, 0)

            pool.wait_ge(S["z_ready"], 1)
            pool.sem_inc(S["pool_may"], 1)
            gather(z_table, "second", 0, BACK_TURNS)

        @block.scalar
        def _(act):
            for d, s in ((wio[:, :, 0:D], w_in.rearrange("(k p) n -> p k n", p=P)),
                         (wio[:, :, D:2 * D], w_out.rearrange("(k p) n -> p k n", p=P)),
                         (wx[:, :, :], w_x2i.rearrange("(k p) n -> p k n", p=P)),
                         (wh[:, :, :], w_h2h.rearrange("(k p) n -> p k n", p=P)),
                         (w1[:, :, :], w_l1.rearrange("(k p) n -> p k n", p=P)),
                         (gamma_b[:, :], row_view(gamma).broadcast_to([P, D])),
                         (beta_b[:, :], row_view(beta).broadcast_to([P, D])),
                         (bio_b[:, 0:D], row_view(b_in).broadcast_to([P, D])),
                         (bio_b[:, D:2 * D], row_view(b_out).broadcast_to([P, D])),
                         (bx_b[:, :], row_view(b_x2i).broadcast_to([P, 2 * D])),
                         (b1_b[:, :], row_view(b_l1).broadcast_to([P, D]))):
                act.dma_start(d, s).then_inc(S["weights"], 16)

            def squares(table, made, used, signal):
                def step(t, s):
                    if not is_tile(t):
                        return
                    act.wait_ge(made, t + 1)
                    need(act, used, t - 1)
                    act.sem_inc(S["act_may"], 1)
                    nc.scalar.activation(sq[:, s, :], tile_of(table, t), ACT.Square).then_inc(signal, 1)
                over_tiles(act, step, 0)

            squares(node_a, S["x_centred"], S["x_sq_used"], S["x_sq"])
            act.wait_ge(S["x_var"], 1)
            nc.scalar.activation(scale_b[:, :], scale_b[:, :], ACT.Sqrt, bias=eps_c[:, :]).then_inc(S["x_var"], 1)

            def h_out(t, s):
                if not is_tile(t):
                    return
                act.wait_ge(S["h_turned"], t + 1)
                need(act, S["tables_mm"], t - 1)
                nc.scalar.activation(hT[:, s, :], ps[s][:, 0:D], ACT.Copy).then_inc(S["h_out"], 1)
            over_tiles(act, h_out, 0)

            act.wait_ge(S["flagged"], 1)
            general = nc.scalar.value_load(flag[0:1, 0:1], min_val=0, max_val=1)

            def out_turn(i, tiles):
                if tiles and is_tile(i):
                    need(act, S["c_turned"], i)
                    act.sem_inc(S["act_may"], 1)
                    nc.scalar.activation(cs, tile_of(node_a, i), ACT.Copy).then_inc(S["c_sums"], 1)
                for s in range(RING):
                    g = RING * i + s
                    act.wait_ge(S["out_mm"], g + 1)
                    need(act, S[f"sent{s}"], i * 16 * CPG)
                    act.sem_inc(S["act_may"], 1)
                    for j in range(CPG):
                        b = ps[2 * (s % 2) + j // 2]
                        last = nc.scalar.activation(big[:, s, j, 0:D], b[:, (j % 2) * D:(j % 2 + 1) * D], ACT.Copy,
                                                    scale=ow_col[:, bass.ds(g * CPG + j, 1)])
                    last.then_inc(S["out_msg"], 1)
                    if s == 0 and tiles and is_tile(i):
                        act.wait_ge(S["c_turned"], i + 1)
                        need(act, S["c_mm"], i)
                        nc.scalar.activation(ct, ps[6][:, :], ACT.Copy).then_inc(S["c_out"], 1)

            act.wait_ge(S["in_done"], 1)
            out_turn(0, True)
            with act.Fori(1, NT) as i:
                out_turn(i, True)
            for i in range(NT, NG_PLAIN // RING):
                out_turn(i, False)
            with act.If(general):
                with act.Fori(*IN_TURNS[1]) as i:
                    out_turn(i, False)

            def keep(i):
                for s in range(RING):
                    u = RING * i + s
                    act.wait_ge(S[f"back_load{s}"], (i + 1) * 16)
                    act.sem_inc(S["act_may"], 1)
                    nc.scalar.activation(back[:, bass.ds(2 * u, 2), :], unit[:, s, :, D:D + RW], ACT.Copy).then_inc(S["back_kept"], 1)
            with act.Fori(0, NU // RING) as i:
                keep(i)
            act.wait_ge(S["back_kept"], NU)
            nc.scalar.activation(back_id, back[:, :, 1], ACT.Copy).then_inc(S["back_ids"], 1)

            act.wait_ge(S["out_done"], 1)

            def sums_step(t, s):
                if is_tile(t):
                    need(act, S["e_turned"], t - 1)
                    act.sem_inc(S["act_may"], 1)
                    nc.scalar.activation(st[:, s, :], tile_of(node_c, t), ACT.Copy).then_inc(S["e_sums"], 1)

            def gates_step(t, s):
                if isinstance(t, int) and t == 0:
                    sums_step(0, 0)
                sums_step(t + 1, 1 - s)
                if is_tile(t):
                    act.wait_ge(S["e_turned"], t + 1)
                    need(act, S["e_mm"], t - 1)
                    nc.scalar.activation(tT[:, s, :], ps[s][:, 0:D], ACT.Copy).then_inc(S["e_out"], 1)
                if is_tile(t - 1):
                    r = 1 - s
                    act.wait_ge(S["gate_sums"], t)
                    need(act, S["y_made"], t - 2)
                    need(act, S["xn_made"], t - 2)
                    nc.scalar.activation(gb[:, r, 0:D], ub[:, r, 0:D], ACT.Sigmoid)
                    nc.scalar.activation(gb[:, r, D:2 * D], ub[:, r, D:2 * D], ACT.Tanh).then_inc(S["gates_made"], 1)
            over_tiles(act, gates_step, 1)

            act.wait_ge(S["y_stats"], 1)
            nc.scalar.activation(rstd[:, :], mv[:, :, 1], ACT.Sqrt, bias=eps_c[:, :]).then_inc(S["y_stats"], 1)
            squares(node_c, S["d_made"], S["d_sq_used"], S["d_sq"])
            act.wait_ge(S["d_var"], 1)
            nc.scalar.activation(scale_b[:, :], scale_b[:, :], ACT.Sqrt).then_inc(S["d_var"], 1)

            act.wait_ge(S["second_done"], 1)

            def second_sums(t, s):
                if is_tile(t):
                    need(act, S["l_turned"], t - 1)
                    act.sem_inc(S["act_may"], 1)
                    nc.scalar.activation(st[:, s, :], tile_of(node_c, t), ACT.Copy).then_inc(S["l_sums"], 1)

            def second_step(t, s):
                if isinstance(t, int) and t == 0:
                    second_sums(0, 0)
                second_sums(t + 1, 1 - s)
                if is_tile(t):
                    act.wait_ge(S["l_turned"], t + 1)
                    need(act, S["l_mm"], t - 1)
                    nc.scalar.activation(tT[:, s, :], ps[s][:, 0:D], ACT.Copy).then_inc(S["l_out"], 1)
            over_tiles(act, second_step, 0)
            act.wait_ge(S["l_stats"], 1)
            nc.scalar.activation(rstd[:, :], mv[:, :, 1], ACT.Sqrt, bias=eps_c[:, :]).then_inc(S["l_stats"], 1)

        @block.tensor
        def _(pe):
            pe.wait_ge(S["constants"], 5)

            def node_sum(to, table, ready, signal):
                if ready is not None:
                    pe.wait_ge(ready, 1)
                nc.tensor.matmul(to, ones[:, :], table[:, 0, :], start=True, stop=False)
                with pe.Fori(1, FULL) as t:
                    if ready is not None:
                        pe.wait_ge(ready, t + 1)
                    nc.tensor.matmul(to, ones[:, :], table[:, bass.ds(t, 1), :], start=False, stop=False)
                if ready is not None:
                    pe.wait_ge(ready, NT)
                nc.tensor.matmul(to, ones[0:TAIL, :], table[0:TAIL, FULL, :], start=False, stop=True).then_inc(signal, 1)

            def square_sum(to, made, used):
                def step(t, s):
                    if not is_tile(t):
                        return
                    pe.wait_ge(made, t + 1)
                    last = isinstance(t, int) and t == FULL
                    n = TAIL if last else P
                    nc.tensor.matmul(to, ones[0:n, :], sq[0:n, s, :], start=isinstance(t, int) and t == 0, stop=last).then_inc(used, 1)
                over_tiles(pe, step, 0)

            pe.wait_ge(S["x_loaded"], 32)
            node_sum(ps[4][:, 0:D], node_a, None, S["x_sum"])
            pe.wait_ge(S["widest"], 1)
            nc.tensor.matmul(ps[6][:, 0:1], ones[:, :], widest[:, :], start=True, stop=True).then_inc(S["widest"], 1)
            square_sum(ps[5][:, 0:D], S["x_sq"], S["x_sq_used"])

            pe.wait_ge(S["weights"], LOADS_W)

            def table_step(t, s):
                if is_tile(t):
                    pe.wait_ge(S["h_made"], t + 1)
                    need(pe, S["h_out"], t - 1)
                    for k in range(2):
                        last = nc.tensor.transpose(ps[s][:, k * P:(k + 1) * P], hr[:, s, k * P:(k + 1) * P], ident[:, :])
                    last.then_inc(S["h_turned"], 1)
                if is_tile(t - 1):
                    r = 1 - s
                    pe.wait_ge(S["h_out"], t)
                    need(pe, S["tables_made"], t - 2)
                    for k in range(2):
                        last = nc.tensor.matmul(ps[2 + r][:, :], hT[:, r, k * P:(k + 1) * P], wio[:, k, :], start=k == 0, stop=k == 1)
                    last.then_inc(S["tables_mm"], 1)
            over_tiles(pe, table_step, 1)

            def place_sums(ready, done):
                pe.wait_ge(ready, 1)
                nc.tensor.matmul(ps[6][:, 0:NTP], upper[:, :], cnt[:, :], start=True, stop=True)
                nc.tensor.matmul(ps[7][:, 0:NTP], ones[:, :], cnt[:, :], start=True, stop=True).then_inc(done, 1)

            pe.wait_ge(S["flagged"], 1)
            general = nc.tensor.value_load(flag[0:1, 0:1], min_val=0, max_val=1)

            def by_chunk(v):
                return v.rearrange("p (h j q) -> p h j q", h=2, j=CPG)

            with pe.If(general):
                for n in range(8):
                    if n:
                        pe.wait_ge(S["re_copied"], n)
                    for j in range(CPG):
                        last = nc.tensor.transpose(ps[6][:, j * P:(j + 1) * P], by_chunk(raw[n // 2])[:, n % 2, j, :], ident[:, :])
                    last.then_inc(S["re_turned"], 1)
                place_sums(S["re_counted"], S["re_sums"])

            pe.wait_ge(S["places"], 1)
            for n in range(10):
                v = (raw[0], raw[2], raw[3], raw_place2, raw[1])[n // 2]
                if n >= 2:
                    pe.wait_ge(S["columns_copied"], n - 1)
                for j in range(CPG):
                    last = nc.tensor.transpose(ps[6 + n % 2][:, j * P:(j + 1) * P], by_chunk(v)[:, n % 2, j, :], ident[:, :])
                last.then_inc(S["columns_turned"], 1)

            def in_turn(i):
                for s in range(RING):
                    g, h = RING * i + s, s % 2
                    pe.wait_ge(S[f"in_rows{s}"], (i + 1) * 16 * CPG)
                    pe.wait_ge(S["in_hot"], g + 1)
                    need(pe, S["in_added"], g - 1)
                    for w in range(2):
                        for j in range(CPG):
                            last = nc.tensor.matmul(ps[4 + h][:, w * D:(w + 1) * D], hot[:, h, j, w * P:(w + 1) * P],
                                                    big[:, s, j, 0:D], start=j == 0, stop=j == CPG - 1)
                    last.then_inc(S["in_mm"], 1)

            in_turn(0)
            with pe.Fori(1, 1 + PACKED) as i:
                in_turn(i)
            place_sums(S["counted"], S["place_sums"])
            pe.wait_ge(S["counted"], 2)
            nc.tensor.matmul(ps[7][:, 0:NU], ones[0:NT, :], mask[0:NT, 0:NU], start=True, stop=True).then_inc(S["place_sums"], 1)
            with pe.Fori(1 + PACKED, IN_TURNS[0][1]) as i:
                in_turn(i)
            with pe.If(general):
                with pe.Fori(*IN_TURNS[1]) as i:
                    in_turn(i)

            def out_turn(i, tiles):
                for s in range(RING):
                    g, h = RING * i + s, s % 2
                    pe.wait_ge(S["out_hot"], g + 1)
                    need(pe, S["out_msg"], g - 1)
                    for j in range(CPG):
                        b = ps[2 * h + j // 2]
                        last = nc.tensor.matmul(b[:, (j % 2) * D:(j % 2 + 1) * D], hot_flat(h)[:, j * P:(j + 1) * P],
                                                tab[:, h, :], start=True, stop=True)
                    last.then_inc(S["out_mm"], 1)
                    if s == 0 and tiles:
                        pe.wait_ge(S["c_sums"], i + 1)
                        pe.wait_ge(S["c_h"], i + 1)
                        need(pe, S["c_out"], i)
                        for k in range(4):
                            v = cs[:, k * P:(k + 1) * P] if k < 2 else cg[:, k * P + D:(k + 1) * P + D]
                            last = nc.tensor.transpose(ps[6][:, k * P:(k + 1) * P], v, ident[:, :])
                        last.then_inc(S["c_turned"], 1)
                    if s == 1 and tiles:
                        pe.wait_ge(S["c_out"], i + 1)
                        need(pe, S["c_sum"], i)
                        for k in range(4):
                            w = wx[:, k, :] if k < 2 else wh[:, k - 2, :]
                            last = nc.tensor.matmul(ps[7][:, :], ct[:, k * P:(k + 1) * P], w, start=k == 0, stop=k == 3)
                        last.then_inc(S["c_mm"], 1)

            out_turn(0, True)
            with pe.Fori(1, NT) as i:
                out_turn(i, True)
            for i in range(NT, NG_PLAIN // RING):
                out_turn(i, False)
            with pe.If(general):
                with pe.Fori(*IN_TURNS[1]) as i:
                    out_turn(i, False)

            def back_turn(i):
                for s in range(RING):
                    u, h = RING * i + s, s % 2
                    pe.wait_ge(S["back_hot"], u + 1)
                    need(pe, S["back_added"], u - 1)
                    for j in range(2):
                        last = nc.tensor.matmul(ps[4 + h][:, 0:D], hot[:, h, j, 0:P], unit[:, s, j, 0:D], start=j == 0, stop=j == 1)
                    last.then_inc(S["back_mm"], 1)
            back_turn(0)
            with pe.Fori(1, NU // RING) as i:
                back_turn(i)

            def gates_step(t, s):
                if is_tile(t):
                    pe.wait_ge(S["e_sums"], t + 1)
                    need(pe, S["e_out"], t - 1)
                    for k in range(2):
                        last = nc.tensor.transpose(ps[s][:, k * P:(k + 1) * P], st[:, s, k * P:(k + 1) * P], ident[:, :])
                    last.then_inc(S["e_turned"], 1)
                if is_tile(t - 1):
                    r = 1 - s
                    pe.wait_ge(S["e_out"], t)
                    need(pe, S["gate_sums"], t - 2)
                    for k in range(2):
                        last = nc.tensor.matmul(ps[2 + r][:, :], tT[:, r, k * P:(k + 1) * P], wx[:, 2 + k, :], start=k == 0, stop=k == 1)
                    last.then_inc(S["e_mm"], 1)
            over_tiles(pe, gates_step, 1)

            node_sum(ps[6][:, 0:D], node_a, S["x1_made"], S["x1_sum"])
            square_sum(ps[7][:, 0:D], S["d_sq"], S["d_sq_used"])

            def second_turn(i):
                for s in range(RING):
                    g, h = RING * i + s, s % 2
                    pe.wait_ge(S[f"second_rows{s}"], (i + 1) * 16 * CPG)
                    pe.wait_ge(S["second_hot"], g + 1)
                    need(pe, S["second_added"], g - 1)
                    for j in range(CPG):
                        last = nc.tensor.matmul(ps[4 + h][:, (j // 2) * D:(j // 2 + 1) * D], hot[:, h, j, 0:P],
                                                big[:, s, j, 0:D], start=j % 2 == 0, stop=j % 2 == 1)
                    last.then_inc(S["second_mm"], 1)
            second_turn(0)
            with pe.Fori(1, BACK_TURNS) as i:
                second_turn(i)

            def second_step(t, s):
                if is_tile(t):
                    pe.wait_ge(S["l_sums"], t + 1)
                    need(pe, S["l_out"], t - 1)
                    for k in range(2):
                        last = nc.tensor.transpose(ps[s][:, k * P:(k + 1) * P], st[:, s, k * P:(k + 1) * P], ident[:, :])
                    last.then_inc(S["l_turned"], 1)
                if is_tile(t - 1):
                    r = 1 - s
                    pe.wait_ge(S["l_out"], t)
                    need(pe, S["l_y"], t - 2)
                    for k in range(2):
                        last = nc.tensor.matmul(ps[2 + r][:, 0:D], tT[:, r, k * P:(k + 1) * P], w1[:, k, :], start=k == 0, stop=k == 1)
                    last.then_inc(S["l_mm"], 1)
            over_tiles(pe, second_step, 1)

        @block.vector
        def _(dve):
            link = Chain(dve, S["dve_chain"])
            V = nc.vector
            V.memset(raw_si[:, GE:2 * GE], NT * P)
            V.memset(raw_di[:, GE:2 * GE], N - 1)
            V.memset(raw[2][:, GE:2 * GE], 0.0)
            V.memset(raw[3][:, GE:2 * GE], 0.0)
            link(V.memset(node_a[:, FULL:NTP, :], 0.0))
            dve.sem_inc(S["pads_set"], 1)
            dve.wait_ge(S["edges_loaded"], 192)
            V.tensor_copy(raw[0], raw_si)
            link(V.tensor_copy(raw[1], raw_di))

            def by_half(v):
                return v.rearrange("p (h q) -> p h q", h=2)

            def low_high():
                V.tensor_reduce(dlow[:, :], by_half(raw[1]), AX.X, ALU.min)
                link(V.tensor_reduce(dhigh[:, :], by_half(raw[1]), AX.X, ALU.max))

            low_high()
            link(V.tensor_tensor(wide[:, :], dhigh[:, :], dlow[:, :], ALU.subtract))
            link(V.tensor_scalar(wide[:, :], wide[:, :], float(P - 1), None, ALU.is_gt))
            V.tensor_reduce(widest[:, :], wide[:, :], AX.X, ALU.max).then_inc(S["widest"], 1)

            dve.wait_ge(S["x_sum"], 1)
            link(V.tensor_scalar(mean_b[:, :], ps[4][:, 0:D], 1.0 / N, None, ALU.mult))
            with dve.Fori(0, NT) as t:
                V.tensor_tensor(tile_of(node_a, t), tile_of(node_a, t), mean_b[:, :], ALU.subtract).then_inc(S["x_centred"], 1)
            dve.wait_ge(S["widest"], 2)
            link(V.tensor_scalar(flag[0:1, 0:1], ps[6][0:1, 0:1], 1.0, None, ALU.min))
            dve.sem_inc(S["flagged"], 1)
            dve.wait_ge(S["x_sq_used"], NT)
            V.tensor_scalar(scale_b[:, :], ps[5][:, 0:D], 1.0 / N, None, ALU.mult).then_inc(S["x_var"], 1)
            dve.wait_ge(S["x_var"], 2)
            link(V.reciprocal(scale_b[:, :], scale_b[:, :]))
            dve.wait_ge(S["weights"], LOADS_W)
            link(V.tensor_tensor(scale_b[:, :], scale_b[:, :], gamma_b[:, :], ALU.mult))

            def table_step(t, s):
                if is_tile(t):
                    need(dve, S["h_turned"], t - 1)
                    V.tensor_tensor(hr[:, s, :], tile_of(node_a, t), scale_b[:, :], ALU.mult).then_inc(S["h_scaled"], 1)
                if is_tile(t - 2):
                    dve.wait_ge(S["tables_mm"], t - 1)
                    need(dve, S[f"tables_stored{s}"], 32 * (t // 2 - 1) if isinstance(t, int) else 32 * (t_half[0] - 1))
                    V.tensor_tensor(tabs[:, s, :], ps[2 + s][:, :], bio_b[:, :], ALU.add).then_inc(S["tables_made"], 1)
                if is_tile(t):
                    dve.wait_ge(S["h_scaled"], t + 1)
                    V.tensor_tensor(hr[:, s, :], hr[:, s, :], beta_b[:, :], ALU.add).then_inc(S["h_made"], 1)
            t_half = [None]
            for s in range(2):
                table_step(s, s)
            with dve.Fori(1, FULL // 2) as i:
                t_half[0] = i
                for s in range(2):
                    table_step(2 * i + s, s)
            for t in range(FULL, FULL + 3):
                table_step(t, t % 2)

            general = V.value_load(flag[0:1, 0:1], min_val=0, max_val=1)
            with dve.If(general):
                sub = Chain(dve, S["re_chain"])
                r4 = rec[:, 0:16 * GE // P, :]
                sub(V.memset(r4, 0.0))
                V.memset(r4[:, :, 0], float(NT * P))
                sub(V.memset(r4[:, :, 1], -1.0))
                dve.sem_inc(S["re_empty"], 1)
                dve.wait_ge(S["re_cleared"], 16 * (NG // 16))
                for n in range(8):
                    k, hh = n // 2, n % 2
                    dve.wait_ge(S["re_turned"], n + 1)
                    o = rec[:, hh * NC // 2:(hh + 1) * NC // 2, k].rearrange("p (g j) -> p g j", j=CPG)
                    V.tensor_copy(o, ps[6][:, :].rearrange("p (j g) -> p g j", j=CPG)).then_inc(S["re_copied"], 1)
                dve.wait_ge(S["re_copied"], 8)
                V.tensor_copy(mask_i, rec[:, :, 1])
                sub(V.tensor_copy(scan_i, rec[:, :, 0]))
                V.tensor_scalar(mask_i, mask_i, 7, None, ALU.logical_shift_right)
                sub(V.tensor_scalar(scan_i, scan_i, 7, None, ALU.logical_shift_right))
                V.tensor_copy(win, mask_i)
                sub(V.tensor_copy(win_b, scan_i))
                sub(V.tensor_scalar(win_b, win_b, float(NT), None, ALU.is_equal))
                sub(V.tensor_tensor(win, win, win_b, ALU.add))
                sub(V.memset(rank, 0.0))
                with dve.Fori(0, NTP) as w:
                    chain = Chain(dve, S["re_count"], w * 4)
                    chain(V.tensor_scalar(mask, win, iota_w[:, bass.ds(w, 1)], None, ALU.is_equal))
                    chain(V.tensor_tensor_scan(scan, mask, mask, 0.0, ALU.add, ALU.max))
                    V.tensor_copy(cnt[:, bass.ds(w, 1)], scan[:, NC - 1:NC])
                    chain(V.tensor_tensor(mask, scan, mask, ALU.mult))
                    chain(V.tensor_tensor(rank, rank, mask, ALU.add))
                dve.sem_inc(S["re_counted"], 1)
                dve.wait_ge(S["re_sums"], 1)
                sub(V.tensor_copy(aligi[:, :], ps[7][:, 0:NTP]))
                sub(V.tensor_scalar(aligi[:, :], aligi[:, :], ~(GE - 1), None, ALU.bitwise_and))
                sub(V.tensor_scalar(alig[:, :], aligi[:, :], float(GE), None, ALU.add))
                sub(V.tensor_tensor_scan(ends[:, :], alig[:, :], alig[:, :], 0.0, ALU.add, ALU.max))
                sub(V.tensor_tensor(starts[:, :], ends[:, :], alig[:, :], ALU.subtract))
                sub(V.scalar_tensor_tensor(basew[:, :], starts[:, :], -1.0, ps[6][:, 0:NTP], ALU.add, ALU.add))
                with dve.Fori(0, NTP) as w:
                    chain = Chain(dve, S["re_base"], w * 2)
                    chain(V.tensor_scalar(mask, win, iota_w[:, bass.ds(w, 1)], basew[:, bass.ds(w, 1)], ALU.is_equal, ALU.mult))
                    chain(V.tensor_tensor(rank, rank, mask, ALU.add))

                def hand(i):
                    need(dve, S["re_put"], i * 16 * RING)
                    dve.sem_inc(S["dve_may"], 1)
                    V.tensor_copy(rec_put[:, :, :], rec[:, bass.ds(i * RING, RING), :])
                    V.tensor_copy(stage[:, :, 0], rank[:, bass.ds(i * RING, RING)]).then_inc(S["re_handed"], 1)
                    dve.wait_ge(S["re_handed"], i + 1)
                    dve.sem_inc(S["re_staged"], 1)
                hand(0)
                with dve.Fori(1, NC // RING) as i:
                    hand(i)
                dve.wait_ge(S["re_loaded"], 32)
                for k in range(4):
                    last = V.tensor_copy(by_half(raw[k]), reload[:, :, :, k])
                sub(last)
                sub(V.tensor_reduce(dhigh[:, :], by_half(raw[1]), AX.X, ALU.max))
                sub(V.tensor_scalar(dhigh[:, :], dhigh[:, :], 0.0, None, ALU.max))
                sub(V.tensor_copy(dwini[:, :], dhigh[:, :]))
                sub(V.tensor_scalar(dwini[:, :], dwini[:, :], ~(P - 1), None, ALU.bitwise_and))
                sub(V.tensor_copy(dhigh[:, :], dwini[:, :]))
                for hh in range(2):
                    v = raw[1][:, hh * GE:(hh + 1) * GE]
                    last = V.tensor_scalar(v, v, dhigh[:, hh:hh + 1], None, ALU.max)
                sub(last)

            low_high()
            link(V.tensor_copy(dlowi[:, :], dlow[:, :]))
            V.tensor_scalar(dwini[:, :], dlowi[:, :], 7, None, ALU.logical_shift_right)
            link(V.tensor_scalar(doffi[:, :], dlowi[:, :], P - 1, None, ALU.bitwise_and))
            link(V.tensor_copy(doff[:, :], doffi[:, :]))
            for hh in range(2):
                c = slice(hh * GE, (hh + 1) * GE)
                V.tensor_scalar(raw_place[:, c], raw[1][:, c], dlow[:, hh:hh + 1], None, ALU.subtract)
                last = V.tensor_scalar(raw_place2[:, c], raw[1][:, c], dlow[:, hh:hh + 1], doff[:, hh:hh + 1], ALU.subtract, ALU.add)
            link(last)
            dve.sem_inc(S["lows"], 1)
            dve.sem_inc(S["places"], 1)
            for n in range(10):
                k, hh = n // 2, n % 2
                dve.wait_ge(S["columns_turned"], n + 1)
                c = slice(hh * NC // 2, (hh + 1) * NC // 2)
                to = (win_b[:, c], carried[:, c, 2], ow_col[:, c], place2[:, c], carried[:, c, 1])[k]
                V.tensor_copy(to.rearrange("p (g j) -> p g j", j=CPG),
                              ps[6 + n % 2][:, :].rearrange("p (j g) -> p g j", j=CPG)).then_inc(S["columns_copied"], 1)
            dve.wait_ge(S["columns_copied"], 10)
            link(V.tensor_copy(src_id, win_b))
            V.tensor_scalar(mask_i, src_id, 7, None, ALU.logical_shift_right)
            link(V.tensor_scalar(scan_i, src_id, P - 1, None, ALU.bitwise_and))
            V.tensor_copy(win, mask_i)
            link(V.tensor_copy(carried[:, :, 0], scan_i))
            V.memset(rank, 0.0)
            link(V.tensor_scalar(upper_half, win, float(PACKED), None, ALU.is_ge))
            link(V.scalar_tensor_tensor(half_win, upper_half, -float(PACKED), win, ALU.mult, ALU.add))
            link(V.tensor_scalar(half_unit, upper_half, 4095.0, 1.0, ALU.mult, ALU.add))
            link(V.memset(node_a[:, :, :], 0.0))

            def stage_in(g, s):
                V.tensor_copy(stage[:, s, :], src_id[:, bass.ds(g * CPG, CPG)]).then_inc(S["in_staged"], 1)

            def hot_in(g, s):
                need(dve, S["in_mm"], g - 1)
                for j in range(CPG):
                    last = V.tensor_scalar(hot[:, s % 2, j, :], iota2[:, :], place2[:, bass.ds(g * CPG + j, 1)],
                                           carried[:, bass.ds(g * CPG + j, 1), 2], ALU.is_equal, ALU.mult)
                last.then_inc(S["in_hot"], 1)

            def add_in(g, s):
                w = V.value_load(win_tab[0:1, bass.ds(g, 1)], min_val=0, max_val=NT - 1)
                dve.wait_ge(S["in_mm"], g + 1)
                need(dve, S["in_added"], g)
                o = node_a[:, bass.ds(w, 2), :].rearrange("p a d -> p (a d)")
                V.tensor_tensor(o, o, ps[4 + s % 2][:, :], ALU.add).then_inc(S["in_added"], 1)

            def in_turn(i, beside=(), first=False, last=False):
                for s in range(RING):
                    g = RING * i + s
                    hot_in(g, s)
                    if not (first and s == 0):
                        add_in(g - 1, (s - 1) % RING)
                        if not (last and s > 0):
                            dve.sem_inc(S["dve_may"], 1)
                            stage_in(g + RING - 1, (s - 1) % RING)
                    if s < len(beside):
                        beside[s]()

            def in_start(lo):
                dve.sem_inc(S["dve_may"], 1)
                for s in range(RING):
                    stage_in(lo * RING + s, s)

            def in_end(hi):
                add_in(hi * RING - 1, RING - 1)

            def rank_steps(k):
                chain = Chain(dve, S["rank_chain"], k * 4)

                def mark():
                    chain(V.scalar_tensor_tensor(mask, half_win, iota_w[:, bass.ds(k, 1)], half_unit, ALU.is_equal, ALU.mult))

                def run():
                    chain(V.tensor_tensor_scan(scan, mask, mask, 0.0, ALU.add, ALU.max))

                def pick():
                    V.tensor_scalar(cnt[:, bass.ds(k, 1)], scan[:, NC - 1:NC], 0.0, None, ALU.add)
                    chain(V.scalar_tensor_tensor(mask, half_win, iota_w[:, bass.ds(k, 1)], scan, ALU.is_equal, ALU.mult))

                def add():
                    chain(V.tensor_tensor(rank, rank, mask, ALU.add))
                return mark, run, pick, add

            def base_steps(k):
                chain = Chain(dve, S["base_chain"], k * 4)

                def of(w):
                    chain(V.tensor_scalar(mask, win, iota_w[:, bass.ds(w, 1)], basew[:, bass.ds(w, 1)], ALU.is_equal, ALU.mult))

                def add():
                    chain(V.tensor_tensor(rank, rank, mask, ALU.add))
                return (lambda: of(2 * k)), add, (lambda: of(2 * k + 1)), add

            in_start(0)
            dve.wait_ge(S["low_tabs"], 64)
            in_turn(0, first=True)
            with dve.Fori(1, 1 + PACKED) as i:
                in_turn(i, rank_steps(i - 1))
            V.tensor_copy(mask_i, rank)
            link(V.tensor_copy(aligi[:, 0:PACKED], cnt[:, 0:PACKED]))
            V.tensor_scalar(scan_i, mask_i, 12, None, ALU.logical_shift_right)
            V.tensor_scalar(aligi[:, PACKED:NTP], aligi[:, 0:PACKED], 12, None, ALU.logical_shift_right)
            link(V.tensor_scalar(aligi[:, 0:PACKED], aligi[:, 0:PACKED], 4095, None, ALU.bitwise_and))
            link(V.tensor_scalar(mask_i, mask_i, 4095, None, ALU.bitwise_and))
            V.tensor_copy(cnt[:, :], aligi[:, :])
            V.tensor_copy(rank, mask_i)
            link(V.tensor_copy(half_unit, scan_i))
            dve.sem_inc(S["counted"], 1)
            link(V.tensor_tensor(half_unit, half_unit, rank, ALU.subtract))
            link(V.tensor_tensor(half_unit, half_unit, upper_half, ALU.mult))
            link(V.tensor_tensor(rank, rank, half_unit, ALU.add))
            dve.wait_ge(S["place_sums"], 1)
            link(V.tensor_copy(aligi[:, :], ps[7][:, 0:NTP]))
            link(V.tensor_scalar(aligi[:, :], aligi[:, :], ~(UR - 1), None, ALU.bitwise_and))
            link(V.tensor_scalar(alig[:, :], aligi[:, :], float(UR), None, ALU.add))
            link(V.tensor_tensor_scan(ends[:, :], alig[:, :], alig[:, :], 0.0, ALU.add, ALU.max))
            link(V.tensor_tensor(starts[:, :], ends[:, :], alig[:, :], ALU.subtract))
            link(V.scalar_tensor_tensor(basew[:, :], starts[:, :], -1.0, ps[6][:, 0:NTP], ALU.add, ALU.add))
            link(V.tensor_tensor(diag[:, :], ends[:, :], ident[:, 0:NTP], ALU.mult))
            link(V.tensor_reduce(endcol[:, :], diag[:, :], AX.X, ALU.add))
            link(V.tensor_scalar(mask[:, 0:NU], iota_u, endcol[:, :], None, ALU.is_ge))
            dve.sem_inc(S["counted"], 1)
            link(V.tensor_scalar(starts[:, :], ends[:, :], float(-UR), None, ALU.add))
            V.tensor_copy(fill_row[:, :], starts[0:1, :])
            V.tensor_scalar(unit_row, iota_u[32:33, :], starts[32:33, NT - 1:NT], None, ALU.min)
            dve.wait_ge(S["place_sums"], 2)
            link(V.tensor_copy(unit_win, ps[7][0:1, 0:NU]))
            dve.sem_inc(S["rows_ready"], 1)
            with dve.Fori(1 + PACKED, 1 + 2 * PACKED) as i:
                in_turn(i, base_steps(i - (1 + PACKED)))
            for i in range(1 + 2 * PACKED, IN_TURNS[0][1]):
                in_turn(i, last=i == IN_TURNS[0][1] - 1)
            in_end(IN_TURNS[0][1])
            with dve.If(general):
                lo, hi = IN_TURNS[1]
                in_start(lo)
                in_turn(lo, first=True)
                with dve.Fori(lo + 1, hi - 1) as i:
                    in_turn(i)
                in_turn(hi - 1, last=True)
                in_end(hi)
                dve.wait_ge(S["in_added"], NG)
            dve.wait_ge(S["in_added"], NG_PLAIN)
            link(V.tensor_copy(slot, rank))
            dve.sem_inc(S["in_done"], 1)
            link(V.memset(node_c[:, :, :], 0.0))

            def out_turn(i, tiles):
                if tiles:
                    chain = Chain(dve, S["c_chain"], i * 2)
                    dve.wait_ge(S["cx_loaded"], (i + 1) * 16)
                    need(dve, S["c_stored"], i * 16)
                    h = cg[:, 2 * D:3 * D]
                    chain(V.tensor_tensor(h, cx, mean_b[:, :], ALU.subtract))
                    chain(V.tensor_tensor(h, h, scale_b[:, :], ALU.mult))
                    V.tensor_tensor(h, h, beta_b[:, :], ALU.add).then_inc(S["c_h"], 1)
                for s in range(RING):
                    g, h = RING * i + s, s % 2
                    dve.wait_ge(S[f"out_load{h}"], (2 * i + s // 2 + 1) * 32)
                    need(dve, S["out_mm"], g - 1)
                    V.tensor_scalar(hot_flat(h)[:, 0:GE], place_b[:, h, :], pcol[:, :], None, ALU.is_equal).then_inc(S["out_hot"], 1)
                    need(dve, S[f"sent{s}"], i * 16 * CPG)
                    dve.sem_inc(S["dve_may"], 1)
                    V.tensor_copy(big[:, s, :, D:D + RW], carried[:, bass.ds(g * CPG, CPG), :])
                    V.tensor_copy(stage[:, s, :], slot[:, bass.ds(g * CPG, CPG)]).then_inc(S["out_carried"], 1)
                    if s == 2 and tiles:
                        dve.wait_ge(S["c_mm"], i + 1)
                        V.tensor_tensor(cg[:, 0:2 * D], ps[7][:, :], bx_b[:, :], ALU.add).then_inc(S["c_sum"], 1)

            out_turn(0, True)
            with dve.Fori(1, NT) as i:
                out_turn(i, True)
            for i in range(NT, NG_PLAIN // RING):
                out_turn(i, False)
            with dve.If(general):
                with dve.Fori(*IN_TURNS[1]) as i:
                    out_turn(i, False)

            def hot_back(u, s, i):
                dve.wait_ge(S[f"back_load{s}"], (i + 1) * 16)
                need(dve, S["back_mm"], u - 1)
                for j in range(2):
                    last = V.tensor_scalar(hot[:, s % 2, j, 0:P], iota2[:, 0:P], unit[:, s, j, D:D + 1], None, ALU.is_equal)
                last.then_inc(S["back_hot"], 1)

            def add_back(u, s):
                w = V.value_load(unit_win[0:1, bass.ds(u, 1)], min_val=0, max_val=NT)
                dve.wait_ge(S["back_mm"], u + 1)
                need(dve, S["back_added"], u)
                V.tensor_tensor(tile_of(node_c, w), tile_of(node_c, w), ps[4 + s % 2][:, 0:D], ALU.add).then_inc(S["back_added"], 1)

            def back_turn(i, first=False):
                for s in range(RING):
                    hot_back(RING * i + s, s, i)
                    if not (first and s == 0):
                        add_back(RING * i + s - 1, (s - 1) % RING)
            back_turn(0, True)
            with dve.Fori(1, NU // RING) as i:
                back_turn(i)
            add_back(NU - 1, RING - 1)
            dve.wait_ge(S["back_added"], NU)
            dve.sem_inc(S["out_done"], 1)

            def gates_step(t, s):
                if is_tile(t - 1):
                    r = 1 - s
                    dve.wait_ge(S["e_mm"], t)
                    dve.wait_ge(S[f"gates_load{r}"], gates_loads(t, s))
                    need(dve, S["gates_made"], t - 2)
                    V.tensor_tensor(ub[:, r, :], ps[2 + r][:, :], gates_in[:, r, 0:2 * D], ALU.add).then_inc(S["gate_sums"], 1)
                if is_tile(t - 2):
                    u = t - 2
                    chain = Chain(dve, S["e_chain"], u * 5)
                    dve.wait_ge(S["gates_made"], t - 1)
                    y, gate, new = tile_of(node_a, u), gb[:, s, 0:D], gb[:, s, D:2 * D]
                    chain(V.tensor_tensor(y, gates_in[:, s, 2 * D:3 * D], new, ALU.subtract))
                    chain(V.tensor_tensor(y, y, gate, ALU.mult))
                    dve.wait_ge(S["xn_made"], t - 1)
                    chain(V.tensor_tensor(y, y, xn[:, s, :], ALU.add))
                    dve.sem_inc(S["y_made"], 1)
                    chain(V.bn_stats(bn6[:, :], y))
                    dve.sem_inc(S["dve_may"], 1)
                    chain(V.bn_aggr(mv_t[:, :], bn6[:, :]))
                    V.tensor_scalar(mv[:, bass.ds(u, 1), :].rearrange("p a d -> p (a d)"), mv_t[:, :], 0.0, None, ALU.add).then_inc(S["e_mv"], 1)

            def gates_loads(t, s):
                if isinstance(t, int):
                    return 32 * ((t - 1) // 2 + 1)
                return 32 * (now[0] + s)

            now = [None]
            for t in range(2):
                gates_step(t, t)
            with dve.Fori(1, FULL // 2) as i:
                now[0] = i
                for s in range(2):
                    gates_step(2 * i + s, s)
            for t in range(FULL, FULL + 3):
                gates_step(t, t % 2)
            dve.wait_ge(S["e_mv"], NT)
            dve.sem_inc(S["y_stats"], 1)
            dve.wait_ge(S["y_stats"], 2)
            link(V.reciprocal(rstd[:, :], rstd[:, :]))

            with dve.Fori(0, NT) as t:
                V.tensor_scalar(tile_of(node_a, t), tile_of(node_a, t), mv[:, bass.ds(t, 1), 0], rstd[:, bass.ds(t, 1)],
                                ALU.subtract, ALU.mult).then_inc(S["x1_made"], 1)
            dve.wait_ge(S["x1_sum"], 1)
            link(V.tensor_scalar(mean_b[:, :], ps[6][:, 0:D], 1.0 / N, None, ALU.mult))
            with dve.Fori(0, NT) as t:
                V.tensor_tensor(tile_of(node_c, t), tile_of(node_a, t), mean_b[:, :], ALU.subtract).then_inc(S["d_made"], 1)
            dve.wait_ge(S["d_sq_used"], NT)
            V.tensor_scalar(scale_b[:, :], ps[7][:, 0:D], 1.0 / (N - 1), None, ALU.mult).then_inc(S["d_var"], 1)
            dve.wait_ge(S["d_var"], 2)
            link(V.tensor_scalar(scale_b[:, :], scale_b[:, :], 1e-4, None, ALU.add))
            link(V.reciprocal(scale_b[:, :], scale_b[:, :]))
            with dve.Fori(0, NT) as t:
                V.tensor_tensor(tile_of(node_c, t), tile_of(node_c, t), scale_b[:, :], ALU.mult).then_inc(S["z_made"], 1)

            def stage_second(g, s):
                V.tensor_copy(stage[:, s, :], back_id[:, bass.ds(g * CPG, CPG)]).then_inc(S["second_staged"], 1)

            def hot_second(g, s):
                need(dve, S["second_mm"], g - 1)
                for j in range(CPG):
                    last = V.tensor_scalar(hot[:, s % 2, j, 0:P], iota2[:, 0:P], back[:, bass.ds(g * CPG + j, 1), 0],
                                           back[:, bass.ds(g * CPG + j, 1), 2], ALU.is_equal, ALU.mult)
                last.then_inc(S["second_hot"], 1)

            def add_second(g, s):
                for k in range(2):
                    w = V.value_load(unit_win[0:1, bass.ds(g * 2 + k, 1)], min_val=0, max_val=NT)
                    if k == 0:
                        dve.wait_ge(S["second_mm"], g + 1)
                    need(dve, S["second_adds"], g * 2 + k)
                    last = V.tensor_tensor(tile_of(node_c, w), tile_of(node_c, w), ps[4 + s % 2][:, k * D:(k + 1) * D], ALU.add)
                    last.then_inc(S["second_adds"], 1)
                dve.wait_ge(S["second_adds"], g * 2 + 2)
                dve.sem_inc(S["second_added"], 1)

            def second_turn(i, first=False, last=False):
                for s in range(RING):
                    g = RING * i + s
                    hot_second(g, s)
                    if not (first and s == 0):
                        add_second(g - 1, (s - 1) % RING)
                        if not (last and s > 0):
                            dve.sem_inc(S["dve_may"], 1)
                            stage_second(g + RING - 1, (s - 1) % RING)

            dve.wait_ge(S["back_ids"], 1)
            dve.sem_inc(S["dve_may"], 1)
            for s in range(RING):
                stage_second(s, s)
            dve.wait_ge(S["z_ready"], 1)
            link(V.memset(node_c[:, :, :], 0.0))
            second_turn(0, first=True)
            with dve.Fori(1, BACK_TURNS - 1) as i:
                second_turn(i)
            second_turn(BACK_TURNS - 1, last=True)
            add_second(BACK_TURNS * RING - 1, RING - 1)
            dve.sem_inc(S["second_done"], 1)

            def second_step(t, s):
                if is_tile(t - 1):
                    r, u = 1 - s, t - 1
                    chain = Chain(dve, S["l_chain"], u * 4)
                    dve.wait_ge(S["l_mm"], t)
                    y = tile_of(node_c, u)
                    chain(V.tensor_tensor(y, ps[2 + r][:, 0:D], b1_b[:, :], ALU.add))
                    dve.sem_inc(S["l_y"], 1)
                    chain(V.tensor_tensor(y, y, tile_of(node_a, u), ALU.add))
                    dve.sem_inc(S["dve_may"], 1)
                    chain(V.bn_stats(bn6[:, :], y))
                    dve.sem_inc(S["dve_may"], 1)
                    chain(V.bn_aggr(mv_t[:, :], bn6[:, :]))
                    V.tensor_scalar(mv[:, bass.ds(u, 1), :].rearrange("p a d -> p (a d)"), mv_t[:, :], 0.0, None, ALU.add).then_inc(S["l_mv"], 1)
            over_tiles(dve, second_step, 1)
            dve.wait_ge(S["l_mv"], NT)
            dve.sem_inc(S["l_stats"], 1)
            dve.wait_ge(S["l_stats"], 2)
            link(V.reciprocal(rstd[:, :], rstd[:, :]))

            def result_tile(t, s, stored):
                need(dve, S[f"result_stored{s}"], stored)
                V.tensor_scalar(gb[:, s, 0:D], tile_of(node_c, t), mv[:, bass.ds(t, 1), 0], rstd[:, bass.ds(t, 1)],
                                ALU.subtract, ALU.mult).then_inc(S["result"], 1)
            for s in range(2):
                result_tile(s, s, 0)
            with dve.Fori(1, FULL // 2) as i:
                for s in range(2):
                    result_tile(2 * i + s, s, 16 * i)
            result_tile(FULL, 0, 16 * (FULL // 2))


_INS = ["x", "src", "dst", "edge_weight", "edge_weight_n2", "L0_gnn_gamma", "L0_gnn_beta", "L0_gnn_W_in",
        "L0_gnn_b_in", "L0_gnn_W_out", "L0_gnn_b_out", "L0_gnn_W_x2i", "L0_gnn_b_x2i", "L0_gnn_W_h2h",
        "L1_gnn_weight", "L1_gnn_bias"]


def kernel(**inputs):
    import numpy as _np
    import concourse.bacc as _bacc
    from concourse import mybir as _mybir
    from concourse.bass_utils import run_bass_kernel_spmd as _run

    nc = _bacc.Bacc("TRN2", target_bir_lowering=False, num_devices=1)
    arrays, args = {}, []
    for name in _INS:
        a = _np.ascontiguousarray(inputs[name])
        arrays[f"in_{name}"] = a
        args.append(nc.dram_tensor(f"in_{name}", a.shape, _mybir.dt.from_np(a.dtype), kind="ExternalInput").ap())
    args.append(nc.dram_tensor("out_0", (N, D), _mybir.dt.float32, kind="ExternalOutput").ap())
    gnn_program(nc, *args)
    r = _run(nc, [arrays], core_ids=[0])
    return r.results[0]["out_0"]
```

```python
import concourse.bass as bass
import concourse.mybir as mybir
from contextlib import ExitStack

P = 128
N, D, E = 6250, 256, 106250
NT = -(-N // P)
NTP = NT + 1
FULL = N // P
TAIL = N - FULL * P
CPG = 4
GE = CPG * P
NG = -(-(E // GE + NT) // 8) * 8
NG_PLAIN = -(-(-(-E // GE)) // 8) * 8
NC = NG * CPG
UR = 256
NU = E // UR + NT
RW = 3
MW = 260
MROWS = NU * UR + NG * GE - E
SPAN = 6
SPANS = FULL // SPAN
FIRST = 23
RING = 4
EPS = 1e-5

F32 = mybir.dt.float32
I32 = mybir.dt.int32
ALU = mybir.AluOpType
ACT = mybir.ActivationFunctionType
AX = mybir.AxisListType


class Chain:

    def __init__(self, engine, semaphore, base=0):
        self.engine, self.semaphore, self.base, self.n = engine, semaphore, base, 0

    def __call__(self, instruction):
        instruction.then_inc(self.semaphore, 1)
        self.n += 1
        self.engine.wait_ge(self.semaphore, self.base + self.n)


def need(engine, semaphore, value):
    if not isinstance(value, int) or value > 0:
        engine.wait_ge(semaphore, value)


def is_tile(t):
    return not isinstance(t, int) or 0 <= t < NT


def over_tiles(engine, step, after=0, lag=1, turn=2):
    peeled = -(-lag // turn)
    for t in range(turn * peeled):
        step(t, t % turn)
    with engine.Fori(peeled, FULL // turn) as i:
        for s in range(turn):
            step(turn * i + s, s)
    for t in range(FULL, FULL + 1 + after):
        step(t, t % turn)


def gnn_program(nc, x, src, dst, edge_weight, edge_weight_n2, gamma, beta, w_in, b_in, w_out, b_out,
                w_x2i, b_x2i, w_h2h, w_l1, b_l1, out):
    ctx = ExitStack()
    with ctx:
        def sb(name, shape, dt=F32):
            return ctx.enter_context(nc.sbuf_tensor(name, shape, dt))

        def dram(name, shape, dt=F32):
            return nc.dram_tensor(name, shape, dt, kind="Internal").ap()

        class Semaphores(dict):
            def __missing__(self, name):
                self[name] = ctx.enter_context(nc.semaphore(name))
                return self[name]

        S = Semaphores()

        in_table = dram("in_table", [NTP * P, D])
        out_table = dram("out_table", [NTP * P, D])
        h_turned = dram("h_turned", [NT * P, D])
        d_table = dram("d_table", [NTP * P, D])
        place_row = dram("place_row", [NG * GE])
        group_row = dram("group_row", [NG], I32)
        records = dram("records", [NG * GE, 4])
        messages = dram("messages", [MROWS, MW])
        gate_rows = dram("gate_rows", [NT * P, 3 * D])

        node_a = sb("node_a", [P, NTP, D])
        node_c = sb("node_c", [P, NTP, D])
        work = sb("work", [P, max(6 * NC + 4096, RING * CPG * MW + 4 * GE + RING * 4 * MW)])

        def area(at, shape, dt=F32):
            n = 1
            for d in shape:
                n *= d
            v = work[:, at:at + n]
            if len(shape) == 2:
                v = v.rearrange("p (a b) -> p a b", b=shape[1])
            elif len(shape) == 3:
                v = v.rearrange("p (a b c) -> p a b c", b=shape[1], c=shape[2])
            return v if dt == F32 else v.bitcast(dt)

        flat_c = node_c[:, :, :].rearrange("p t d -> p (t d)")

        def part_c(k, n=1):
            return flat_c[:, k * NC:(k + n) * NC]

        raw_si, raw_di = area(0, [NC], I32), area(NC, [NC], I32)
        raw_place = area(0, [NC])
        raw = [area((2 + k) * NC, [NC]) for k in range(4)]
        win, mask, scan, rank, half_win, half_unit, upper_half, win_b = (part_c(k) for k in range(8))
        mask_i, scan_i = mask.bitcast(I32), scan.bitcast(I32)
        rec = part_c(8, 4).rearrange("p (c k) -> p c k", k=4)
        reload = part_c(8, 4).rearrange("p (h q k) -> p h q k", h=2, k=4)
        rec_put = sb("rec_put", [P, RING, 4])

        columns = sb("columns", [P, 4 * D + 7 * NC])
        wio = columns[:, 0:4 * D].rearrange("p (k n) -> p k n", k=2)
        ow_col, slot_f, src_f, place = (columns[:, 4 * D + k * NC:4 * D + (k + 1) * NC] for k in range(4))
        slot, src_id = slot_f.bitcast(I32), src_f.bitcast(I32)
        carried = columns[:, 4 * D + 4 * NC:4 * D + 7 * NC].rearrange("p (c k) -> p c k", k=RW)
        back = columns[:, 0:2 * NU * RW].rearrange("p (c k) -> p c k", k=RW)
        back_id = src_id[:, 0:2 * NU]

        wx = sb("wx", [P, 4, 2 * D])
        wh = sb("wh", [P, 2, 2 * D])
        w1 = sb("w1", [P, 2, D])
        gamma_b, beta_b, b1_b = sb("gamma_b", [P, D]), sb("beta_b", [P, D]), sb("b1_b", [P, D])
        bias_b = sb("bias_b", [P, 4 * D])
        bio_b, bx_b = bias_b[:, 0:2 * D], bias_b[:, 2 * D:4 * D]
        mean_b, scale_b = sb("mean_b", [P, D]), sb("scale_b", [P, D])
        eps_c = sb("eps_c", [P, 1])
        dev = sb("dev", [P, 2])

        ident, ones, upper = sb("ident", [P, P]), sb("ones", [P, P]), sb("upper", [P, P])
        iota = sb("iota", [P, P])
        iota_w = sb("iota_w", [P, NTP])
        iota_u = flat_c[:, 12 * NC:12 * NC + NU]
        pcol = sb("pcol", [P, 1])
        cnt, ends, starts = sb("cnt", [P, NTP]), sb("ends", [P, NTP]), sb("starts", [P, NTP])
        alig, aligi = sb("alig", [P, NTP]), sb("aligi", [P, NTP], I32)
        basew, diag = sb("basew", [P, NTP]), sb("diag", [P, NTP])
        endcol = sb("endcol", [P, 1])
        dlow, dhigh = sb("dlow", [P, 2]), sb("dhigh", [P, 2])
        dlowi, dwini = sb("dlowi", [P, 2], I32), sb("dwini", [P, 2], I32)
        wide, widest = sb("wide", [P, 2]), sb("widest", [P, 1])
        flag = sb("flag", [1, 1], I32)
        low_tab = sb("low_tab", [1, NG], I32)
        low_two = sb("low_two", [1, NG // 2], I32)
        four_wins = sb("four_wins", [1, NU // 4], I32)
        wins_f = sb("wins_f", [1, NU // 4])
        pair_row = sb("pair_row", [1, NU // 2], I32)
        fill_row, flat_row = sb("fill_row", [1, NTP], I32), sb("flat_row", [1, 1], I32)
        zeros = sb("zeros", [P, UR // P, MW])
        stage = sb("stage", [P, RING, CPG], I32)
        bn6, mv, rstd = sb("bn6", [P, 2, 6]), sb("mv", [P, 4, 2]), sb("rstd", [P, 4, 1])
        mv_all, rstd_all = sb("mv_all", [P, NT, 2]), sb("rstd_all", [P, NT])

        big = area(0, [RING, CPG, MW])
        hot_at = RING * CPG * MW
        hot = area(hot_at, [2, CPG, P])
        hot_b = [area(hot_at + 1024 + k * GE, [CPG, P]) for k in range(2)] + [v.rearrange("p (a b) -> p a b", b=P) for v in (bio_b, bx_b)]
        tab = area(hot_at + 2048, [2, D])
        place_b = area(hot_at + 2560, [2, GE])
        extra = hot_at + 3584
        cx, cg, ct = (area(extra + a, [n]) for a, n in ((0, D), (D, 3 * D), (4 * D, D)))
        h_in, o_out = area(extra, [2, D]), area(extra + 512, [2, D])
        pair = area(hot_at + 2048, [RING, 4, MW])
        gates_in = area(0, [2, 4 * D])
        ub, gb = area(2048, [2, 2 * D]), area(3072, [2, 2 * D])
        st = area(hot_at, [2, 4, P])
        result = area(3072, [4, D])
        xn, hn = area(hot_at + 1024, [2, D]), area(hot_at + 1536, [2, D])
        hr = area(6 * NC, [2, D])
        sq = area(6 * NC + 1536, [SPAN // 2, 2 * D])
        hT, tabs = area(6 * NC + 512, [4, D]), area(6 * NC + 1536, [4, D])

        in_sums = node_a[:, :, :].rearrange("p t d -> p (t d)").rearrange("p (k n) -> p k n", k=2)

        def hot_flat(h):
            return hot[:, h, :, :].rearrange("p a b -> p (a b)")

        def halves(v):
            return v.rearrange("p (k n) -> p k n", k=2)

        ps = [ctx.enter_context(nc.psum_tensor(f"ps{i}", [P, 2 * D], F32)) for i in range(8)]

        def tile_of(table, t):
            return table[:, bass.ds(t, 1), :].rearrange("p o d -> p (o d)")

        def row_view(v):
            return v.rearrange("(o n) -> o n", o=1)

        PLAIN, ALL = NG_PLAIN // RING, NG // RING
        PAIRS = NU // 2
        PAIRS_T = PAIRS // (PLAIN - FIRST)
        PACKED = NTP // 2
        LOW_BITS, WIN_BITS = 13, 6
        RANKED = 1 + (PACKED + 1) // 2
        BASES_T = 6
        BACK_TURNS = NU // (2 * RING)
        LOADS_W = 11 * 16

        block = ctx.enter_context(nc.Block())

        @block.sync
        def _(sp):
            sp.wait_ge(S["pads_set"], 1)
            full2 = (E - P * GE) // GE
            rest = E - (P + full2) * GE
            for a, to in ((src, raw_si), (dst, raw_di), (edge_weight, raw[2]), (edge_weight_n2, raw[3])):
                v = to.rearrange("p (h q) -> p h q", h=2)
                for s, d in ((a[0:P * GE].rearrange("(g q) -> g q", q=GE), v[:, 0, :]),
                             (a[P * GE:(P + full2) * GE].rearrange("(g q) -> g q", q=GE), v[0:full2, 1, :]),
                             (a[(P + full2) * GE:E].rearrange("(g q) -> g q", g=1), v[full2:full2 + 1, 1, 0:rest])):
                    sp.dma_start(d, s).then_inc(S["edges_loaded"], 16)
            sp.dma_start(node_a[0:TAIL, FULL, :], x[FULL * P:N, :]).then_inc(S[f"span_moved{SPANS}"], 16)
            for k in range(SPANS):
                t = k * SPAN
                sp.dma_start(node_a[:, t:t + SPAN, :],
                             x[t * P:(t + SPAN) * P, :].rearrange("(t p) d -> p t d", p=P)).then_inc(S[f"span_moved{k}"], 16)
            sp.wait_ge(S["constants"], 5)
            for tb in (in_table, out_table, d_table):
                sp.dma_start(tb[NT * P:NTP * P, :], zeros[:, 0, 0:D]).then_inc(S["spare_rows"], 16)

            sp.wait_ge(S["flagged"], 1)
            general = nc.sync.value_load(flag[0:1, 0:1], min_val=0, max_val=1)
            with sp.If(general):
                sp.wait_ge(S["re_empty"], 1)
                for g in range(NG // 16):
                    sp.dma_start(records[g * 16 * GE:(g + 1) * 16 * GE, :].rearrange("(p q) k -> p (q k)", p=P),
                                 rec[:, 0:16 * GE // P, :].rearrange("p q k -> p (q k)")).then_inc(S["re_cleared"], 16)
                sp.wait_ge(S["re_put"], 16 * NC)
                rv = records.rearrange("(h g q) k -> h g (q k)", h=2, q=GE)
                for hh in range(2):
                    sp.dma_start(reload[:, hh, :, :].rearrange("p q k -> p (q k)"), rv[hh]).then_inc(S["re_loaded"], 16)

            sp.wait_ge(S["lows"], 1)
            sp.dma_start(group_row.rearrange("(h g) -> g h", h=2), dlowi[:, :],
                         allow_slow_non_contiguous=True).then_inc(S["low_tabs"], 16)
            sp.dma_start(place_row.rearrange("(h g q) -> g h q", h=2, q=GE),
                         raw_place.rearrange("p (h q) -> p h q", h=2)).then_inc(S["places_stored"], 16)
            sp.wait_ge(S["low_tabs"], 16)
            sp.dma_start(low_tab[:, :], row_view(group_row)).then_inc(S["low_tabs"], 16)

            def store_tables(t, s):
                sp.wait_ge(S["tables_made"], t + 1)
                sp.dma_start(in_table[bass.ds(t * P, P), :], tabs[:, s, :]).then_inc(S[f"tables_stored{s}"], 16)
                sp.dma_start(h_turned[bass.ds(t * P, P), :], hT[:, s, :]).then_inc(S[f"tables_stored{s}"], 16)
            over_tiles(sp, store_tables, turn=4)

            sp.wait_ge(S["tables_stored0"], 32 * (FULL // 4 + 1))
            for s in range(1, 4):
                sp.wait_ge(S[f"tables_stored{s}"], 32 * (FULL // 4))
            sp.wait_ge(S["spare_rows"], 48)
            sp.wait_ge(S["places_stored"], 16)
            sp.wait_ge(S["low_tabs"], 32)
            sp.sem_inc(S["tables_ready"], 1)

            def second_table(t, s):
                if is_tile(t):
                    need(sp, S["o_mm"], t - 1)
                    sp.dma_start(h_in[:, s, :], h_turned[bass.ds(t * P, P), :]).then_inc(S[f"h_loaded{s}"], 16)
                if is_tile(t - 1):
                    sp.wait_ge(S["o_made"], t)
                    sp.dma_start(out_table[bass.ds((t - 1) * P, P), :], o_out[:, 1 - s, :]).then_inc(S[f"o_stored{1 - s}"], 16)
            over_tiles(sp, second_table, 1)

            sp.wait_ge(S["rows_ready"], 1)
            for w in range(NTP):
                r = nc.sync.value_load(fill_row[0:1, w:w + 1], min_val=0, max_val=NU * UR)
                sp.dma_start(messages[bass.ds(r, UR), :].rearrange("(p j) c -> p j c", p=P), zeros[:, :, :]).then_inc(S["zero_rows"], 16)

            sp.wait_ge(S["o_stored0"], 16 * (FULL // 2 + 1))
            sp.wait_ge(S["o_stored1"], 16 * (FULL // 2))
            sp.dma_start(cx, x[0:P, :]).then_inc(S["cx_loaded"], 16)

            def out_loads(g, s):
                need(sp, S["out_mm"], g - 1)
                r = nc.sync.value_load(low_tab[0:1, bass.ds(g, 1)], min_val=0, max_val=N - 1)
                sp.dma_start(tab[:, s % 2, :], out_table[bass.ds(r, P), :]).then_inc(S[f"out_load{s % 2}"], 16)
                sp.dma_start(place_b[:, s % 2, :],
                             row_view(place_row[bass.ds(g * GE, GE)]).broadcast_to([P, GE])).then_inc(S[f"out_load{s % 2}"], 16)

            def out_turn(i):
                for s in range(RING):
                    out_loads(RING * i + s, s)
                    if s == 2 and is_tile(i):
                        sp.wait_ge(S["c_h"], i + 1)
                        if isinstance(i, int) and i + 1 == FULL:
                            sp.dma_start(cx[0:TAIL, :], x[FULL * P:N, :]).then_inc(S["cx_loaded"], 16)
                        elif is_tile(i + 1):
                            sp.dma_start(cx, x[bass.ds((i + 1) * P, P), :]).then_inc(S["cx_loaded"], 16)
                    if s == 3 and is_tile(i):
                        sp.wait_ge(S["c_sum"], i + 1)
                        sp.dma_start(gate_rows[bass.ds(i * P, P), :], cg).then_inc(S["c_stored"], 16)

            out_turn(0)
            with sp.Fori(1, FULL - 1) as i:
                out_turn(i)
            for i in range(FULL - 1, PLAIN):
                out_turn(i)
            with sp.If(general):
                with sp.Fori(PLAIN, ALL) as i:
                    for s in range(RING):
                        out_loads(RING * i + s, s)
            for k in range(RING):
                sp.wait_ge(S[f"sent{k}"], 16 * CPG * PLAIN)
            with sp.If(general):
                for k in range(RING):
                    sp.wait_ge(S[f"sent{k}"], 16 * CPG * ALL)

            def back_load(q, k):
                need(sp, S["back_mm"], q - RING + 1)
                need(sp, S["back_kept"], q - RING + 1)
                r = nc.sync.value_load(pair_row[0:1, bass.ds(q, 1)], min_val=0, max_val=(NU - 2) * UR)
                sp.dma_start(pair[:, k, :, :].rearrange("p (u j) c -> p u (j c)", u=2),
                             messages[bass.ds(r, 2 * UR), :].rearrange("(u p j) c -> p u (j c)", u=2, p=P)).then_inc(S[f"back_load{k}"], 16)
            for k in range(RING):
                back_load(k, k)
            with sp.Fori(1, PAIRS // RING) as i:
                for k in range(RING):
                    back_load(RING * i + k, k)

            def gates_load(t, s):
                need(sp, S["gate_sums"], t - 1)
                need(sp, S["xn_made"], t - 1)
                sp.dma_start(gates_in[:, s, 0:3 * D], gate_rows[bass.ds(t * P, P), :]).then_inc(S[f"gates_load{s}"], 16)
                if isinstance(t, int) and t == FULL:
                    sp.dma_start(gates_in[0:TAIL, s, 3 * D:4 * D], x[FULL * P:N, :]).then_inc(S[f"gates_load{s}"], 16)
                else:
                    sp.dma_start(gates_in[:, s, 3 * D:4 * D], x[bass.ds(t * P, P), :]).then_inc(S[f"gates_load{s}"], 16)
            sp.wait_ge(S["c_stored"], 16 * NT)
            sp.wait_ge(S["sums_done"], 1)
            over_tiles(sp, gates_load)

            for k in range(SPANS + 1):
                t, n = k * SPAN, SPAN if k < SPANS else 1
                sp.wait_ge(S["d_made"], k + 1)
                sp.dma_start(d_table[t * P:(t + n) * P, :].rearrange("(t p) d -> p t d", p=P),
                             node_a[:, t:t + n, :]).then_inc(S[f"span_moved{k}"], 16)
            for k in range(SPANS + 1):
                sp.wait_ge(S[f"span_moved{k}"], 32)
            sp.sem_inc(S["d_ready"], 1)

            def result_store(t, s):
                sp.wait_ge(S["result"], t + 1)
                if isinstance(t, int) and t == FULL:
                    sp.dma_start(out[FULL * P:N, :], result[0:TAIL, s, :]).then_inc(S[f"result_stored{s}"], 16)
                else:
                    sp.dma_start(out[bass.ds(t * P, P), :], result[:, s, :]).then_inc(S[f"result_stored{s}"], 16)
            over_tiles(sp, result_store, turn=4)
            sp.wait_ge(S["result_stored0"], 16 * (FULL // 4 + 1))
            for s in range(1, 4):
                sp.wait_ge(S[f"result_stored{s}"], 16 * (FULL // 4))
            sp.wait_ge(S["zero_rows"], 16 * NTP)

        @block.gpsimd
        def _(pool):
            link = Chain(pool, S["constants"])
            nc.gpsimd.memset(ones[:, :], 1.0)
            link(nc.gpsimd.memset(ident[:, :], 0.0))
            link(nc.gpsimd.affine_select(out=ident[:, :], in_=ident[:, :], compare_op=ALU.not_equal, fill=1.0,
                                         base=0, pattern=[[-1, P]], channel_multiplier=1))
            link(nc.gpsimd.affine_select(out=upper[:, :], in_=ones[:, :], compare_op=ALU.is_gt, fill=0.0,
                                         base=0, pattern=[[1, P]], channel_multiplier=-1))
            nc.gpsimd.memset(zeros[:, :, :], 0.0)
            nc.gpsimd.memset(eps_c[:, :], EPS)
            nc.gpsimd.iota(iota[:, :], [[1, P]], base=0, channel_multiplier=0, allow_small_or_imprecise_dtypes=True)
            nc.gpsimd.iota(iota_u, [[UR, NU]], base=0, channel_multiplier=0, allow_small_or_imprecise_dtypes=True)
            nc.gpsimd.iota(pcol[:, :], [[0, 1]], base=0, channel_multiplier=1, allow_small_or_imprecise_dtypes=True)
            nc.gpsimd.iota(iota_w[:, :], [[1, NTP]], base=0, channel_multiplier=0,
                           allow_small_or_imprecise_dtypes=True).then_inc(S["constants"], 2)

            pool.wait_ge(S["flagged"], 1)
            general = nc.gpsimd.value_load(flag[0:1, 0:1], min_val=0, max_val=1)
            with pool.If(general):
                pool.wait_ge(S["re_cleared"], 16 * (NG // 16))
                with pool.Fori(0, NC // RING) as i:
                    pool.wait_ge(S["re_staged"], i + 1)
                    pool.sem_inc(S["pool_may"], 1)
                    for j in range(RING):
                        nc.gpsimd.indirect_dma_start(
                            out=records, out_offset=bass.IndirectOffsetOnAxis(ap=stage[:, j, 0:1], axis=0),
                            in_=rec_put[:, j, :], in_offset=None, bounds_check=NG * GE - 1, oob_is_err=False).then_inc(S["re_put"], 16)

            def gather(table, tag, lo, hi):
                with pool.Fori(lo, hi) as i:
                    for s in range(RING):
                        pool.wait_ge(S[f"{tag}_staged"], RING * i + s + 1)
                        pool.sem_inc(S["pool_may"], 1)
                        for j in range(CPG):
                            nc.gpsimd.indirect_dma_start(
                                out=big[:, s, j, 0:D], out_offset=None, in_=table,
                                in_offset=bass.IndirectOffsetOnAxis(ap=stage[:, s, j:j + 1], axis=0)).then_inc(S[f"{tag}_rows{s}"], 16)

            pool.wait_ge(S["tables_ready"], 1)
            pool.sem_inc(S["pool_may"], 1)
            gather(in_table, "in", 0, FIRST)

            def scatter(lo, hi):
                with pool.Fori(lo, hi) as i:
                    for s in range(RING):
                        g = RING * i + s
                        pool.wait_ge(S["out_msg"], g + 1)
                        pool.wait_ge(S["out_carried"], g + 1)
                        pool.sem_inc(S["pool_may"], 1)
                        for j in range(CPG):
                            nc.gpsimd.indirect_dma_start(
                                out=messages, out_offset=bass.IndirectOffsetOnAxis(ap=stage[:, s, j:j + 1], axis=0),
                                in_=big[:, s, j, :], in_offset=None).then_inc(S[f"sent{s}"], 16)
            pool.wait_ge(S["zero_rows"], 16 * NTP)
            pool.sem_inc(S["pool_may"], 1)
            scatter(0, PLAIN)
            with pool.If(general):
                scatter(PLAIN, ALL)

            gather(in_table, "in", FIRST, PLAIN)
            with pool.If(general):
                gather(in_table, "in", PLAIN, ALL)

            def x_and_new(t, s):
                pool.wait_ge(S["gates_made"], t + 1)
                need(pool, S["e_y"], t - 1)
                pool.sem_inc(S["pool_may"], 1)
                new = gb[:, s, D:2 * D]
                nc.gpsimd.tensor_tensor(hn[:, s, :], gates_in[:, s, 2 * D:3 * D], new, ALU.subtract).then_inc(S["hn_made"], 1)
                nc.gpsimd.tensor_tensor(xn[:, s, :], new, gates_in[:, s, 3 * D:4 * D], ALU.add).then_inc(S["xn_made"], 1)
            over_tiles(pool, x_and_new)

            pool.wait_ge(S["d_ready"], 1)
            pool.sem_inc(S["pool_may"], 1)
            gather(d_table, "second", 0, BACK_TURNS)

        @block.scalar
        def _(act):
            for d, s in ((wio[:, :, 0:D], w_in.rearrange("(k p) n -> p k n", p=P)),
                         (wio[:, :, D:2 * D], w_out.rearrange("(k p) n -> p k n", p=P)),
                         (wx[:, :, :], w_x2i.rearrange("(k p) n -> p k n", p=P)),
                         (wh[:, :, :], w_h2h.rearrange("(k p) n -> p k n", p=P)),
                         (w1[:, :, :], w_l1.rearrange("(k p) n -> p k n", p=P)),
                         (gamma_b[:, :], row_view(gamma).broadcast_to([P, D])),
                         (beta_b[:, :], row_view(beta).broadcast_to([P, D])),
                         (bio_b[:, 0:D], row_view(b_in).broadcast_to([P, D])),
                         (bio_b[:, D:2 * D], row_view(b_out).broadcast_to([P, D])),
                         (bx_b, row_view(b_x2i).broadcast_to([P, 2 * D])),
                         (b1_b[:, :], row_view(b_l1).broadcast_to([P, D]))):
                act.dma_start(d, s).then_inc(S["weights"], 16)

            def squares(table, made, used, signal):
                def pairs(i):
                    act.wait_ge(made, i + 1)
                    for k in range(SPAN // 2):
                        need(act, used, (i - 1) * (SPAN // 2) + k + 1)
                        act.sem_inc(S["act_may"], 1)
                        nc.scalar.activation(sq[:, k, :], table[:, bass.ds(i * SPAN + 2 * k, 2), :].rearrange("p t d -> p (t d)"),
                                             ACT.Square).then_inc(signal, 1)
                pairs(0)
                with act.Fori(1, SPANS) as i:
                    pairs(i)
                act.wait_ge(made, SPANS + 1)
                act.wait_ge(used, FULL // 2 - SPAN // 2 + 1)
                nc.scalar.activation(sq[:, 0, :], table[:, FULL:NTP, :].rearrange("p t d -> p (t d)"), ACT.Square).then_inc(signal, 1)

            squares(node_a, S["x_centred"], S["x_sq_used"], S["x_sq"])
            act.wait_ge(S["x_var"], 1)
            nc.scalar.activation(scale_b[:, :], scale_b[:, :], ACT.Sqrt, bias=eps_c[:, :]).then_inc(S["x_var"], 1)

            def h_out(t, s):
                act.wait_ge(S["h_turned"], t + 1)
                need(act, S["tables_mm"], t - 3)
                need(act, S[f"tables_stored{s}"], 32 * (t // 4) if isinstance(t, int) else 32 * now[0])
                act.sem_inc(S["act_may"], 1)
                nc.scalar.activation(hT[:, s, :], ps[s % 2][:, 0:D], ACT.Copy).then_inc(S["h_out"], 1)

            act.wait_ge(S["beta_turned"], 1)
            nc.scalar.activation(hT[:, 1, :], ps[6][:, 0:D], ACT.Copy).then_inc(S["beta_out"], 1)
            act.wait_ge(S["beta_mm"], 1)
            now = [None]
            for t in range(4):
                h_out(t, t)
            with act.Fori(1, FULL // 4) as i:
                now[0] = i
                for s in range(4):
                    h_out(4 * i + s, s)
            h_out(FULL, 0)

            def second_table(t, s):
                act.wait_ge(S["o_mm"], t + 1)
                need(act, S[f"o_stored{s}"], 16 * (t // 2) if isinstance(t, int) else 16 * now[0])
                act.sem_inc(S["act_may"], 1)
                nc.scalar.activation(o_out[:, s, :], ps[s][:, 0:D], ACT.Copy).then_inc(S["o_made"], 1)

            act.wait_ge(S["flagged"], 1)
            general = nc.scalar.value_load(flag[0:1, 0:1], min_val=0, max_val=1)

            for s in range(2):
                second_table(s, s)
            with act.Fori(1, FULL // 2) as i:
                now[0] = i
                for s in range(2):
                    second_table(2 * i + s, s)
            second_table(FULL, 0)

            def out_turn(i, tiles):
                for s in range(RING):
                    g = RING * i + s
                    act.wait_ge(S["out_mm"], g + 1)
                    need(act, S[f"sent{s}"], i * 16 * CPG)
                    act.sem_inc(S["act_may"], 1)
                    for j in range(CPG):
                        b = ps[2 * (s % 2) + j // 2]
                        last = nc.scalar.activation(big[:, s, j, 0:D], b[:, (j % 2) * D:(j % 2 + 1) * D], ACT.Copy,
                                                    scale=ow_col[:, bass.ds(g * CPG + j, 1)])
                    last.then_inc(S["out_msg"], 1)
                    if s == 0 and tiles:
                        act.wait_ge(S["c_turned"], i + 1)
                        need(act, S["c_mm"], i)
                        nc.scalar.activation(ct, ps[6][:, 0:D], ACT.Copy).then_inc(S["c_out"], 1)

            act.wait_ge(S["slots_ready"], 1)
            out_turn(0, True)
            with act.Fori(1, NT) as i:
                out_turn(i, True)
            for i in range(NT, PLAIN):
                out_turn(i, False)
            with act.If(general):
                with act.Fori(PLAIN, ALL) as i:
                    out_turn(i, False)

            def keep(q, k, n):
                act.wait_ge(S[f"back_load{k}"], n * 16)
                act.sem_inc(S["act_may"], 1)
                nc.scalar.activation(back[:, bass.ds(4 * q, 4), :], pair[:, k, :, D:D + RW], ACT.Copy).then_inc(S["back_kept"], 1)
            with act.Fori(0, PAIRS // RING) as i:
                for k in range(RING):
                    keep(RING * i + k, k, i + 1)

            act.wait_ge(S["back_kept"], PAIRS)
            act.wait_ge(S["sums_done"], 1)
            nc.scalar.activation(back_id, back[:, :, 1], ACT.Copy).then_inc(S["back_ids"], 1)

            def gates_step(t, s):
                if is_tile(t):
                    need(act, S["e_mm"], t - 1)
                    act.sem_inc(S["act_may"], 1)
                    nc.scalar.activation(st[:, s, 0:2, :], in_sums[:, :, bass.ds(t * P, P)], ACT.Copy)
                    nc.scalar.activation(st[:, s, 2:4, :], halves(tile_of(node_c, t)), ACT.Copy).then_inc(S["e_out"], 1)
                if is_tile(t - 2):
                    act.wait_ge(S["gate_sums"], t - 1)
                    need(act, S["e_m"], t - 3)
                    need(act, S["xn_made"], t - 3)
                    nc.scalar.activation(gb[:, s, 0:D], ub[:, s, 0:D], ACT.Sigmoid)
                    nc.scalar.activation(gb[:, s, D:2 * D], ub[:, s, D:2 * D], ACT.Tanh).then_inc(S["gates_made"], 1)
            over_tiles(act, gates_step, 2, lag=4)

            act.wait_ge(S["y_stats"], 1)
            nc.scalar.activation(rstd_all[:, :], mv_all[:, :, 1], ACT.Sqrt, bias=eps_c[:, :]).then_inc(S["y_stats"], 1)
            squares(node_a, S["d_made"], S["d_sq_used"], S["d_sq"])
            act.wait_ge(S["d_var"], 1)
            nc.scalar.activation(scale_b[:, :], scale_b[:, :], ACT.Sqrt).then_inc(S["d_var"], 1)

            act.wait_ge(S["second_done"], 1)

            def second_step(t, s):
                if is_tile(t):
                    need(act, S["l_mm"], t - 1)
                    act.sem_inc(S["act_may"], 1)
                    nc.scalar.activation(st[:, s % 2, 0:2, :], halves(tile_of(node_a, t)), ACT.Copy).then_inc(S["l_out"], 1)
                if is_tile(t - 3):
                    r = (s - 3) % 4
                    act.wait_ge(S["l_mv"], t - 2)
                    need(act, S["result"], t - 6)
                    act.sem_inc(S["act_may"], 1)
                    nc.scalar.activation(rstd[:, r, :], mv[:, r, 1:2], ACT.Sqrt, bias=eps_c[:, :]).then_inc(S["l_dev"], 1)
            over_tiles(act, second_step, 3, lag=7, turn=4)

        @block.tensor
        def _(pe):
            pe.wait_ge(S["constants"], 5)

            def span_sum(k, to, table):
                for t in range(k * SPAN, (k + 1) * SPAN, 2):
                    nc.tensor.matmul(to, ones[:, :], table[:, t:t + 2, :].rearrange("p t d -> p (t d)"), start=t == 0, stop=False)

            def last_sum(to, table, signal):
                nc.tensor.matmul(to, ones[0:TAIL, :], table[0:TAIL, FULL:NTP, :].rearrange("p t d -> p (t d)"),
                                 start=False, stop=True).then_inc(signal, 1)

            def square_sum(to, made, used):
                def pairs(i):
                    for k in range(SPAN // 2):
                        pe.wait_ge(made, i * (SPAN // 2) + k + 1)
                        nc.tensor.matmul(to[:, :], ones[:, :], sq[:, k, :], start=isinstance(i, int) and i == k == 0,
                                         stop=False).then_inc(used, 1)
                pairs(0)
                with pe.Fori(1, SPANS) as i:
                    pairs(i)
                pe.wait_ge(made, FULL // 2 + 1)
                nc.tensor.matmul(to[:, :], ones[0:TAIL, :], sq[0:TAIL, 0, :], start=False, stop=True).then_inc(used, 1)

            pe.wait_ge(S["widest"], 1)
            nc.tensor.matmul(ps[6][:, 0:1], ones[:, :], widest[:, :], start=True, stop=True).then_inc(S["widest"], 1)

            def place_sums(ready, done):
                pe.wait_ge(ready, 1)
                nc.tensor.matmul(ps[6][:, 0:NTP], upper[:, :], cnt[:, :], start=True, stop=True)
                nc.tensor.matmul(ps[7][:, 0:NTP], ones[:, :], cnt[:, :], start=True, stop=True).then_inc(done, 1)

            pe.wait_ge(S["flagged"], 1)
            general = nc.tensor.value_load(flag[0:1, 0:1], min_val=0, max_val=1)

            def by_chunk(v):
                return v.rearrange("p (h j q) -> p h j q", h=2, j=CPG)

            with pe.If(general):
                for n in range(8):
                    if n:
                        pe.wait_ge(S["re_copied"], n)
                    for j in range(CPG):
                        last = nc.tensor.transpose(ps[6][:, j * P:(j + 1) * P], by_chunk(raw[n // 2])[:, n % 2, j, :], ident[:, :])
                    last.then_inc(S["re_turned"], 1)
                place_sums(S["re_counted"], S["re_sums"])

            pe.wait_ge(S["places"], 1)
            for n in range(10):
                v = (raw[0], raw[2], raw[3], raw_place, raw[1])[n // 2]
                if n >= 2:
                    pe.wait_ge(S["columns_copied"], n - 1)
                for j in range(CPG):
                    last = nc.tensor.transpose(ps[6 + n % 2][:, j * P:(j + 1) * P], by_chunk(v)[:, n % 2, j, :], ident[:, :])
                last.then_inc(S["columns_turned"], 1)
                if n < SPANS:
                    pe.wait_ge(S[f"span_moved{n}"], 16)
                    span_sum(n, ps[4][:, :], node_a)

            pe.wait_ge(S[f"span_moved{SPANS}"], 16)
            last_sum(ps[4][:, :], node_a, S["x_sum"])
            square_sum(ps[5], S["x_sq"], S["x_sq_used"])

            pe.wait_ge(S["weights"], LOADS_W)
            for k in range(2):
                last = nc.tensor.transpose(ps[6][:, k * P:(k + 1) * P], beta_b[:, k * P:(k + 1) * P], ident[:, :])
            last.then_inc(S["beta_turned"], 1)
            pe.wait_ge(S["beta_out"], 1)
            for k in range(2):
                last = nc.tensor.matmul(ps[7][:, :], hT[:, 1, k * P:(k + 1) * P], wio[:, k, :], start=k == 0, stop=k == 1)
            last.then_inc(S["beta_mm"], 1)

            def table_step(t, s):
                if is_tile(t):
                    pe.wait_ge(S["h_made"], t + 1)
                    need(pe, S["h_out"], t - 1)
                    for k in range(2):
                        last = nc.tensor.transpose(ps[s % 2][:, k * P:(k + 1) * P], hr[:, s % 2, k * P:(k + 1) * P], ident[:, :])
                    last.then_inc(S["h_turned"], 1)
                if is_tile(t - 1):
                    r = (s - 1) % 4
                    pe.wait_ge(S["h_out"], t)
                    need(pe, S["tables_made"], t - 2)
                    for k in range(2):
                        last = nc.tensor.matmul(ps[2 + r % 2][:, 0:D], hT[:, r, k * P:(k + 1) * P], wio[:, k, 0:D], start=k == 0, stop=k == 1)
                    last.then_inc(S["tables_mm"], 1)
            over_tiles(pe, table_step, 1, turn=4)

            def in_mm(i, s):
                g, h = RING * i + s, s % 2
                pe.wait_ge(S[f"in_rows{s}"], (i + 1) * 16 * CPG)
                pe.wait_ge(S["in_hot"], g + 1)
                need(pe, S["in_added"], g - 1)
                for k in range(2):
                    for j in range(CPG):
                        last = nc.tensor.matmul(ps[4 + h][:, k * P:(k + 1) * P], big[:, s, j, k * P:(k + 1) * P],
                                                hot[:, h, j, :], start=j == 0, stop=j == CPG - 1)
                last.then_inc(S["in_mm"], 1)

            def in_turn(i):
                for s in range(RING):
                    in_mm(i, s)

            def second_table(t, s, h_loads):
                pe.wait_ge(S[f"h_loaded{s % 2}"], h_loads)
                need(pe, S["o_made"], t - 1)
                for k in range(2):
                    nc.tensor.matmul(ps[s % 2][:, 0:D], h_in[:, s % 2, k * P:(k + 1) * P], wio[:, k, D:2 * D], start=k == 0, stop=False)
                nc.tensor.matmul(ps[s % 2][:, 0:D], ones[0:1, :], bio_b[0:1, D:2 * D], start=False, stop=True).then_inc(S["o_mm"], 1)

            def in_turn_and_tiles(i):
                for s in range(RING):
                    in_mm(i, s)
                    second_table(RING * (i - 1) + s, s, h_loads=16 * (2 * (i - 1) + s // 2 + 1))

            in_turn(0)
            in_turn_and_tiles(1)
            with pe.Fori(2, 1 + FULL // RING) as i:
                in_turn_and_tiles(i)
            for i in range(1 + FULL // RING, RANKED):
                in_turn(i)
                if i == 1 + FULL // RING:
                    second_table(FULL, 0, h_loads=16 * (FULL // 2 + 1))
            place_sums(S["counted"], S["place_sums"])
            pe.wait_ge(S["counted"], 2)
            nc.tensor.matmul(ps[7][:, 0:NU], ones[0:NT, :], mask[0:NT, 0:NU], start=True, stop=True).then_inc(S["place_sums"], 1)
            with pe.Fori(RANKED, FIRST) as i:
                in_turn(i)

            def out_turn(i, tiles):
                for s in range(RING):
                    g, h = RING * i + s, s % 2
                    pe.wait_ge(S["out_hot"], g + 1)
                    need(pe, S["out_msg"], g - 1)
                    for j in range(CPG):
                        b = ps[2 * h + j // 2]
                        last = nc.tensor.matmul(b[:, (j % 2) * D:(j % 2 + 1) * D], hot_flat(h)[:, j * P:(j + 1) * P],
                                                tab[:, h, :], start=True, stop=True)
                    last.then_inc(S["out_mm"], 1)
                    if s == 0 and tiles:
                        pe.wait_ge(S["c_h"], i + 1)
                        need(pe, S["c_out"], i)
                        for k in range(2):
                            last = nc.tensor.transpose(ps[6][:, k * P:(k + 1) * P], cg[:, (k + 4) * P:(k + 5) * P], ident[:, :])
                        last.then_inc(S["c_turned"], 1)
                    if s == 1 and tiles:
                        pe.wait_ge(S["c_out"], i + 1)
                        need(pe, S["c_sum"], i)
                        for k in range(2):
                            last = nc.tensor.matmul(ps[7][:, :], ct[:, k * P:(k + 1) * P], wh[:, k, :], start=k == 0, stop=k == 1)
                        last.then_inc(S["c_mm"], 1)

            out_turn(0, True)
            with pe.Fori(1, NT) as i:
                out_turn(i, True)
            for i in range(NT, PLAIN):
                out_turn(i, False)
            with pe.If(general):
                with pe.Fori(PLAIN, ALL) as i:
                    out_turn(i, False)

            def back_mm(q, k):
                pe.wait_ge(S["back_hot"], q + 1)
                need(pe, S["back_added"], 2 * (q - RING + 1))
                for u in range(2):
                    for d in range(2):
                        for j in range(2):
                            last = nc.tensor.matmul(ps[k][:, (2 * u + d) * P:(2 * u + d + 1) * P],
                                                    pair[:, k, 2 * u + j, d * P:(d + 1) * P], hot_b[k][:, 2 * u + j, :],
                                                    start=j == 0, stop=j == 1)
                last.then_inc(S["back_mm"], 1)

            def both_turn(i):
                for s in range(RING):
                    in_mm(FIRST + i, s)
                    for n in range(2):
                        back_mm(PAIRS_T * i + 2 * s + n, (2 * s + n) % RING)
            both_turn(0)
            with pe.Fori(1, PLAIN - FIRST) as i:
                both_turn(i)
            with pe.If(general):
                with pe.Fori(PLAIN, ALL) as i:
                    in_turn(i)

            def gates_step(t, s):
                if is_tile(t):
                    pe.wait_ge(S["e_out"], t + 1)
                    need(pe, S["gate_sums"], t - 1)
                    for k in range(4):
                        last = nc.tensor.matmul(ps[2 + s][:, :], st[:, s, k, :], wx[:, k, :], start=k == 0, stop=k == 3)
                    last.then_inc(S["e_mm"], 1)
            over_tiles(pe, gates_step)

            for k in range(SPANS):
                pe.wait_ge(S["x1_made"], (k + 1) * SPAN)
                span_sum(k, ps[6][:, :], node_c)
            pe.wait_ge(S["x1_made"], NT)
            last_sum(ps[6][:, :], node_c, S["x1_sum"])
            square_sum(ps[7], S["d_sq"], S["d_sq_used"])

            def second_turn(i):
                for s in range(RING):
                    g, h = RING * i + s, s % 2
                    pe.wait_ge(S[f"second_rows{s}"], (i + 1) * 16 * CPG)
                    pe.wait_ge(S["second_hot"], g + 1)
                    need(pe, S["second_added"], g - 1)
                    for u in range(2):
                        for d in range(2):
                            for j in range(2 * u, 2 * u + 2):
                                last = nc.tensor.matmul(ps[4 + h][:, (2 * u + d) * P:(2 * u + d + 1) * P],
                                                        big[:, s, j, d * P:(d + 1) * P], hot[:, h, j, :], start=j % 2 == 0, stop=j % 2 == 1)
                    last.then_inc(S["second_mm"], 1)
            second_turn(0)
            pe.wait_ge(S["d_var"], 3)
            for k in range(2):
                last = nc.tensor.transpose(ps[7][:, k * P:(k + 1) * P], scale_b[:, k * P:(k + 1) * P], ident[:, :])
            last.then_inc(S["d_turned"], 1)
            with pe.Fori(1, BACK_TURNS) as i:
                second_turn(i)

            def second_step(t, s):
                if is_tile(t):
                    pe.wait_ge(S["l_out"], t + 1)
                    need(pe, S["l_y"], t - 1)
                    for k in range(2):
                        last = nc.tensor.matmul(ps[2 + s][:, 0:D], st[:, s, k, :], w1[:, k, :], start=k == 0, stop=k == 1)
                    last.then_inc(S["l_mm"], 1)
            over_tiles(pe, second_step)

        @block.vector
        def _(dve):
            link = Chain(dve, S["dve_chain"])
            V = nc.vector
            V.memset(raw_si[:, GE:2 * GE], NT * P)
            V.memset(raw_di[:, GE:2 * GE], N - 1)
            V.memset(raw[2][:, GE:2 * GE], 0.0)
            V.memset(raw[3][:, GE:2 * GE], 0.0)
            link(V.memset(node_a[:, FULL:NTP, :], 0.0))
            dve.sem_inc(S["pads_set"], 1)
            dve.wait_ge(S["edges_loaded"], 16 * 12)
            V.tensor_copy(raw[0], raw_si)
            link(V.tensor_copy(raw[1], raw_di))

            def mean_of(to, sums, n=N):
                link(V.tensor_scalar(to[:, :], sums[:, 0:D], 1.0 / n, None, ALU.mult))
                link(V.scalar_tensor_tensor(to[:, :], sums[:, D:2 * D], 1.0 / n, to[:, :], ALU.mult, ALU.add))

            def centre(to, table, signal):
                for k in range(SPANS + 1):
                    t, n = k * SPAN, SPAN if k < SPANS else 1
                    mean = mean_b[:, :].rearrange("p (o d) -> p o d", o=1).broadcast_to([P, n, D])
                    V.tensor_tensor(to[:, t:t + n, :], table[:, t:t + n, :], mean, ALU.subtract).then_inc(signal, 1)

            def by_half(v):
                return v.rearrange("p (h q) -> p h q", h=2)

            def low_high():
                V.tensor_reduce(dlow[:, :], by_half(raw[1]), AX.X, ALU.min)
                link(V.tensor_reduce(dhigh[:, :], by_half(raw[1]), AX.X, ALU.max))

            low_high()
            link(V.tensor_tensor(wide[:, :], dhigh[:, :], dlow[:, :], ALU.subtract))
            link(V.tensor_scalar(wide[:, :], wide[:, :], float(P - 1), None, ALU.is_gt))
            V.tensor_reduce(widest[:, :], wide[:, :], AX.X, ALU.max).then_inc(S["widest"], 1)
            dve.wait_ge(S["widest"], 2)
            link(V.tensor_scalar(flag[0:1, 0:1], ps[6][0:1, 0:1], 1.0, None, ALU.min))
            dve.sem_inc(S["flagged"], 1)

            general = V.value_load(flag[0:1, 0:1], min_val=0, max_val=1)
            with dve.If(general):
                sub = Chain(dve, S["re_chain"])
                r4 = rec[:, 0:16 * GE // P, :]
                sub(V.memset(r4, 0.0))
                V.memset(r4[:, :, 0], float(NT * P))
                sub(V.memset(r4[:, :, 1], -1.0))
                dve.sem_inc(S["re_empty"], 1)
                dve.wait_ge(S["re_cleared"], 16 * (NG // 16))
                for n in range(8):
                    k, hh = n // 2, n % 2
                    dve.wait_ge(S["re_turned"], n + 1)
                    o = rec[:, hh * NC // 2:(hh + 1) * NC // 2, k].rearrange("p (g j) -> p g j", j=CPG)
                    V.tensor_copy(o, ps[6][:, :].rearrange("p (j g) -> p g j", j=CPG)).then_inc(S["re_copied"], 1)
                dve.wait_ge(S["re_copied"], 8)
                V.tensor_copy(mask_i, rec[:, :, 1])
                sub(V.tensor_copy(scan_i, rec[:, :, 0]))
                V.tensor_scalar(mask_i, mask_i, 7, None, ALU.logical_shift_right)
                sub(V.tensor_scalar(scan_i, scan_i, 7, None, ALU.logical_shift_right))
                V.tensor_copy(win, mask_i)
                sub(V.tensor_copy(win_b, scan_i))
                sub(V.tensor_scalar(win_b, win_b, float(NT), None, ALU.is_equal))
                sub(V.tensor_tensor(win, win, win_b, ALU.add))
                sub(V.memset(rank, 0.0))
                with dve.Fori(0, NTP) as w:
                    chain = Chain(dve, S["re_count"], w * 4)
                    chain(V.tensor_scalar(mask, win, iota_w[:, bass.ds(w, 1)], None, ALU.is_equal))
                    chain(V.tensor_tensor_scan(scan, mask, mask, 0.0, ALU.add, ALU.max))
                    V.tensor_copy(cnt[:, bass.ds(w, 1)], scan[:, NC - 1:NC])
                    chain(V.tensor_tensor(mask, scan, mask, ALU.mult))
                    chain(V.tensor_tensor(rank, rank, mask, ALU.add))
                dve.sem_inc(S["re_counted"], 1)
                dve.wait_ge(S["re_sums"], 1)
                sub(V.tensor_copy(aligi[:, :], ps[7][:, 0:NTP]))
                sub(V.tensor_scalar(aligi[:, :], aligi[:, :], ~(GE - 1), None, ALU.bitwise_and))
                sub(V.tensor_scalar(alig[:, :], aligi[:, :], float(GE), None, ALU.add))
                sub(V.tensor_tensor_scan(ends[:, :], alig[:, :], alig[:, :], 0.0, ALU.add, ALU.max))
                sub(V.tensor_tensor(starts[:, :], ends[:, :], alig[:, :], ALU.subtract))
                sub(V.scalar_tensor_tensor(basew[:, :], starts[:, :], -1.0, ps[6][:, 0:NTP], ALU.add, ALU.add))
                with dve.Fori(0, NTP) as w:
                    chain = Chain(dve, S["re_base"], w * 2)
                    chain(V.tensor_scalar(mask, win, iota_w[:, bass.ds(w, 1)], basew[:, bass.ds(w, 1)], ALU.is_equal, ALU.mult))
                    chain(V.tensor_tensor(rank, rank, mask, ALU.add))

                def hand(i):
                    need(dve, S["re_put"], i * 16 * RING)
                    dve.sem_inc(S["dve_may"], 1)
                    V.tensor_copy(rec_put[:, :, :], rec[:, bass.ds(i * RING, RING), :])
                    V.tensor_copy(stage[:, :, 0], rank[:, bass.ds(i * RING, RING)]).then_inc(S["re_handed"], 1)
                    dve.wait_ge(S["re_handed"], i + 1)
                    dve.sem_inc(S["re_staged"], 1)
                hand(0)
                with dve.Fori(1, NC // RING) as i:
                    hand(i)
                dve.wait_ge(S["re_loaded"], 32)
                for k in range(4):
                    last = V.tensor_copy(by_half(raw[k]), reload[:, :, :, k])
                sub(last)
                sub(V.tensor_reduce(dhigh[:, :], by_half(raw[1]), AX.X, ALU.max))
                sub(V.tensor_scalar(dhigh[:, :], dhigh[:, :], 0.0, None, ALU.max))
                sub(V.tensor_copy(dwini[:, :], dhigh[:, :]))
                sub(V.tensor_scalar(dwini[:, :], dwini[:, :], ~(P - 1), None, ALU.bitwise_and))
                sub(V.tensor_copy(dhigh[:, :], dwini[:, :]))
                for hh in range(2):
                    v = raw[1][:, hh * GE:(hh + 1) * GE]
                    last = V.tensor_scalar(v, v, dhigh[:, hh:hh + 1], None, ALU.max)
                sub(last)

            low_high()
            link(V.tensor_copy(dlowi[:, :], dlow[:, :]))
            for hh in range(2):
                c = slice(hh * GE, (hh + 1) * GE)
                last = V.tensor_scalar(raw_place[:, c], raw[1][:, c], dlow[:, hh:hh + 1], None, ALU.subtract)
            link(last)
            dve.sem_inc(S["lows"], 1)
            dve.sem_inc(S["places"], 1)
            for n in range(10):
                k, hh = n // 2, n % 2
                dve.wait_ge(S["columns_turned"], n + 1)
                c = slice(hh * NC // 2, (hh + 1) * NC // 2)
                to = (win_b[:, c], carried[:, c, 2], ow_col[:, c], place[:, c], carried[:, c, 1])[k]
                V.tensor_copy(to.rearrange("p (g j) -> p g j", j=CPG),
                              ps[6 + n % 2][:, :].rearrange("p (j g) -> p g j", j=CPG)).then_inc(S["columns_copied"], 1)
            dve.wait_ge(S["columns_copied"], 10)
            dve.wait_ge(S["x_sum"], 1)
            mean_of(mean_b, ps[4])
            centre(node_a, node_a, S["x_centred"])
            link(V.tensor_copy(src_id, win_b))
            V.tensor_scalar(mask_i, src_id, 7, None, ALU.logical_shift_right)
            link(V.tensor_scalar(scan_i, src_id, P - 1, None, ALU.bitwise_and))
            V.tensor_copy(win, mask_i)
            link(V.tensor_copy(carried[:, :, 0], scan_i))
            V.memset(rank, 0.0)
            link(V.tensor_scalar(upper_half, win, float(PACKED), None, ALU.is_ge))
            link(V.scalar_tensor_tensor(half_win, upper_half, -float(PACKED), win, ALU.mult, ALU.add))
            link(V.tensor_scalar(half_unit, upper_half, 4095.0, 1.0, ALU.mult, ALU.add))
            dve.wait_ge(S["x_sq_used"], FULL // 2 + 1)
            mean_of(scale_b, ps[5])
            dve.sem_inc(S["x_var"], 1)
            dve.wait_ge(S["x_var"], 2)
            link(V.reciprocal(scale_b[:, :], scale_b[:, :]))
            dve.wait_ge(S["weights"], LOADS_W)
            link(V.tensor_tensor(scale_b[:, :], scale_b[:, :], gamma_b[:, :], ALU.mult))

            dve.wait_ge(S["beta_mm"], 1)
            link(V.tensor_tensor(bio_b, bio_b, ps[7][:, :], ALU.add))

            def table_step(t, s):
                if is_tile(t):
                    need(dve, S["h_turned"], t - 1)
                    V.tensor_tensor(hr[:, s % 2, :], tile_of(node_a, t), scale_b[:, :], ALU.mult).then_inc(S["h_made"], 1)
                if is_tile(t - 2):
                    r = (s - 2) % 4
                    dve.wait_ge(S["tables_mm"], t - 1)
                    need(dve, S[f"tables_stored{r}"], 32 * ((t - 2) // 4) if isinstance(t, int) else 32 * (now[0] - (s < 2)))
                    V.tensor_tensor(tabs[:, r, :], ps[2 + s % 2][:, 0:D], bio_b[:, 0:D], ALU.add).then_inc(S["tables_made"], 1)
            now = [None]
            for t in range(8):
                table_step(t, t % 4)
            with dve.Fori(2, FULL // 4) as i:
                now[0] = i
                for s in range(4):
                    table_step(4 * i + s, s)
            for t in range(FULL, FULL + 3):
                table_step(t, t % 4)

            def stage_in(g, s):
                V.tensor_copy(stage[:, s, :], src_id[:, bass.ds(g * CPG, CPG)]).then_inc(S["in_staged"], 1)

            def hot_in(g, s):
                need(dve, S["in_mm"], g - 1)
                for j in range(CPG):
                    last = V.tensor_scalar(hot[:, s % 2, j, :], iota[:, :], place[:, bass.ds(g * CPG + j, 1)],
                                           carried[:, bass.ds(g * CPG + j, 1), 2], ALU.is_equal, ALU.mult)
                last.then_inc(S["in_hot"], 1)

            def two_lows(i, s):
                v = V.value_load(low_two[0:1, bass.ds(2 * i + s // 2, 1)], min_val=0, max_val=(N << LOW_BITS) + N)
                return [(v & ((1 << LOW_BITS) - 1)).with_bounds(min_val=0, max_val=N - 1),
                        (v >> LOW_BITS).with_bounds(min_val=0, max_val=N - 1)]

            def add_in(g, s, low):
                dve.wait_ge(S["in_mm"], g + 1)
                need(dve, S["in_added"], g)
                o = in_sums[:, :, bass.ds(low, P)]
                V.tensor_tensor(o, o, halves(ps[4 + s % 2][:, 0:D]), ALU.add).then_inc(S["in_added"], 1)

            def in_turn(i, beside=(), first=False, last=False):
                for s in range(RING):
                    g = RING * i + s
                    hot_in(g, s)
                    steps = beside[s::RING]
                    for step in steps[:1]:
                        step()
                    if s == 0 and not first:
                        lows = two_lows(i - 1, 2)
                    elif s % 2:
                        lows = two_lows(i, s - 1)
                    if not (first and s == 0):
                        add_in(g - 1, (s - 1) % RING, lows[(s - 1) % 2])
                        if not (last and s > 0):
                            dve.sem_inc(S["dve_may"], 1)
                            stage_in(g + RING - 1, (s - 1) % RING)
                    for step in steps[1:]:
                        step()

            def in_start(lo):
                dve.sem_inc(S["dve_may"], 1)
                for s in range(RING):
                    stage_in(lo * RING + s, s)

            def in_end(hi):
                add_in(hi * RING - 1, RING - 1, two_lows(hi - 1, 2)[1])

            def rank_steps(k):
                def step(n, do):
                    def run():
                        dve.wait_ge(S["rank_chain"], k * 4 + n + 1)
                        do().then_inc(S["rank_chain"], 1)
                    return run

                def pick():
                    V.tensor_scalar(cnt[:, bass.ds(k, 1)], scan[:, NC - 1:NC], 0.0, None, ALU.add)
                    return V.scalar_tensor_tensor(mask, half_win, iota_w[:, bass.ds(k, 1)], scan, ALU.is_equal, ALU.mult)
                return [step(0, lambda: V.scalar_tensor_tensor(mask, half_win, iota_w[:, bass.ds(k, 1)], half_unit,
                                                               ALU.is_equal, ALU.mult)),
                        step(1, lambda: V.tensor_tensor_scan(scan, mask, mask, 0.0, ALU.add, ALU.max)),
                        step(2, pick),
                        step(3, lambda: V.tensor_tensor(rank, rank, mask, ALU.add))]

            def base_steps(w):
                def step(n, do):
                    def run():
                        dve.wait_ge(S["base_chain"], w * 2 + n + 1)
                        do().then_inc(S["base_chain"], 1)
                    return run
                return [step(0, lambda: V.tensor_scalar(mask, win, iota_w[:, bass.ds(w, 1)], basew[:, bass.ds(w, 1)],
                                                        ALU.is_equal, ALU.mult)),
                        step(1, lambda: V.tensor_tensor(rank, rank, mask, ALU.add))]

            def in_order(steps):
                n = -(-len(steps) // RING)
                steps = steps + [lambda: None] * (n * RING - len(steps))
                return [steps[b * n + a] for a in range(n) for b in range(RING)]

            dve.sem_inc(S["rank_chain"], 1)
            in_start(0)
            link(V.memset(node_a[:, :, :], 0.0))
            dve.wait_ge(S["low_tabs"], 32)
            lows = low_tab[:, :].rearrange("p (n u) -> p n u", u=2)
            link(V.tensor_scalar(low_two[:, :], lows[:, :, 1], LOW_BITS, None, ALU.logical_shift_left))
            link(V.tensor_tensor(low_two[:, :], low_two[:, :], lows[:, :, 0], ALU.bitwise_or))
            in_turn(0, first=True)
            with dve.Fori(1, RANKED - 1) as i:
                in_turn(i, in_order(rank_steps(2 * i - 2) + rank_steps(2 * i - 1)))
            in_turn(RANKED - 1, in_order(rank_steps(PACKED - 1)))
            dve.wait_ge(S["rank_chain"], 4 * PACKED + 1)
            V.tensor_copy(mask_i, rank)
            link(V.tensor_copy(aligi[:, 0:PACKED], cnt[:, 0:PACKED]))
            V.tensor_scalar(scan_i, mask_i, 12, None, ALU.logical_shift_right)
            V.tensor_scalar(aligi[:, PACKED:NTP], aligi[:, 0:PACKED], 12, None, ALU.logical_shift_right)
            link(V.tensor_scalar(aligi[:, 0:PACKED], aligi[:, 0:PACKED], 4095, None, ALU.bitwise_and))
            link(V.tensor_scalar(mask_i, mask_i, 4095, None, ALU.bitwise_and))
            V.tensor_copy(cnt[:, :], aligi[:, :])
            V.tensor_copy(rank, mask_i)
            link(V.tensor_copy(half_unit, scan_i))
            dve.sem_inc(S["counted"], 1)
            link(V.tensor_tensor(half_unit, half_unit, rank, ALU.subtract))
            link(V.tensor_tensor(half_unit, half_unit, upper_half, ALU.mult))
            link(V.tensor_tensor(rank, rank, half_unit, ALU.add))
            dve.wait_ge(S["place_sums"], 1)
            link(V.tensor_copy(aligi[:, :], ps[7][:, 0:NTP]))
            link(V.tensor_scalar(aligi[:, :], aligi[:, :], ~(UR - 1), None, ALU.bitwise_and))
            link(V.tensor_scalar(alig[:, :], aligi[:, :], float(UR), None, ALU.add))
            link(V.tensor_tensor_scan(ends[:, :], alig[:, :], alig[:, :], 0.0, ALU.add, ALU.max))
            link(V.tensor_tensor(starts[:, :], ends[:, :], alig[:, :], ALU.subtract))
            link(V.scalar_tensor_tensor(basew[:, :], starts[:, :], -1.0, ps[6][:, 0:NTP], ALU.add, ALU.add))
            link(V.tensor_tensor(diag[:, :], ends[:, :], ident[:, 0:NTP], ALU.mult))
            link(V.tensor_reduce(endcol[:, :], diag[:, :], AX.X, ALU.add))
            link(V.tensor_scalar(mask[:, 0:NU], iota_u, endcol[:, :], None, ALU.is_ge))
            dve.sem_inc(S["counted"], 1)
            link(V.tensor_scalar(starts[:, :], ends[:, :], float(-UR), None, ALU.add))
            V.tensor_copy(fill_row[:, 0:NT], starts[0:1, 0:NT])
            V.tensor_copy(fill_row[:, NT:NTP], ends[0:1, NT - 1:NT])
            link(V.tensor_copy(flat_row[:, :], starts[0:1, NT - 1:NT]))
            link(V.tensor_scalar(flat_row[:, :], flat_row[:, :], ~(2 * UR - 1), None, ALU.bitwise_and))
            link(V.tensor_copy(starts[0:1, 0:1], flat_row[:, :]))
            V.tensor_scalar(pair_row[:, :], iota_u[0:1, :].rearrange("p (q u) -> p q u", u=2)[:, :, 0], starts[0:1, 0:1],
                            None, ALU.min)
            dve.wait_ge(S["place_sums"], 2)
            wins = ps[7][0:1, 0:NU].rearrange("p (n u) -> p n u", u=4)
            link(V.tensor_copy(wins_f[:, :], wins[:, :, 3]))
            for u in (2, 1, 0):
                link(V.scalar_tensor_tensor(wins_f[:, :], wins_f[:, :], float(1 << WIN_BITS), wins[:, :, u], ALU.mult, ALU.add))
            link(V.tensor_copy(four_wins[:, :], wins_f[:, :]))
            dve.sem_inc(S["rows_ready"], 1)
            dve.sem_inc(S["base_chain"], 1)
            with dve.Fori(RANKED, FIRST - 1) as i:
                in_turn(i, in_order([step for n in range(BASES_T) for step in base_steps((i - RANKED) * BASES_T + n)]))
            in_turn(FIRST - 1, in_order([step for w in range((FIRST - 1 - RANKED) * BASES_T, NTP) for step in base_steps(w)]),
                    last=True)
            in_end(FIRST)
            dve.wait_ge(S["in_added"], RING * FIRST)
            dve.wait_ge(S["base_chain"], 2 * NTP + 1)
            link(V.tensor_copy(slot, rank))
            dve.sem_inc(S["slots_ready"], 1)

            def out_turn(i, tiles):
                for s in range(RING):
                    g, h = RING * i + s, s % 2
                    dve.wait_ge(S[f"out_load{h}"], (2 * i + s // 2 + 1) * 32)
                    need(dve, S["out_mm"], g - 1)
                    V.tensor_scalar(hot_flat(h)[:, 0:GE], place_b[:, h, :], pcol[:, :], None, ALU.is_equal).then_inc(S["out_hot"], 1)
                    need(dve, S[f"sent{s}"], i * 16 * CPG)
                    dve.sem_inc(S["dve_may"], 1)
                    V.tensor_copy(big[:, s, :, D:D + RW], carried[:, bass.ds(g * CPG, CPG), :])
                    V.tensor_copy(stage[:, s, :], slot[:, bass.ds(g * CPG, CPG)]).then_inc(S["out_carried"], 1)
                    if s == 0 and tiles:
                        chain = Chain(dve, S["c_chain"], i * 2)
                        dve.wait_ge(S["cx_loaded"], (i + 1) * 16)
                        need(dve, S["c_stored"], i * 16)
                        row = cg[:, 2 * D:3 * D]
                        chain(V.tensor_tensor(row, cx, mean_b[:, :], ALU.subtract))
                        chain(V.tensor_tensor(row, row, scale_b[:, :], ALU.mult))
                        V.tensor_tensor(row, row, beta_b[:, :], ALU.add).then_inc(S["c_h"], 1)
                    if s == 2 and tiles:
                        dve.wait_ge(S["c_mm"], i + 1)
                        V.tensor_tensor(cg[:, 0:2 * D], ps[7][:, :], bx_b, ALU.add).then_inc(S["c_sum"], 1)

            out_turn(0, True)
            with dve.Fori(1, NT) as i:
                out_turn(i, True)
            n = PLAIN - NT
            for i in range(n):
                V.memset(node_c[:, i * NTP // n:(i + 1) * NTP // n, :], 0.0).then_inc(S["sums_zeroed"], 1)
                out_turn(NT + i, False)
            with dve.If(general):
                with dve.Fori(PLAIN, ALL) as i:
                    out_turn(i, False)
            for k in range(RING):
                dve.wait_ge(S[f"sent{k}"], 16 * CPG * PLAIN)
            with dve.If(general):
                for k in range(RING):
                    dve.wait_ge(S[f"sent{k}"], 16 * CPG * ALL)
            dve.wait_ge(S["sums_zeroed"], n)

            def hot_back(q, k, n):
                dve.wait_ge(S[f"back_load{k}"], 16 * n)
                need(dve, S["back_mm"], q - RING + 1)
                V.tensor_tensor(hot_b[k], iota[:, :].rearrange("p (o n) -> p o n", o=1).broadcast_to([P, CPG, P]),
                                pair[:, k, :, D:D + 1].broadcast_to([P, CPG, P]), ALU.is_equal).then_inc(S["back_hot"], 1)

            def windows(n, of):
                v = V.value_load(four_wins[0:1, bass.ds(n, 1)], min_val=0, max_val=1 << (4 * WIN_BITS))
                return [((v >> (WIN_BITS * u)) & ((1 << WIN_BITS) - 1)).with_bounds(min_val=0, max_val=NT) for u in of]

            def add_back(q, k, u, w):
                if u == 0:
                    dve.wait_ge(S["back_mm"], q + 1)
                need(dve, S["back_added"], 2 * q + u)
                V.tensor_tensor(tile_of(node_c, w), tile_of(node_c, w), ps[k][:, u * D:(u + 1) * D],
                                ALU.add).then_inc(S["back_added"], 1)

            def both_turn(i, first=False, last=False):
                for s in range(RING):
                    g, m = RING * (FIRST + i) + s, 2 * s
                    q = PAIRS_T * i + m
                    lag = not (first and s == 0)
                    if lag:
                        wins = windows(RING * i + s - 1, range(4))
                    if s % 2 == 0:
                        lows = two_lows(FIRST + i, s)
                    hot_back(q + 1, (m + 1) % RING, 2 * i + (m + 1) // RING + 1)
                    if lag:
                        add_back(q - 2, (m - 2) % RING, 0, wins[0])
                    if not (last and s == RING - 1):
                        hot_in(g + 1, (s + 1) % RING)
                    if lag:
                        add_back(q - 2, (m - 2) % RING, 1, wins[1])
                    if not (last and m + 1 == PAIRS_T - 1):
                        hot_back(q + 2, (m + 2) % RING, 2 * i + (m + 2) // RING + 1)
                    if lag:
                        add_back(q - 1, (m - 1) % RING, 0, wins[2])
                    add_in(g, s, lows[s % 2])
                    if not last:
                        dve.sem_inc(S["dve_may"], 1)
                        stage_in(g + RING, s)
                    if lag:
                        add_back(q - 1, (m - 1) % RING, 1, wins[3])

            in_start(FIRST)
            hot_in(RING * FIRST, 0)
            hot_back(0, 0, 1)
            both_turn(0, first=True)
            with dve.Fori(1, PLAIN - FIRST - 1) as i:
                both_turn(i)
            both_turn(PLAIN - FIRST - 1, last=True)
            wins = windows(NU // 4 - 1, range(4))
            for n in range(4):
                add_back(PAIRS - 2 + n // 2, RING - 2 + n // 2, n % 2, wins[n])
            with dve.If(general):
                in_start(PLAIN)
                in_turn(PLAIN, first=True)
                with dve.Fori(PLAIN + 1, ALL - 1) as i:
                    in_turn(i)
                in_turn(ALL - 1, last=True)
                in_end(ALL)
                dve.wait_ge(S["in_added"], NG)
            dve.wait_ge(S["in_added"], NG_PLAIN)
            dve.wait_ge(S["back_added"], NU)
            dve.sem_inc(S["sums_done"], 1)

            def stats(y, t, s, made, prefix):
                dve.wait_ge(S[made], t + 1)
                need(dve, S[prefix + "_mv"], t - 1)
                dve.sem_inc(S["dve_may"], 1)
                V.bn_stats(bn6[:, s, :], y).then_inc(S[prefix + "_bn"], 1)

            def mean_var(t, s, used, prefix):
                dve.wait_ge(S[prefix + "_bn"], t + 1)
                need(dve, S[used], t - 1)
                dve.sem_inc(S["dve_may"], 1)
                V.bn_aggr(mv[:, s, :], bn6[:, s, :]).then_inc(S[prefix + "_mv"], 1)

            def gates_step(t, s):
                r = 1 - s
                if is_tile(t - 1):
                    dve.wait_ge(S["e_mm"], t)
                    dve.wait_ge(S[f"gates_load{r}"], gates_loads(t, s))
                    need(dve, S["gates_made"], t - 2)
                    V.tensor_tensor(ub[:, r, :], ps[2 + r][:, :], gates_in[:, r, 0:2 * D], ALU.add).then_inc(S["gate_sums"], 1)
                if is_tile(t - 4):
                    stats(tile_of(node_c, t - 4), t - 4, s, "e_y", "e")
                if is_tile(t - 3):
                    y = tile_of(node_c, t - 3)
                    dve.wait_ge(S["gates_made"], t - 2)
                    dve.wait_ge(S["hn_made"], t - 2)
                    V.tensor_tensor(y, hn[:, r, :], gb[:, r, 0:D], ALU.mult).then_inc(S["e_m"], 1)
                    dve.wait_ge(S["xn_made"], t - 2)
                    dve.wait_ge(S["e_m"], t - 2)
                    V.tensor_tensor(y, y, xn[:, r, :], ALU.add).then_inc(S["e_y"], 1)
                if is_tile(t - 5):
                    dve.wait_ge(S["e_mv"], t - 4)
                    V.tensor_scalar(mv_all[:, bass.ds(t - 5, 1), :].rearrange("p a d -> p (a d)"), mv[:, r, :], 0.0, None,
                                    ALU.add).then_inc(S["mv_kept"], 1)
                if is_tile(t - 4):
                    mean_var(t - 4, s, "mv_kept", "e")

            def gates_loads(t, s):
                if isinstance(t, int):
                    return 32 * ((t - 1) // 2 + 1)
                return 32 * (now[0] + s)

            now = [None]
            for t in range(6):
                gates_step(t, t % 2)
            with dve.Fori(3, FULL // 2) as i:
                now[0] = i
                for s in range(2):
                    gates_step(2 * i + s, s)
            for t in range(FULL, FULL + 6):
                gates_step(t, t % 2)
            dve.wait_ge(S["mv_kept"], NT)
            link(V.memset(node_c[:, NT:NTP, :], 0.0))
            dve.sem_inc(S["y_stats"], 1)
            dve.wait_ge(S["y_stats"], 2)
            link(V.reciprocal(rstd_all[:, :], rstd_all[:, :]))

            def normalise(t):
                V.tensor_scalar(tile_of(node_c, t), tile_of(node_c, t), mv_all[:, bass.ds(t, 1), 0], rstd_all[:, bass.ds(t, 1)],
                                ALU.subtract, ALU.mult).then_inc(S["x1_made"], 1)
            with dve.Fori(0, SPANS // 2) as i:
                for k in range(2 * SPAN):
                    normalise(2 * SPAN * i + k)
            normalise(FULL)

            dve.wait_ge(S["x1_sum"], 1)
            mean_of(mean_b, ps[6])
            link(V.memset(node_a[:, NT:NTP, :], 0.0))
            centre(node_a, node_c, S["d_made"])

            def variance():
                dve.wait_ge(S["d_sq_used"], FULL // 2 + 1)
                mean_of(scale_b, ps[7], N - 1)
                dve.sem_inc(S["d_var"], 1)

            def scale_weights():
                dve.wait_ge(S["d_var"], 2)
                link(V.tensor_scalar(scale_b[:, :], scale_b[:, :], 1e-4, None, ALU.add))
                link(V.reciprocal(scale_b[:, :], scale_b[:, :]))
                dve.sem_inc(S["d_var"], 1)
                dve.wait_ge(S["d_turned"], 1)
                link(V.tensor_copy(dev[:, :], ps[7][:, 0:D].rearrange("p (k n) -> p k n", k=2)[:, :, 0]))
                for k in range(2):
                    last = V.tensor_scalar(w1[:, k, :], w1[:, k, :], dev[:, k:k + 1], None, ALU.mult)
                link(last)

            def stage_second(g, s):
                V.tensor_copy(stage[:, s, :], back_id[:, bass.ds(g * CPG, CPG)]).then_inc(S["second_staged"], 1)

            def hot_second(g, s):
                need(dve, S["second_mm"], g - 1)
                for j in range(CPG):
                    last = V.tensor_scalar(hot[:, s % 2, j, :], iota[:, :], back[:, bass.ds(g * CPG + j, 1), 0],
                                           back[:, bass.ds(g * CPG + j, 1), 2], ALU.is_equal, ALU.mult)
                last.then_inc(S["second_hot"], 1)

            def add_second(g, s, i):
                for k, w in enumerate(windows(2 * i + s // 2, (2 * (s % 2), 2 * (s % 2) + 1))):
                    if k == 0:
                        dve.wait_ge(S["second_mm"], g + 1)
                    need(dve, S["second_adds"], g * 2 + k)
                    last = V.tensor_tensor(tile_of(node_a, w), tile_of(node_a, w), ps[4 + s % 2][:, k * D:(k + 1) * D], ALU.add)
                    last.then_inc(S["second_adds"], 1)
                dve.wait_ge(S["second_adds"], g * 2 + 2)
                dve.sem_inc(S["second_added"], 1)

            def second_turn(i, first=False, last=False, tiles=False):
                if tiles:
                    V.tensor_tensor(tile_of(node_c, i), tile_of(node_c, i), b1_b[:, :], ALU.add).then_inc(S["x1_biased"], 1)
                for s in range(RING):
                    g = RING * i + s
                    hot_second(g, s)
                    if not (first and s == 0):
                        add_second(g - 1, (s - 1) % RING, i if s else i - 1)
                        if not (last and s > 0):
                            dve.sem_inc(S["dve_may"], 1)
                            stage_second(g + RING - 1, (s - 1) % RING)

            dve.wait_ge(S["back_ids"], 1)
            dve.sem_inc(S["dve_may"], 1)
            for s in range(RING):
                stage_second(s, s)
            for k in range(SPANS + 1):
                dve.wait_ge(S["d_sq_used"], min((k + 1) * (SPAN // 2), FULL // 2 + 1))
                dve.wait_ge(S[f"span_moved{k}"], 32)
                last = V.memset(node_a[:, k * SPAN:min((k + 1) * SPAN, NTP), :], 0.0)
            link(last)
            variance()
            second_turn(0, first=True, tiles=True)
            scale_weights()
            with dve.Fori(1, NT) as i:
                second_turn(i, tiles=True)
            with dve.Fori(NT, BACK_TURNS - 1) as i:
                second_turn(i)
            second_turn(BACK_TURNS - 1, last=True)
            add_second(BACK_TURNS * RING - 1, RING - 1, BACK_TURNS - 1)
            dve.sem_inc(S["second_done"], 1)

            dve.wait_ge(S["x1_biased"], NT)

            def second_step(t, s):
                r, two = (s - 1) % 2, (s - 2) % 4
                if is_tile(t - 4):
                    dve.wait_ge(S["l_dev"], t - 3)
                    V.reciprocal(rstd[:, s, :], rstd[:, s, :]).then_inc(S["l_rstd"], 1)
                if is_tile(t - 1):
                    y = tile_of(node_c, t - 1)
                    dve.wait_ge(S["l_mm"], t)
                    V.tensor_tensor(y, y, ps[2 + r][:, 0:D], ALU.add).then_inc(S["l_y"], 1)
                if is_tile(t - 2):
                    stats(tile_of(node_c, t - 2), t - 2, two % 2, "l_y", "l")
                if is_tile(t - 4):
                    need(dve, S[f"result_stored{s}"], 16 * ((t - 4) // 4) if isinstance(t, int) else 16 * (now[0] - 1))
                    dve.wait_ge(S["l_rstd"], t - 3)
                    V.tensor_scalar(result[:, s, :], tile_of(node_c, t - 4), mv[:, s, 0:1], rstd[:, s, :],
                                    ALU.subtract, ALU.mult).then_inc(S["result"], 1)
                if is_tile(t - 2):
                    dve.wait_ge(S["l_bn"], t - 1)
                    need(dve, S["result"], t - 5)
                    dve.sem_inc(S["dve_may"], 1)
                    V.bn_aggr(mv[:, two, :], bn6[:, two % 2, :]).then_inc(S["l_mv"], 1)

            for t in range(8):
                second_step(t, t % 4)
            with dve.Fori(2, FULL // 4) as i:
                now[0] = i
                for s in range(4):
                    second_step(4 * i + s, s)
            for t in range(FULL, FULL + 5):
                second_step(t, t % 4)


_INS = ["x", "src", "dst", "edge_weight", "edge_weight_n2", "L0_gnn_gamma", "L0_gnn_beta", "L0_gnn_W_in",
        "L0_gnn_b_in", "L0_gnn_W_out", "L0_gnn_b_out", "L0_gnn_W_x2i", "L0_gnn_b_x2i", "L0_gnn_W_h2h",
        "L1_gnn_weight", "L1_gnn_bias"]


def kernel(**inputs):
    import numpy as _np
    import concourse.bacc as _bacc
    from concourse import mybir as _mybir
    from concourse.bass_utils import run_bass_kernel_spmd as _run

    nc = _bacc.Bacc("TRN2", target_bir_lowering=False, num_devices=1)
    arrays, args = {}, []
    for name in _INS:
        a = _np.ascontiguousarray(inputs[name])
        arrays[f"in_{name}"] = a
        args.append(nc.dram_tensor(f"in_{name}", a.shape, _mybir.dt.from_np(a.dtype), kind="ExternalInput").ap())
    args.append(nc.dram_tensor("out_0", (N, D), _mybir.dt.float32, kind="ExternalOutput").ap())
    gnn_program(nc, *args)
    r = _run(nc, [arrays], core_ids=[0])
    return r.results[0]["out_0"]
```
